# Optimizing a Trainium2 kernel written in Bass

```python
import numpy as np
import jax
import jax.numpy as jnp

def _softmax(x, axis=-1):
    return jax.nn.softmax(x, axis=axis)

def _gelu(x):
    return jax.nn.gelu(x, approximate=True)

def _silu(x):
    return jax.nn.silu(x)

def _sigmoid(x):
    return jax.nn.sigmoid(x)

def _layernorm(x, axis=-1, eps=1e-05):
    m = jnp.mean(x, axis=axis, keepdims=True)
    v = jnp.var(x, axis=axis, keepdims=True)
    return (x - m) / jnp.sqrt(v + eps)

def _scatter_add(tgt, idx, src, axis=0):
    return tgt.at[idx].add(src)

def _segment_sum(src, seg, n):
    return jax.ops.segment_sum(src, seg, n)
kernel_name = 'mk_perceiver_d2_seqx_r8_d35dc0'

def setup_inputs(seed: int=0):
    np.random.seed(seed)
    _w = jnp.asarray

    def _rec_inputs():
        import jax
        import jax.numpy as jnp
        _rk = jax.random.key(seed)
        x = -0.0005146 + 1 * jax.random.normal(jax.random.fold_in(_rk, 1), (4, 128, 128), jnp.float32)
        _lenS = 128 - jax.random.randint(jax.random.fold_in(_rk, 7), (4,), 0, max(1, 128 // 4) + 1, jnp.int32)
        _lenS2 = 2048 - jax.random.randint(jax.random.fold_in(_rk, 8), (4,), 0, max(1, 2048 // 4) + 1, jnp.int32)
        _ctx_1024P = jax.random.normal(jax.random.fold_in(_rk, 11), (4, 16, 128), jnp.float32)
        _ctx_1024c = jax.random.dirichlet(jax.random.fold_in(_rk, 511), 0.3 * jnp.ones((16,), jnp.float32), (4, 2048))
        _ctx_1024t = jnp.einsum('bsk,bkd->bsd', _ctx_1024c, _ctx_1024P)
        _ctx_1024t = _ctx_1024t * jax.lax.rsqrt(jnp.mean(jnp.square(_ctx_1024t)) + 1e-12) * 0.953939
        ctx_1024 = -0.000392918 + 0.999932 * (_ctx_1024t + 0.3 * jax.random.normal(jax.random.fold_in(_rk, 611), (4, 2048, 128), jnp.float32))
        _validS = jnp.arange(128)[None, :] < _lenS[:, None]
        _validS2 = jnp.arange(2048)[None, :] < _lenS2[:, None]
        _causal = jnp.tril(jnp.ones((128, 128), dtype=bool))
        mask_BxS2_bf1 = jnp.ones((4, 2048), dtype=bool)
        return (x, ctx_1024, mask_BxS2_bf1)
    x, ctx_1024, mask_BxS2_bf1 = _rec_inputs()

    def _L0_xattn_setup():
        import jax, jax.numpy as jnp
        import numpy as np
        DIM = 128
        DIM_LATENT = 128
        DIM_HEAD = 64
        HEADS = 16
        INNER = HEADS * DIM_HEAD

        def layernorm(x, g, b, eps=1e-05):
            m = jnp.mean(x, axis=-1, keepdims=True)
            v = jnp.mean((x - m) ** 2, axis=-1, keepdims=True)
            return (x - m) / jnp.sqrt(v + eps) * g + b

        def rmsnorm(x, gamma, eps=1e-08):
            n = jnp.linalg.norm(x, axis=-1, keepdims=True) * x.shape[-1] ** (-0.5)
            return x / jnp.maximum(n, eps) * gamma
        key = jax.random.key(seed)
        ks = jax.random.split(key, 8)
        b, n, m = (4, 512, 64)
        x = jax.random.normal(ks[0], (b, n, DIM), dtype=jnp.float32)
        latents = jax.random.normal(ks[1], (b, m, DIM_LATENT), dtype=jnp.float32)
        mask = jnp.ones((b, n), dtype=bool)
        s = 0.02
        return {'x': x, 'latents': latents, 'mask': mask, 'ln_x_g': jnp.ones((DIM,), jnp.float32), 'ln_x_b': jnp.zeros((DIM,), jnp.float32), 'ln_l_g': jnp.ones((DIM_LATENT,), jnp.float32), 'ln_l_b': jnp.zeros((DIM_LATENT,), jnp.float32), 'qn_g': jnp.ones((DIM_HEAD,), jnp.float32), 'kn_g': jnp.ones((DIM_HEAD,), jnp.float32), 'Wq': jax.random.normal(ks[2], (DIM_LATENT, INNER), jnp.float32) * s, 'Wkv': jax.random.normal(ks[3], (DIM, 2 * INNER), jnp.float32) * s, 'Wout': jax.random.normal(ks[4], (INNER, DIM_LATENT), jnp.float32) * s, 'bout': jnp.zeros((DIM_LATENT,), jnp.float32)}
    _L0_xattn_all = _L0_xattn_setup()
    _L0_xattn_in = {k: v for k, v in _L0_xattn_all.items() if k in ('ln_x_g', 'ln_x_b', 'ln_l_g', 'ln_l_b', 'qn_g', 'kn_g', 'Wq', 'Wkv', 'Wout', 'bout')}
    del _L0_xattn_all

    def _L0_attn_setup():
        import jax, jax.numpy as jnp
        import numpy as np
        B, S, D, H, DH, FF = (4, 512, 128, 16, 64, 512)
        EPS = 1e-06

        def _layer_norm(x, g, b):
            m = jnp.mean(x, axis=-1, keepdims=True)
            v = jnp.mean(jnp.square(x - m), axis=-1, keepdims=True)
            return (x - m) * jax.lax.rsqrt(v + 1e-05) * g + b
        key = jax.random.key(seed)
        ks = jax.random.split(key, 8)
        s = 0.02
        return {'src': jax.random.normal(ks[0], (B, S, D), dtype=jnp.float32), 'Wq': jax.random.normal(ks[1], (D, H * DH), dtype=jnp.float32) * s, 'bq': jnp.zeros((H * DH,), jnp.float32), 'Wk': jax.random.normal(ks[2], (D, H * DH), dtype=jnp.float32) * s, 'bk': jnp.zeros((H * DH,), jnp.float32), 'Wv': jax.random.normal(ks[3], (D, H * DH), dtype=jnp.float32) * s, 'bv': jnp.zeros((H * DH,), jnp.float32), 'Wo': jax.random.normal(ks[4], (H * DH, D), dtype=jnp.float32) * s, 'bo': jnp.zeros((D,), jnp.float32), 'W1': jax.random.normal(ks[5], (D, FF), dtype=jnp.float32) * s, 'b1': jnp.zeros((FF,), jnp.float32), 'W2': jax.random.normal(ks[6], (FF, D), dtype=jnp.float32) * s, 'b2': jnp.zeros((D,), jnp.float32), 'g1': jnp.ones((D,), jnp.float32), 'be1': jnp.zeros((D,), jnp.float32), 'g2': jnp.ones((D,), jnp.float32), 'be2': jnp.zeros((D,), jnp.float32)}
    _L0_attn_all = _L0_attn_setup()
    _L0_attn_in = {k: v for k, v in _L0_attn_all.items() if k in ('Wq', 'bq', 'Wk', 'bk', 'Wv', 'bv', 'Wo', 'bo', 'W1', 'b1', 'W2', 'b2', 'g1', 'be1', 'g2', 'be2')}
    del _L0_attn_all

    def _L0_ffn_setup():
        import jax, jax.numpy as jnp
        import numpy as np
        DIM = 128
        DEPTH = 6
        HEADS = 16
        DIM_HEAD = 64
        WINDOW = 32
        INNER = HEADS * DIM_HEAD
        DIM_INNER = int(DIM * 4 * 2 / 3)
        QK_SCALE = 8.0

        def shift_tokens(t):
            a, s = jnp.split(t, 2, -1)
            s = jnp.pad(s, ((0, 0), (1, 0), (0, 0)))[:, :-1]
            return jnp.concatenate([a, s], -1)

        def l2norm(t):
            return t / jnp.maximum(jnp.linalg.norm(t, axis=-1, keepdims=True), 1e-12)

        def rotate_half(x):
            x1, x2 = jnp.split(x, 2, -1)
            return jnp.concatenate([-x2, x1], -1)

        def rotary_tables(n):
            half = jnp.arange(0, DIM_HEAD, 2, dtype=jnp.float32)
            inv_freq = 1.0 / 10000.0 ** (half / DIM_HEAD)
            t = jnp.arange(n, dtype=jnp.float32)
            freqs = t[:, None] * inv_freq[None, :]
            freqs = jnp.concatenate([freqs, freqs], -1)
            base_scale = (half + 0.4 * DIM_HEAD) / (1.4 * DIM_HEAD)
            power = (t - n // 2) / (WINDOW // 2)
            scale = base_scale[None, :] ** power[:, None]
            scale = jnp.concatenate([scale, scale], -1)
            return (freqs, scale)

        def local_attention(q, k, v):
            b, h, n, d = q.shape
            w = WINDOW
            nw = n // w
            bq = q.reshape(b, h, nw, w, d)
            bk = k.reshape(b, h, nw, w, d)
            bv = v.reshape(b, h, nw, w, d)

            def look(t):
                p = jnp.pad(t, ((0, 0), (0, 0), (1, 0), (0, 0), (0, 0)))
                return jnp.concatenate([p[:, :, :nw], p[:, :, 1:]], axis=3)
            bk2, bv2 = (look(bk), look(bv))
            seq = jnp.arange(n).reshape(nw, w)
            seq_p = jnp.pad(seq, ((1, 0), (0, 0)), constant_values=-1)
            jt = jnp.concatenate([seq_p[:nw], seq_p[1:]], axis=1)
            it = seq[:, :, None]
            jb = jt[:, None, :]
            mask = (it < jb) | (it > jb + w) | (jb == -1)
            sim = jnp.einsum('bhwie,bhwje->bhwij', bq, bk2) * QK_SCALE
            sim = jnp.where(mask, -jnp.finfo(sim.dtype).max, sim)
            attn = jax.nn.softmax(sim, -1)
            out = jnp.einsum('bhwij,bhwje->bhwie', attn, bv2)
            return out.reshape(b, h, n, d)

        def attn_layer(x, Wqkv, qs, ksc, Wo):
            b, n, _ = x.shape
            qkv = x @ Wqkv
            q, k, v = jnp.split(qkv, 3, -1)
            sh = lambda t: t.reshape(b, n, HEADS, DIM_HEAD).transpose(0, 2, 1, 3)
            q, k, v = (sh(q), sh(k), sh(v))
            q = l2norm(q) * qs
            k = l2norm(k) * ksc
            freqs, scale = rotary_tables(n)
            cos, sin = (jnp.cos(freqs), jnp.sin(freqs))
            q = q * cos * scale + rotate_half(q) * sin * scale
            inv = 1.0 / scale
            k = k * cos * inv + rotate_half(k) * sin * inv
            out = local_attention(q, k, v)
            out = out.transpose(0, 2, 1, 3).reshape(b, n, INNER)
            return out @ Wo

        def ffn_layer(x, g, bln, W1, b1, W2, b2):
            mu = x.mean(-1, keepdims=True)
            var = ((x - mu) ** 2).mean(-1, keepdims=True)
            xn = (x - mu) / jnp.sqrt(var + 1e-05) * g + bln
            hg = xn @ W1 + b1
            a, gate = jnp.split(hg, 2, -1)
            return a * jax.nn.gelu(gate, approximate=False) @ W2 + b2
        key = jax.random.key(seed)
        ks = jax.random.split(key, 8)
        B, N = (2, 256)
        init = lambda k, shape: jax.random.normal(k, shape, jnp.float32) * 0.02
        return {'x': jax.random.normal(ks[0], (B, N, DIM), jnp.float32), 'Wqkv': init(ks[1], (DEPTH, DIM, 3 * INNER)), 'q_scale': jnp.ones((DEPTH, DIM_HEAD), jnp.float32), 'k_scale': jnp.ones((DEPTH, DIM_HEAD), jnp.float32), 'Wo': init(ks[2], (DEPTH, INNER, DIM)), 'ln_g': jnp.ones((DEPTH, DIM), jnp.float32), 'ln_b': jnp.zeros((DEPTH, DIM), jnp.float32), 'W1': init(ks[3], (DEPTH, DIM, 2 * DIM_INNER)), 'b1': jnp.zeros((DEPTH, 2 * DIM_INNER), jnp.float32), 'W2': init(ks[4], (DEPTH, DIM_INNER, DIM)), 'b2': jnp.zeros((DEPTH, DIM), jnp.float32)}
    _L0_ffn_all = _L0_ffn_setup()
    _L0_ffn_in = {k: v for k, v in _L0_ffn_all.items() if k in ('Wqkv', 'q_scale', 'k_scale', 'Wo', 'ln_g', 'ln_b', 'W1', 'b1', 'W2', 'b2')}
    del _L0_ffn_all

    def _L1_xattn_setup():
        import jax, jax.numpy as jnp
        import numpy as np
        H = 128
        B = 8
        L_CHAR = 256
        L_SUB = 128

        def _linear(x, W, b):
            return jnp.einsum('blh,oh->blo', x, W) + b

        def _interp_linear(x, out_len):
            L_in = x.shape[1]
            pos = (jnp.arange(out_len, dtype=x.dtype) + 0.5) * (L_in / out_len) - 0.5
            pos = jnp.clip(pos, 0.0, L_in - 1)
            lo = jnp.floor(pos).astype(jnp.int32)
            hi = jnp.minimum(lo + 1, L_in - 1)
            w = (pos - lo.astype(x.dtype))[None, :, None]
            return x[:, lo] * (1 - w) + x[:, hi] * w
        key = jax.random.key(seed)
        ks = jax.random.split(key, 18)
        s = 0.02
        inp = {'char_emb': jax.random.normal(ks[0], (B, L_CHAR, H), jnp.float32), 'subword_emb': jax.random.normal(ks[1], (B, L_SUB, H), jnp.float32)}
        names = ['Wq_c', 'Wk_s', 'Wv_s', 'Wq_s', 'Wk_c', 'Wv_c']
        for i, n in enumerate(names):
            inp[n] = jax.random.normal(ks[2 + 2 * i], (H, H), jnp.float32) * s
            inp['b' + n[1:]] = jax.random.normal(ks[3 + 2 * i], (H,), jnp.float32) * s
        inp['Wg'] = jax.random.normal(ks[14], (H, 2 * H), jnp.float32) * s
        inp['bg'] = jax.random.normal(ks[15], (H,), jnp.float32) * s
        return inp
    _L1_xattn_all = _L1_xattn_setup()
    _L1_xattn_in = {k: v for k, v in _L1_xattn_all.items() if k in ('Wq_c', 'bq_c', 'Wk_s', 'bk_s', 'Wv_s', 'bv_s', 'Wq_s', 'bq_s', 'Wk_c', 'bk_c', 'Wv_c', 'bv_c', 'Wg', 'bg')}
    del _L1_xattn_all

    def _L1_attn_setup():
        import jax, jax.numpy as jnp
        import numpy as np
        B, L, D, H = (2, 256, 128, 16)
        d = D // H
        key = jax.random.key(seed)
        ks = jax.random.split(key, 6)
        X = jax.random.normal(ks[0], (B, L, D), dtype=jnp.float32)
        scale = 0.02
        Wq = scale * jax.random.normal(ks[1], (D, D), dtype=jnp.float32)
        Wk = scale * jax.random.normal(ks[2], (D, D), dtype=jnp.float32)
        Wv = scale * jax.random.normal(ks[3], (D, D), dtype=jnp.float32)
        Wc = scale * jax.random.normal(ks[4], (D, D), dtype=jnp.float32)
        Ltri = scale * jax.random.normal(ks[5], (H, d, d), dtype=jnp.float32)
        return {'X': X, 'Wq': Wq, 'Wk': Wk, 'Wv': Wv, 'Wc': Wc, 'Ltri': Ltri}
    _L1_attn_all = _L1_attn_setup()
    _L1_attn_in = {k: v for k, v in _L1_attn_all.items() if k in ('Wq', 'Wk', 'Wv', 'Wc', 'Ltri')}
    del _L1_attn_all

    def _L1_ffn_setup():
        import jax, jax.numpy as jnp
        import numpy as np
        D_MODEL = 128
        H_SHARED = 256
        H_ROUTED = 128
        N_EXPERTS = 8
        TOP_K = 2
        key = jax.random.key(seed)
        ks = jax.random.split(key, 8)
        B, T = (2, 256)
        sc_d = 1.0 / np.sqrt(D_MODEL)
        sc_hs = 1.0 / np.sqrt(H_SHARED)
        sc_hr = 1.0 / np.sqrt(H_ROUTED)
        return {'x': jax.random.normal(ks[0], (B, T, D_MODEL), dtype=jnp.float32), 'router_w': jax.random.normal(ks[1], (N_EXPERTS, D_MODEL), dtype=jnp.float32) * sc_d, 'router_bias': jnp.zeros((N_EXPERTS,), dtype=jnp.float32), 'sw1': jax.random.normal(ks[2], (D_MODEL, H_SHARED), dtype=jnp.float32) * sc_d, 'sw3': jax.random.normal(ks[3], (D_MODEL, H_SHARED), dtype=jnp.float32) * sc_d, 'sw2': jax.random.normal(ks[4], (H_SHARED, D_MODEL), dtype=jnp.float32) * sc_hs, 'ew1': jax.random.normal(ks[5], (N_EXPERTS, D_MODEL, H_ROUTED), dtype=jnp.float32) * sc_d, 'ew2': jax.random.normal(ks[6], (N_EXPERTS, H_ROUTED, D_MODEL), dtype=jnp.float32) * sc_hr}
    _L1_ffn_all = _L1_ffn_setup()
    _L1_ffn_in = {k: v for k, v in _L1_ffn_all.items() if k in ('router_w', 'router_bias', 'sw1', 'sw3', 'sw2', 'ew1', 'ew2')}
    del _L1_ffn_all
    return {'x': x, 'ctx_1024': ctx_1024, 'mask_BxS2_bf1': mask_BxS2_bf1, 'L0_xattn_ln_x_g': _L0_xattn_in['ln_x_g'], 'L0_xattn_ln_x_b': _L0_xattn_in['ln_x_b'], 'L0_xattn_ln_l_g': _L0_xattn_in['ln_l_g'], 'L0_xattn_ln_l_b': _L0_xattn_in['ln_l_b'], 'L0_xattn_qn_g': _L0_xattn_in['qn_g'], 'L0_xattn_kn_g': _L0_xattn_in['kn_g'], 'L0_xattn_Wq': _L0_xattn_in['Wq'], 'L0_xattn_Wkv': _L0_xattn_in['Wkv'], 'L0_xattn_Wout': _L0_xattn_in['Wout'], 'L0_xattn_bout': _L0_xattn_in['bout'], 'L0_attn_Wq': _L0_attn_in['Wq'], 'L0_attn_bq': _L0_attn_in['bq'], 'L0_attn_Wk': _L0_attn_in['Wk'], 'L0_attn_bk': _L0_attn_in['bk'], 'L0_attn_Wv': _L0_attn_in['Wv'], 'L0_attn_bv': _L0_attn_in['bv'], 'L0_attn_Wo': _L0_attn_in['Wo'], 'L0_attn_bo': _L0_attn_in['bo'], 'L0_attn_W1': _L0_attn_in['W1'], 'L0_attn_b1': _L0_attn_in['b1'], 'L0_attn_W2': _L0_attn_in['W2'], 'L0_attn_b2': _L0_attn_in['b2'], 'L0_attn_g1': _L0_attn_in['g1'], 'L0_attn_be1': _L0_attn_in['be1'], 'L0_attn_g2': _L0_attn_in['g2'], 'L0_attn_be2': _L0_attn_in['be2'], 'L0_ffn_Wqkv': _L0_ffn_in['Wqkv'], 'L0_ffn_q_scale': _L0_ffn_in['q_scale'], 'L0_ffn_k_scale': _L0_ffn_in['k_scale'], 'L0_ffn_Wo': _L0_ffn_in['Wo'], 'L0_ffn_ln_g': _L0_ffn_in['ln_g'], 'L0_ffn_ln_b': _L0_ffn_in['ln_b'], 'L0_ffn_W1': _L0_ffn_in['W1'], 'L0_ffn_b1': _L0_ffn_in['b1'], 'L0_ffn_W2': _L0_ffn_in['W2'], 'L0_ffn_b2': _L0_ffn_in['b2'], 'L1_xattn_Wq_c': _L1_xattn_in['Wq_c'], 'L1_xattn_bq_c': _L1_xattn_in['bq_c'], 'L1_xattn_Wk_s': _L1_xattn_in['Wk_s'], 'L1_xattn_bk_s': _L1_xattn_in['bk_s'], 'L1_xattn_Wv_s': _L1_xattn_in['Wv_s'], 'L1_xattn_bv_s': _L1_xattn_in['bv_s'], 'L1_xattn_Wq_s': _L1_xattn_in['Wq_s'], 'L1_xattn_bq_s': _L1_xattn_in['bq_s'], 'L1_xattn_Wk_c': _L1_xattn_in['Wk_c'], 'L1_xattn_bk_c': _L1_xattn_in['bk_c'], 'L1_xattn_Wv_c': _L1_xattn_in['Wv_c'], 'L1_xattn_bv_c': _L1_xattn_in['bv_c'], 'L1_xattn_Wg': _L1_xattn_in['Wg'], 'L1_xattn_bg': _L1_xattn_in['bg'], 'L1_attn_Wq': _L1_attn_in['Wq'], 'L1_attn_Wk': _L1_attn_in['Wk'], 'L1_attn_Wv': _L1_attn_in['Wv'], 'L1_attn_Wc': _L1_attn_in['Wc'], 'L1_attn_Ltri': _L1_attn_in['Ltri'], 'L1_ffn_router_w': _L1_ffn_in['router_w'], 'L1_ffn_router_bias': _L1_ffn_in['router_bias'], 'L1_ffn_sw1': _L1_ffn_in['sw1'], 'L1_ffn_sw3': _L1_ffn_in['sw3'], 'L1_ffn_sw2': _L1_ffn_in['sw2'], 'L1_ffn_ew1': _L1_ffn_in['ew1'], 'L1_ffn_ew2': _L1_ffn_in['ew2']}

def reference(x, ctx_1024, mask_BxS2_bf1, L0_xattn_ln_x_g, L0_xattn_ln_x_b, L0_xattn_ln_l_g, L0_xattn_ln_l_b, L0_xattn_qn_g, L0_xattn_kn_g, L0_xattn_Wq, L0_xattn_Wkv, L0_xattn_Wout, L0_xattn_bout, L0_attn_Wq, L0_attn_bq, L0_attn_Wk, L0_attn_bk, L0_attn_Wv, L0_attn_bv, L0_attn_Wo, L0_attn_bo, L0_attn_W1, L0_attn_b1, L0_attn_W2, L0_attn_b2, L0_attn_g1, L0_attn_be1, L0_attn_g2, L0_attn_be2, L0_ffn_Wqkv, L0_ffn_q_scale, L0_ffn_k_scale, L0_ffn_Wo, L0_ffn_ln_g, L0_ffn_ln_b, L0_ffn_W1, L0_ffn_b1, L0_ffn_W2, L0_ffn_b2, L1_xattn_Wq_c, L1_xattn_bq_c, L1_xattn_Wk_s, L1_xattn_bk_s, L1_xattn_Wv_s, L1_xattn_bv_s, L1_xattn_Wq_s, L1_xattn_bq_s, L1_xattn_Wk_c, L1_xattn_bk_c, L1_xattn_Wv_c, L1_xattn_bv_c, L1_xattn_Wg, L1_xattn_bg, L1_attn_Wq, L1_attn_Wk, L1_attn_Wv, L1_attn_Wc, L1_attn_Ltri, L1_ffn_router_w, L1_ffn_router_bias, L1_ffn_sw1, L1_ffn_sw3, L1_ffn_sw2, L1_ffn_ew1, L1_ffn_ew2):
    import jax
    import jax.numpy as jnp

    def _L0_xattn_ref(x, latents, mask, ln_x_g, ln_x_b, ln_l_g, ln_l_b, qn_g, kn_g, Wq, Wkv, Wout, bout):
        import jax, jax.numpy as jnp
        import numpy as np
        DIM = 128
        DIM_LATENT = 128
        DIM_HEAD = 64
        HEADS = 16
        INNER = HEADS * DIM_HEAD

        def layernorm(x, g, b, eps=1e-05):
            m = jnp.mean(x, axis=-1, keepdims=True)
            v = jnp.mean((x - m) ** 2, axis=-1, keepdims=True)
            return (x - m) / jnp.sqrt(v + eps) * g + b

        def rmsnorm(x, gamma, eps=1e-08):
            n = jnp.linalg.norm(x, axis=-1, keepdims=True) * x.shape[-1] ** (-0.5)
            return x / jnp.maximum(n, eps) * gamma
        b, n, _ = x.shape
        m = latents.shape[1]
        h, d = (HEADS, DIM_HEAD)
        scale = d ** (-0.5)
        xn = layernorm(x, ln_x_g, ln_x_b)
        ln = layernorm(latents, ln_l_g, ln_l_b)
        q = (ln @ Wq).reshape(b, m, h, d).transpose(0, 2, 1, 3)
        kv = jnp.concatenate([xn @ Wkv, ln @ Wkv], axis=1)
        kv = kv.reshape(b, n + m, 2, h, d)
        k = kv[:, :, 0].transpose(0, 2, 1, 3)
        v = kv[:, :, 1].transpose(0, 2, 1, 3)
        qn = rmsnorm(q, qn_g) * scale
        kn = rmsnorm(k, kn_g)
        sim = jnp.einsum('bhid,bhjd->bhij', qn, kn)
        max_neg = -jnp.finfo(sim.dtype).max
        padded_mask = jnp.concatenate([mask, jnp.ones((b, m), bool)], axis=1)
        sim = jnp.where(padded_mask[:, None, None, :], sim, max_neg)
        attn = jax.nn.softmax(sim.astype(jnp.float32), axis=-1).astype(sim.dtype)
        out = jnp.einsum('bhij,bhjd->bhid', attn, v)
        out = out.transpose(0, 2, 1, 3).reshape(b, m, h * d)
        return out @ Wout + bout

    def _L0_attn_ref(src, Wq, bq, Wk, bk, Wv, bv, Wo, bo, W1, b1, W2, b2, g1, be1, g2, be2):
        import jax, jax.numpy as jnp
        import numpy as np
        B, S, D, H, DH, FF = (4, 512, 128, 16, 64, 512)
        EPS = 1e-06

        def _layer_norm(x, g, b):
            m = jnp.mean(x, axis=-1, keepdims=True)
            v = jnp.mean(jnp.square(x - m), axis=-1, keepdims=True)
            return (x - m) * jax.lax.rsqrt(v + 1e-05) * g + b
        b, s = (src.shape[0], src.shape[1])
        q = (src @ Wq + bq).reshape(b, s, H, DH)
        k = (src @ Wk + bk).reshape(b, s, H, DH)
        v = (src @ Wv + bv).reshape(b, s, H, DH)
        Q = jax.nn.elu(q) + 1.0
        K = jax.nn.elu(k) + 1.0
        KV = jnp.einsum('bshd,bshm->bhdm', K, v)
        Z = 1.0 / (jnp.einsum('bshd,bhd->bsh', Q, K.sum(axis=1)) + EPS)
        o = jnp.einsum('bshd,bhdm,bsh->bshm', Q, KV, Z).reshape(b, s, H * DH)
        attn_out = o @ Wo + bo
        x = _layer_norm(src + attn_out, g1, be1)
        y = jax.nn.gelu(x @ W1 + b1, approximate=False) @ W2 + b2
        return _layer_norm(x + y, g2, be2)

    def _L0_ffn_ref(x, Wqkv, q_scale, k_scale, Wo, ln_g, ln_b, W1, b1, W2, b2):
        import jax, jax.numpy as jnp
        import numpy as np
        DIM = 128
        DEPTH = 6
        HEADS = 16
        DIM_HEAD = 64
        WINDOW = 32
        INNER = HEADS * DIM_HEAD
        DIM_INNER = int(DIM * 4 * 2 / 3)
        QK_SCALE = 8.0

        def shift_tokens(t):
            a, s = jnp.split(t, 2, -1)
            s = jnp.pad(s, ((0, 0), (1, 0), (0, 0)))[:, :-1]
            return jnp.concatenate([a, s], -1)

        def l2norm(t):
            return t / jnp.maximum(jnp.linalg.norm(t, axis=-1, keepdims=True), 1e-12)

        def rotate_half(x):
            x1, x2 = jnp.split(x, 2, -1)
            return jnp.concatenate([-x2, x1], -1)

        def rotary_tables(n):
            half = jnp.arange(0, DIM_HEAD, 2, dtype=jnp.float32)
            inv_freq = 1.0 / 10000.0 ** (half / DIM_HEAD)
            t = jnp.arange(n, dtype=jnp.float32)
            freqs = t[:, None] * inv_freq[None, :]
            freqs = jnp.concatenate([freqs, freqs], -1)
            base_scale = (half + 0.4 * DIM_HEAD) / (1.4 * DIM_HEAD)
            power = (t - n // 2) / (WINDOW // 2)
            scale = base_scale[None, :] ** power[:, None]
            scale = jnp.concatenate([scale, scale], -1)
            return (freqs, scale)

        def local_attention(q, k, v):
            b, h, n, d = q.shape
            w = WINDOW
            nw = n // w
            bq = q.reshape(b, h, nw, w, d)
            bk = k.reshape(b, h, nw, w, d)
            bv = v.reshape(b, h, nw, w, d)

            def look(t):
                p = jnp.pad(t, ((0, 0), (0, 0), (1, 0), (0, 0), (0, 0)))
                return jnp.concatenate([p[:, :, :nw], p[:, :, 1:]], axis=3)
            bk2, bv2 = (look(bk), look(bv))
            seq = jnp.arange(n).reshape(nw, w)
            seq_p = jnp.pad(seq, ((1, 0), (0, 0)), constant_values=-1)
            jt = jnp.concatenate([seq_p[:nw], seq_p[1:]], axis=1)
            it = seq[:, :, None]
            jb = jt[:, None, :]
            mask = (it < jb) | (it > jb + w) | (jb == -1)
            sim = jnp.einsum('bhwie,bhwje->bhwij', bq, bk2) * QK_SCALE
            sim = jnp.where(mask, -jnp.finfo(sim.dtype).max, sim)
            attn = jax.nn.softmax(sim, -1)
            out = jnp.einsum('bhwij,bhwje->bhwie', attn, bv2)
            return out.reshape(b, h, n, d)

        def attn_layer(x, Wqkv, qs, ksc, Wo):
            b, n, _ = x.shape
            qkv = x @ Wqkv
            q, k, v = jnp.split(qkv, 3, -1)
            sh = lambda t: t.reshape(b, n, HEADS, DIM_HEAD).transpose(0, 2, 1, 3)
            q, k, v = (sh(q), sh(k), sh(v))
            q = l2norm(q) * qs
            k = l2norm(k) * ksc
            freqs, scale = rotary_tables(n)
            cos, sin = (jnp.cos(freqs), jnp.sin(freqs))
            q = q * cos * scale + rotate_half(q) * sin * scale
            inv = 1.0 / scale
            k = k * cos * inv + rotate_half(k) * sin * inv
            out = local_attention(q, k, v)
            out = out.transpose(0, 2, 1, 3).reshape(b, n, INNER)
            return out @ Wo

        def ffn_layer(x, g, bln, W1, b1, W2, b2):
            mu = x.mean(-1, keepdims=True)
            var = ((x - mu) ** 2).mean(-1, keepdims=True)
            xn = (x - mu) / jnp.sqrt(var + 1e-05) * g + bln
            hg = xn @ W1 + b1
            a, gate = jnp.split(hg, 2, -1)
            return a * jax.nn.gelu(gate, approximate=False) @ W2 + b2
        for i in range(DEPTH):
            x = attn_layer(shift_tokens(x), Wqkv[i], q_scale[i], k_scale[i], Wo[i]) + x
            x = ffn_layer(shift_tokens(x), ln_g[i], ln_b[i], W1[i], b1[i], W2[i], b2[i]) + x
        return x

    def _L1_xattn_ref(char_emb, subword_emb, Wq_c, bq_c, Wk_s, bk_s, Wv_s, bv_s, Wq_s, bq_s, Wk_c, bk_c, Wv_c, bv_c, Wg, bg):
        import jax, jax.numpy as jnp
        import numpy as np
        H = 128
        B = 8
        L_CHAR = 256
        L_SUB = 128

        def _linear(x, W, b):
            return jnp.einsum('blh,oh->blo', x, W) + b

        def _interp_linear(x, out_len):
            L_in = x.shape[1]
            pos = (jnp.arange(out_len, dtype=x.dtype) + 0.5) * (L_in / out_len) - 0.5
            pos = jnp.clip(pos, 0.0, L_in - 1)
            lo = jnp.floor(pos).astype(jnp.int32)
            hi = jnp.minimum(lo + 1, L_in - 1)
            w = (pos - lo.astype(x.dtype))[None, :, None]
            return x[:, lo] * (1 - w) + x[:, hi] * w
        h = char_emb.shape[-1]
        scale = 1.0 / jnp.sqrt(jnp.asarray(h, char_emb.dtype))
        Q_char = _linear(char_emb, Wq_c, bq_c)
        K_sub = _linear(subword_emb, Wk_s, bk_s)
        V_sub = _linear(subword_emb, Wv_s, bv_s)
        scores = jnp.einsum('bqh,bkh->bqk', Q_char, K_sub) * scale
        char2sub = jnp.einsum('bqk,bkh->bqh', jax.nn.softmax(scores, axis=-1), V_sub)
        Q_sub = _linear(subword_emb, Wq_s, bq_s)
        K_char = _linear(char_emb, Wk_c, bk_c)
        V_char = _linear(char_emb, Wv_c, bv_c)
        scores2 = jnp.einsum('bqh,bkh->bqk', Q_sub, K_char) * scale
        sub2char = jnp.einsum('bqk,bkh->bqh', jax.nn.softmax(scores2, axis=-1), V_char)
        L_char = char_emb.shape[1]
        if sub2char.shape[1] != L_char:
            sub2char = _interp_linear(sub2char, L_char)
        gate_in = jnp.concatenate([char2sub, sub2char], axis=-1)
        gate = jax.nn.sigmoid(jnp.einsum('blh,oh->blo', gate_in, Wg) + bg)
        return gate * char2sub + (1 - gate) * sub2char

    def _L1_attn_ref(X, Wq, Wk, Wv, Wc, Ltri):
        import jax, jax.numpy as jnp
        import numpy as np
        B, L, D, H = (2, 256, 128, 16)
        d = D // H
        Bsz, Lq, Dm = X.shape
        Q = (X @ Wq.T).reshape(Bsz, Lq, H, d)
        K = (X @ Wk.T).reshape(Bsz, Lq, H, d)
        V = (X @ Wv.T).reshape(Bsz, Lq, H, d)
        KV = jnp.einsum('blhd,blhe->blhde', K, V)
        KVc = jnp.cumsum(KV, axis=1)
        Y = jnp.einsum('blhd,blhde->blhe', Q, KVc)
        mask = jnp.tril(jnp.ones((1, d, d), dtype=X.dtype))
        Lm = Ltri * mask
        Bm = Lm @ jnp.swapaxes(Lm, -2, -1)
        Y = jnp.einsum('hed,blhd->blhe', Bm, Y)
        Y = Y.reshape(Bsz, Lq, Dm)
        return Y @ Wc.T

    def _L1_ffn_ref(x, router_w, router_bias, sw1, sw3, sw2, ew1, ew2):
        import jax, jax.numpy as jnp
        import numpy as np
        D_MODEL = 128
        H_SHARED = 256
        H_ROUTED = 128
        N_EXPERTS = 8
        TOP_K = 2
        B, T, C = x.shape
        xf = x.reshape(-1, C)
        shared_out = jax.nn.silu(xf @ sw1) * (xf @ sw3) @ sw2
        s = jax.nn.sigmoid((xf @ router_w.T).astype(jnp.float32))
        sel_scores = s + router_bias.astype(jnp.float32)
        _, topk_idx = jax.lax.top_k(sel_scores, TOP_K)
        s_sel = jnp.take_along_axis(s, topk_idx, axis=1)
        denom = s_sel.sum(axis=1, keepdims=True)
        gates = jnp.where(denom > 1e-09, s_sel / (denom + 1e-09), 1.0 / TOP_K).astype(x.dtype)
        one_hot = jax.nn.one_hot(topk_idx, N_EXPERTS, dtype=x.dtype)
        comb = jnp.einsum('nke,nk->ne', one_hot, gates)
        h = jax.nn.gelu(jnp.einsum('nd,edh->neh', xf, ew1), approximate=False)
        y = jnp.einsum('neh,ehd->ned', h, ew2)
        routed_out = jnp.einsum('ned,ne->nd', y, comb)
        return (shared_out + routed_out).reshape(B, T, C)
    x = x + _L0_xattn_ref(ctx_1024, _layernorm(x, axis=-1), mask_BxS2_bf1, L0_xattn_ln_x_g, L0_xattn_ln_x_b, L0_xattn_ln_l_g, L0_xattn_ln_l_b, L0_xattn_qn_g, L0_xattn_kn_g, L0_xattn_Wq, L0_xattn_Wkv, L0_xattn_Wout, L0_xattn_bout)
    x = x + _L0_attn_ref(_layernorm(x, axis=-1), L0_attn_Wq, L0_attn_bq, L0_attn_Wk, L0_attn_bk, L0_attn_Wv, L0_attn_bv, L0_attn_Wo, L0_attn_bo, L0_attn_W1, L0_attn_b1, L0_attn_W2, L0_attn_b2, L0_attn_g1, L0_attn_be1, L0_attn_g2, L0_attn_be2)
    x = x + _L0_ffn_ref(_layernorm(x, axis=-1), L0_ffn_Wqkv, L0_ffn_q_scale, L0_ffn_k_scale, L0_ffn_Wo, L0_ffn_ln_g, L0_ffn_ln_b, L0_ffn_W1, L0_ffn_b1, L0_ffn_W2, L0_ffn_b2)
    x = x + _L1_xattn_ref(_layernorm(x, axis=-1), ctx_1024, L1_xattn_Wq_c, L1_xattn_bq_c, L1_xattn_Wk_s, L1_xattn_bk_s, L1_xattn_Wv_s, L1_xattn_bv_s, L1_xattn_Wq_s, L1_xattn_bq_s, L1_xattn_Wk_c, L1_xattn_bk_c, L1_xattn_Wv_c, L1_xattn_bv_c, L1_xattn_Wg, L1_xattn_bg)
    x = x + _L1_attn_ref(_layernorm(x, axis=-1), L1_attn_Wq, L1_attn_Wk, L1_attn_Wv, L1_attn_Wc, L1_attn_Ltri)
    x = x + _L1_ffn_ref(_layernorm(x, axis=-1), L1_ffn_router_w, L1_ffn_router_bias, L1_ffn_sw1, L1_ffn_sw3, L1_ffn_sw2, L1_ffn_ew1, L1_ffn_ew2)
    return x

_drawn_inputs = setup_inputs


def setup_inputs(seed=0):
    import zlib

    import numpy as np

    out = dict(_drawn_inputs(seed))
    spreads = {'L0_xattn_ln_x_g': (1.0, 0.6),
     'L0_xattn_ln_x_b': (0.0, 0.458),
     'L0_xattn_ln_l_g': (1.0, 0.6),
     'L0_xattn_ln_l_b': (0.0, 0.8),
     'L0_xattn_qn_g': (1.0, 0.6),
     'L0_xattn_kn_g': (1.0, 0.6),
     'L0_xattn_bout': (0.0, 0.1),
     'L0_attn_bq': (0.0, 2.0),
     'L0_attn_bk': (0.0, 2.0),
     'L0_attn_bv': (0.0, 0.1),
     'L0_attn_bo': (0.0, 0.1),
     'L0_attn_b1': (0.0, 0.508),
     'L0_attn_b2': (0.0, 0.1),
     'L0_attn_g1': (1.0, 0.2),
     'L0_attn_be1': (0.0, 0.1),
     'L0_attn_g2': (1.0, 0.2),
     'L0_attn_be2': (0.0, 0.1),
     'L0_ffn_q_scale': (1.0, 0.6),
     'L0_ffn_k_scale': (1.0, 0.6),
     'L0_ffn_ln_g': (1.0, 0.6),
     'L0_ffn_ln_b': (0.0, 0.8),
     'L0_ffn_b1': (0.0, 0.8),
     'L0_ffn_b2': (0.0, 0.1),
     'L1_ffn_router_bias': (0.0, 0.8)}
    factors = {'L0_attn_Wq': 200.0,
     'L0_attn_Wk': 171.236,
     'L0_attn_Wv': 3.437,
     'L0_ffn_W1': 3.757,
     'L0_ffn_W2': 3.683,
     'L1_xattn_Wq_c': 8.0,
     'L1_xattn_bq_c': 64.0,
     'L1_xattn_Wk_s': 8.0,
     'L1_xattn_bk_s': 200.0,
     'L1_xattn_bv_s': 8.0,
     'L1_xattn_Wq_s': 8.0,
     'L1_xattn_bq_s': 42.805,
     'L1_xattn_Wk_c': 8.0,
     'L1_xattn_bk_c': 200.0,
     'L1_xattn_Wv_c': 5.573,
     'L1_xattn_bv_c': 8.0,
     'L1_xattn_Wg': 8.0,
     'L1_xattn_bg': 61.193,
     'L1_attn_Wq': 8.0,
     'L1_attn_Wk': 8.0,
     'L1_attn_Wv': 8.0,
     'L1_attn_Wc': 8.0,
     'L1_attn_Ltri': 8.0,
     'L1_ffn_router_w': 8.0,
     'L1_ffn_sw1': 8.0,
     'L1_ffn_sw3': 8.0,
     'L1_ffn_sw2': 8.0,
     'L1_ffn_ew1': 8.0,
     'L1_ffn_ew2': 8.0}
    for name, (base, spread) in spreads.items():
        noise = np.random.default_rng([zlib.crc32(name.encode()), seed]).standard_normal(out[name].shape)
        drawn = base * np.exp(spread * noise) if base else spread * noise
        out[name] = jnp.asarray(drawn.astype(out[name].dtype))
    for name, factor in factors.items():
        out[name] = (out[name] * factor).astype(out[name].dtype)
    return out
```

```python
from contextlib import ExitStack

import concourse.bass as bass
import numpy as np
from concourse import mybir
from concourse.alu_op_type import AluOpType as ALU

F32 = mybir.dt.float32
U8 = mybir.dt.uint8
U32 = mybir.dt.uint32
ACT = mybir.ActivationFunctionType
AX = mybir.AxisListType

P = 128
B = 4
D = 128
H = 16
DH = 64
INNER = H * DH
PAIRS = INNER // P
CTX = 2048
CT = CTX // P
BANK = 512
BIG = 1e30


class Chain:

    def __init__(self, eng, sem):
        self.eng, self.sem, self.done, self.loops = eng, sem, 0, []

    def enter(self, i, per):
        self.loops.append((i, per, self.done))
        self.done = 0

    def leave(self, turns):
        i, per, before = self.loops.pop()
        assert self.done == per, (self.done, per)
        self.done = before + turns * per

    def link(self, ins):
        ins.then_inc(self.sem, 1)
        self.done += 1
        value = self.done
        for i, per, before in self.loops:
            value = i * per + (value + before)
        self.eng.wait_ge(self.sem, value)


def columns(nc_ap, n):
    return nc_ap.rearrange("(c p) -> p c", c=n)


def row(ap, n=P):
    return ap.rearrange("(a d) -> a d", a=1).partition_broadcast(n).rearrange("p a d -> p (a d)")


def step(eng, sem):
    eng.sem_inc(sem, 1)


class Stage:

    def __init__(self, nc, ctx, name):
        self.nc, self.ctx, self.name = nc, ctx, name

    def sb(self, name, shape, dt=F32):
        return self.ctx.enter_context(self.nc.sbuf_tensor(f"{self.name}_{name}", shape, dt))

    def ps(self, name, shape, dt=F32):
        return self.ctx.enter_context(self.nc.psum_tensor(f"{self.name}_{name}", shape, dt))

    def sem(self, name):
        return self.nc.alloc_semaphore(f"{self.name}_{name}")


class Norm:

    def __init__(self, s, tiles, mhalf, name="ln"):
        self.nc, self.tiles, self.mhalf = s.nc, tiles, mhalf
        self.stat, self.mv = s.sb(name + "_stat", [P, tiles, 6]), s.sb(name + "_mv", [P, tiles, 2])
        self.var, self.rstd = s.sb(name + "_var", [P, tiles]), s.sb(name + "_rstd", [P, tiles])
        self.var_ready, self.rstd_ready = s.sem(name + "_var_ready"), s.sem(name + "_rstd_ready")

    def vector(self, eng, own, src, dst, count, passed=None):
        nc = self.nc
        for t in range(self.tiles):
            last = nc.vector.bn_stats(self.stat[:, t, :], src[:, t, :])
        own.link(last)
        if passed is not None:
            step(eng, passed)
        for t in range(self.tiles):
            last = nc.vector.bn_aggr(self.mv[:, t, :], self.stat[:, t, :])
        own.link(last)
        nc.vector.tensor_scalar(self.var[:], self.mv[:, :, 1], 1e-5, None, ALU.add).then_inc(self.var_ready, 1)
        eng.wait_ge(self.rstd_ready, count)
        for t in range(self.tiles):
            last = nc.vector.tensor_scalar(dst[:, t, :], src[:, t, :], self.mv[:, t, 0:1], self.rstd[:, t:t + 1],
                                           ALU.subtract, ALU.mult)
        return last

    def pool(self, eng, count):
        eng.wait_ge(self.var_ready, count)
        self.nc.gpsimd.tensor_tensor(self.rstd[:], self.var[:], self.mhalf[:, 0:self.tiles], ALU.pow).then_inc(self.rstd_ready, 1)


def latent_cross_attention(nc, io, g):
    KT = CT + 1
    KEYS = KT * P
    NT = KT + 1
    LAG = 3
    EARLY = 2
    GIVEN = 1
    GROUPS = [range(a, min(a + 4, KT)) for a in range(0, KT, 4)]
    NG = len(GROUPS)
    with ExitStack() as ctx:
        s = Stage(nc, ctx, "xa")
        w_q = s.sb("w_q", [P, INNER])
        w_kv = s.sb("w_kv", [P, 2 * INNER])
        w_out = s.sb("w_out", [P, PAIRS, D])
        cols = s.sb("cols", [P, 8])
        rows = s.sb("rows", [P, 5, D])
        stat = s.sb("stat", [P, CT, 6])
        mv = s.sb("mv", [P, CT, 2])
        ve = s.sb("ve", [P, CT])
        rstd = s.sb("rstd", [P, CT])
        lat = s.sb("lat", [P, B, D])
        lat_T = s.sb("lat_T", [P, B, P])
        ctx_raw = s.sb("ctx_raw", [P, CT, D])
        z = s.sb("z", [P, CT, D])
        xn = s.sb("xn", [P, KT, D])
        xn_T = s.sb("xn_T", [P, KEYS])
        maskb = s.sb("maskb", [P, CTX], U8)
        pen = s.sb("pen", [P, KEYS])
        ss, root, inv, rn = (s.sb(n, [P, 2, H]) for n in ("ss", "root", "inv", "rn"))
        err = s.sb("err", [P, H])
        kn_T = s.sb("kn_T", [P, PAIRS, KEYS])
        q_T = s.sb("q_T", [P, PAIRS, P])
        q_head = s.sb("q_head", [P, 2, P])
        prob = s.sb("prob", [P, 2, KEYS])
        sq = prob[:, 0, 0:2 * INNER].rearrange("p (a n) -> p a n", a=2)
        kn = prob[:, 1, 0:2 * INNER].rearrange("p (a n) -> p a n", a=2)
        mx = s.sb("mx", [P, 2, 4])
        nmax = s.sb("nmax", [P, 2])
        psumr = s.sb("psumr", [P, 2])
        rsum = s.sb("rsum", [P, 2])
        p_T = s.sb("p_T", [P, KT, 2, P])
        o_T = s.sb("o_T", [P, 2 * P])
        att = s.sb("att", [P, INNER])
        att_T = s.sb("att_T", [P, PAIRS, P])
        bank = s.ps("bank", [P, 8, BANK])

        w_in = s.sem("w_in")
        ctx_in = s.sem("ctx_in")
        mask_in = s.sem("mask_in")
        passed = s.sem("passed")
        dve_own, act_own, pool_own = s.sem("dve_own"), s.sem("act_own"), s.sem("pool_own")
        var_ready, rstd_ready = s.sem("var_ready"), s.sem("rstd_ready")
        z_ready, zT_ready, xnT_ready, xn_ready = s.sem("z_ready"), s.sem("zT_ready"), s.sem("xnT_ready"), s.sem("xn_ready")
        pen_ready = s.sem("pen_ready")
        proj_ready, sq_ready, ss_ready, root_ready, inv_ready, rn_ready, kn_ready = (s.sem(n) for n in
            ("proj_ready", "sq_ready", "ss_ready", "root_ready", "inv_ready", "rn_ready", "kn_ready"))
        kn_turned, knT_ready = s.sem("kn_turned"), s.sem("knT_ready")
        qh_ready, sim_ready, masked, max_ready, exp_ready = (s.sem(n) for n in
            ("qh_ready", "sim_ready", "masked", "max_ready", "exp_ready"))
        p_turned, pT_ready, o_ready, oT_ready, v_ready, att_ready = (s.sem(n) for n in
            ("p_turned", "pT_ready", "o_ready", "oT_ready", "v_ready", "att_ready"))
        lat_ready, latT_turned, latT_ready = s.sem("lat_ready"), s.sem("latT_turned"), s.sem("latT_ready")
        att_turned, attT_ready, y_ready, x_ready = (s.sem(n) for n in ("att_turned", "attT_ready", "y_ready", "x_ready"))

        mask_dram = io["mask_BxS2_bf1"]
        x_res, ident, ones_row = g["x_res"], g["ident"], g["ones_row"]
        block = ctx.enter_context(nc.Block())

        @block.sync
        def _(sp):
            sp.dma_start(w_q[:], io["L0_xattn_Wq"]).then_inc(w_in, 16)
            sp.dma_start(w_kv[:], io["L0_xattn_Wkv"]).then_inc(w_in, 16)
            sp.dma_start(w_out[:], io["L0_xattn_Wout"].rearrange("(c p) n -> p c n", p=P)).then_inc(w_in, 16)
            for j, n in enumerate(("ln_x_g", "ln_x_b", "ln_l_g", "ln_l_b")):
                sp.dma_start(cols[:, j:j + 1], columns(io["L0_xattn_" + n], 1)).then_inc(w_in, 16)
                sp.dma_start(rows[:, j, :], row(io["L0_xattn_" + n])).then_inc(w_in, 16)
            sp.dma_start(rows[:, 4, :], row(io["L0_xattn_bout"])).then_inc(w_in, 16)
            for j, n in enumerate(("qn_g", "kn_g")):
                for half in range(2):
                    sp.dma_start(cols[half * DH:(half + 1) * DH, 5 + j:6 + j],
                                 io["L0_xattn_" + n].rearrange("(p a) -> p a", a=1)).then_inc(w_in, 16)
            with sp.Fori(0, B) as b:
                sp.wait_ge(z_ready, b * CT + GIVEN)
                step(sp, passed)
                sp.dma_start(ctx_raw[:], io["ctx_1024"][bass.ds(b, 1)].rearrange("a (p t) d -> (a p) t d", p=P)).then_inc(ctx_in, 16)
                sp.wait_ge(pen_ready, b + GIVEN)
                step(sp, passed)
                sp.dma_start(maskb[:], mask_dram[bass.ds(b, 1)].partition_broadcast(P).rearrange("p a n -> p (a n)")).then_inc(mask_in, 16)
        W_LOADS = 3 + 8 + 1 + 4

        @block.gpsimd
        def _(pool):
            def power(out, base, expo):
                return nc.gpsimd.tensor_tensor(out, base, expo, ALU.pow)

            def queries(b, p):
                if isinstance(p, int):
                    pool.wait_ge(knT_ready, b * NT + 1)
                    step(pool, passed)
                for e in range(2):
                    if not isinstance(p, int):
                        pool.wait_ge(sim_ready, b * (H * NG) + (p * (2 * NG) + (e - 1) * NG) + GIVEN)
                    half = slice(e * DH, (e + 1) * DH)
                    nc.gpsimd.tensor_copy(q_head[half, e, :], q_T[half, bass.ds(p, 1), :].rearrange("p a d -> p (a d)")).then_inc(qh_ready, 1)

            own = Chain(pool, pool_own)
            nc.gpsimd.memset(pen[:, CTX:KEYS], 0.0)
            own.link(nc.gpsimd.memset(q_head[:], 0.0))
            for n in range(2):
                pool.wait_ge(var_ready, n + 1)
                power(rstd[:, 0:B], ve[:, 0:B], g["mhalf"][:, 0:B]).then_inc(rstd_ready, 1)
            with pool.Fori(0, B) as b:
                own.enter(b, 3 * NT + CT)
                pool.wait_ge(var_ready, b + 3)
                power(rstd[:], ve[:], g["mhalf"][:, 0:CT]).then_inc(rstd_ready, 1)
                pool.wait_ge(z_ready, b * CT + CT + GIVEN)
                pool.wait_ge(o_ready, b * PAIRS + GIVEN)
                for t in range(NT):
                    k = t % 2
                    pool.wait_ge(inv_ready, b * NT + (t + 1))
                    own.link(nc.gpsimd.tensor_tensor(err[:], inv[:, k, :], inv[:, k, :], ALU.mult))
                    own.link(nc.gpsimd.tensor_tensor(err[:], err[:], ss[:, k, :], ALU.mult))
                    step(pool, passed)
                    own.link(nc.gpsimd.tensor_scalar(err[:], err[:], -0.5, 1.5, ALU.mult, ALU.add))
                    nc.gpsimd.tensor_tensor(rn[:, k, :], inv[:, k, :], err[:], ALU.mult).then_inc(rn_ready, 1)
                    if t == LAG + 1:
                        pool.wait_ge(rn_ready, b * NT + (t + 1))
                        queries(b, 0)
                        pool.wait_ge(qh_ready, b * H + 2)
                    if t < CT:
                        own.link(nc.gpsimd.tensor_tensor(xn[:, t, :], z[:, t, :], rows[:, 0, :], ALU.mult))
                        nc.gpsimd.tensor_tensor(xn[:, t, :], xn[:, t, :], rows[:, 1, :], ALU.add).then_inc(xn_ready, 1)
                    elif t == CT:
                        nc.gpsimd.tensor_copy(xn[:, CT, :], lat[:, bass.ds(b, 1), :].rearrange("p a d -> p (a d)")).then_inc(xn_ready, 1)
                with pool.Fori(0, PAIRS - 1) as p:
                    queries(b, p + 1)
                own.leave(B)

        @block.tensor
        def _(pe):
            for freed in (o_ready, sim_ready):
                pe.sem_inc(freed, GIVEN)
            def project(b, t):
                if t >= LAG:
                    pe.wait_ge(kn_ready, b * NT + (t - LAG + 1))
                if t == 0:
                    pe.wait_ge(xnT_ready, b * 5 + 5)
                tile = t - 1 if t > 0 else CT
                keys = xn_T[:, tile * P:(tile + 1) * P]
                for c in range(2):
                    w = w_q[:, c * BANK:(c + 1) * BANK] if t == 0 else w_kv[:, c * BANK:(c + 1) * BANK]
                    mm = nc.tensor.matmul(bank[:, 2 * (t % LAG) + c, :], keys, w, start=True, stop=True)
                mm.then_inc(proj_ready, 1)

            def turn(b, t):
                pe.wait_ge(kn_ready, b * NT + (t + 1))
                if t >= 1:
                    pe.wait_ge(knT_ready, b * NT + t)
                else:
                    pe.wait_ge(x_ready, b + GIVEN)
                for c in range(PAIRS):
                    mm = nc.tensor.transpose(bank[:, 6 + c // 4, (c % 4) * P:(c % 4 + 1) * P],
                                             kn[:, t % 2, c * P:(c + 1) * P], ident[:])
                mm.then_inc(kn_turned, 1)

            def score(b, p, e, c, first=False):
                head = p * 2 + e
                if c == 0:
                    pe.wait_ge(qh_ready, b * H + (head + 1))
                if first:
                    pe.wait_ge(knT_ready, b * NT + min(4 * c + 5, NT))
                    pe.wait_ge(kn_ready, b * NT + (NT - LAG + 1 + c // 2))
                if not first and c in (0, 2, 4):
                    pe.wait_ge(masked, b * (3 * H) + (head * 3 + (c // 2 - 2)))
                n = len(GROUPS[c]) * P
                nc.tensor.matmul(bank[:, c, 0:n], q_head[:, e, :],
                                 kn_T[:, bass.ds(p, 1), c * BANK:c * BANK + n].rearrange("p a n -> p (a n)"),
                                 start=True, stop=True).then_inc(sim_ready, 1)

            def turn_prob(b, p, e, n):
                if n == 0:
                    pe.wait_ge(exp_ready, b * H + (p * 2 + e + 1))
                k = NG * e + n
                pe.wait_ge(pT_ready, b * (H * NG) + (p * (2 * NG) + max(k - 1, 0)) + GIVEN)
                for j, t in enumerate(GROUPS[n]):
                    mm = nc.tensor.transpose(bank[:, 5 + k % 2, j * P:(j + 1) * P], prob[:, e, t * P:(t + 1) * P], ident[:])
                mm.then_inc(p_turned, 1)

            def turn_and_score(b, p, e, scored=None, valued=None):
                for n in range(NG):
                    turn_prob(b, p, e, n)
                    if scored is not None:
                        score(b, scored, e, n)
                    if n == 1 and valued is not None:
                        value(b, valued)

            def turn_context(b):
                if not (isinstance(b, int) and b == 0):
                    pe.wait_ge(masked, b * (3 * H))
                    step(pe, passed)
                for c in range(4):
                    pe.wait_ge(z_ready, b * CT + (4 * c + 4) + GIVEN)
                    for j in range(4):
                        mm = nc.tensor.transpose(bank[:, c, j * P:(j + 1) * P], z[:, 4 * c + j, :], ident[:])
                    mm.then_inc(zT_ready, 1)

            def gather(b, p):
                pe.wait_ge(pT_ready, b * (H * NG) + (p * (2 * NG) + 2 * NG) + GIVEN)
                pe.wait_ge(att_ready, b * PAIRS + (p + GIVEN))
                for t in range(KT):
                    mm = nc.tensor.matmul(bank[:, 7, 0:2 * P], xn[:, t, :], p_T[:, t, :, :].rearrange("p e q -> p (e q)"),
                                          start=(t == 0), stop=(t == KT - 1))
                mm.then_inc(o_ready, 1)

            def value(b, p):
                pe.wait_ge(oT_ready, b * PAIRS + (p + 1))
                w = w_kv[:, INNER:2 * INNER].rearrange("p (c n) -> p c n", n=P)
                for e in range(2):
                    mm = nc.tensor.matmul(bank[:, 7, 2 * P + e * DH:2 * P + (e + 1) * DH], o_T[:, e * P:(e + 1) * P],
                                          w[:, bass.ds(p, 1), e * DH:(e + 1) * DH].rearrange("p a n -> p (a n)"),
                                          start=True, stop=True)
                mm.then_inc(v_ready, 1)

            pe.wait_ge(lat_ready, 1)
            for t in range(B):
                mm = nc.tensor.transpose(bank[:, 0, t * P:(t + 1) * P], z[:, t, :], ident[:])
            mm.then_inc(latT_turned, 1)
            pe.wait_ge(latT_ready, 1)
            pe.wait_ge(w_in, 16 * W_LOADS)

            def batch(b, last):
                for t in range(EARLY, NT + LAG):
                    if t < NT:
                        project(b, t)
                    if t >= LAG:
                        turn(b, t - LAG)
                    if t == NT + 1:
                        score(b, 0, 0, 0, first=True)
                        score(b, 0, 0, 1, first=True)
                for c in range(2, NG):
                    score(b, 0, 0, c, first=True)
                for c in range(NG):
                    score(b, 0, 1, c)
                turn_and_score(b, 0, 0, scored=1)
                pe.wait_ge(xn_ready, b * KT + KT)
                step(pe, passed)
                with pe.Fori(0, PAIRS - 2) as p:
                    turn_and_score(b, p, 1, scored=p + 1)
                    gather(b, p)
                    turn_and_score(b, p + 1, 0, scored=p + 2, valued=p)
                turn_and_score(b, PAIRS - 2, 1, scored=PAIRS - 1)
                gather(b, PAIRS - 2)
                turn_and_score(b, PAIRS - 1, 0, valued=PAIRS - 2)
                turn_and_score(b, PAIRS - 1, 1)
                gather(b, PAIRS - 1)
                value(b, PAIRS - 1)
                if not last:
                    turn_context(b + 1)
                pe.wait_ge(att_ready, b * PAIRS + PAIRS + GIVEN)
                for c in range(PAIRS):
                    mm = nc.tensor.transpose(bank[:, 5 + c // 4, (c % 4) * P:(c % 4 + 1) * P], att[:, c * P:(c + 1) * P], ident[:])
                mm.then_inc(att_turned, 1)
                if not last:
                    for t in range(EARLY):
                        project(b + 1, t)
                pe.wait_ge(attT_ready, b + 1)
                for c in range(PAIRS):
                    mm = nc.tensor.matmul(bank[:, 7, 3 * P:4 * P], att_T[:, c, :], w_out[:, c, :], start=(c == 0), stop=(c == PAIRS - 1))
                mm.then_inc(y_ready, 1)

            turn_context(0)
            for t in range(EARLY):
                project(0, t)
            with pe.Fori(0, B - 1) as b:
                batch(b, last=False)
            batch(B - 1, last=True)

        @block.scalar
        def _(act):
            act.sem_inc(pT_ready, GIVEN)
            own = Chain(act, act_own)

            def square(b, t):
                act.wait_ge(proj_ready, b * NT + (t + 1))
                if t >= 2:
                    act.wait_ge(ss_ready, b * NT + (t - 1))
                src = bank[:, 2 * (t % LAG):2 * (t % LAG) + 2, :].rearrange("p a n -> p (a n)")
                nc.scalar.activation(sq[:, t % 2, :], src, ACT.Square, scale=DH ** -0.5).then_inc(sq_ready, 1)

            def square_root(b, t):
                act.wait_ge(ss_ready, b * NT + (t + 1))
                nc.scalar.activation(root[:, t % 2, :], ss[:, t % 2, :], ACT.Sqrt).then_inc(root_ready, 1)

            def keep_turned(b, t):
                act.wait_ge(kn_turned, b * NT + (t + 1))
                src = bank[:, 6:8, :].rearrange("p a (c k) -> p (a c) k", k=P)
                if t == 0:
                    nc.scalar.activation(q_T[:], src, ACT.Copy, scale=cols[:, 4:5]).then_inc(knT_ready, 1)
                else:
                    nc.scalar.copy(kn_T[:, :, (t - 1) * P:t * P], src).then_inc(knT_ready, 1)

            def exponent(b, p, e):
                act.wait_ge(max_ready, b * H + (p * 2 + e + 1))
                nc.scalar.activation(prob[:, e, :], prob[:, e, :], ACT.Exp, bias=nmax[:, e:e + 1],
                                     accum_out=psumr[:, e:e + 1]).then_inc(exp_ready, 1)

            def keep_prob(b, p, e):
                for n, tiles in enumerate(GROUPS):
                    k = NG * e + n
                    act.wait_ge(p_turned, b * (H * NG) + (p * (2 * NG) + (k + 1)))
                    if k == 0:
                        act.wait_ge(o_ready, b * PAIRS + (p + GIVEN))
                    m = len(tiles)
                    nc.scalar.copy(p_T[:, tiles[0]:tiles[0] + m, e, :],
                                   bank[:, 5 + k % 2, 0:m * P].rearrange("p (t q) -> p t q", t=m)).then_inc(pT_ready, 1)

            act.wait_ge(latT_turned, 1)
            act.wait_ge(w_in, 16 * W_LOADS)
            own.link(nc.scalar.activation(cols[:, 4:5], cols[:, 5:6], ACT.Copy, scale=cols[:, 6:7]))
            own.link(nc.scalar.mul(cols[:, 4:5], cols[:, 4:5], DH ** -0.5))
            nc.scalar.activation(lat_T[:].rearrange("p b t -> p (b t)"), bank[:, 0, :], ACT.Identity,
                                 bias=cols[:, 3:4], scale=cols[:, 2:3]).then_inc(latT_ready, 1)
            act.wait_ge(latT_ready, 1)

            def keep_context(b):
                for c in range(4):
                    act.wait_ge(zT_ready, b * 4 + (c + 1))
                    nc.scalar.activation(xn_T[:, c * BANK:(c + 1) * BANK], bank[:, c, :], ACT.Identity,
                                         bias=cols[:, 1:2], scale=cols[:, 0:1]).then_inc(xnT_ready, 1)
                nc.scalar.copy(xn_T[:, CTX:KEYS], lat_T[:, bass.ds(b, 1), :].rearrange("p a t -> p (a t)")).then_inc(xnT_ready, 1)

            def batch(b, last):
                for t in range(NT + LAG):
                    if t < NT:
                        square(b, t)
                    if 1 <= t <= NT:
                        square_root(b, t - 1)
                    if t >= LAG:
                        keep_turned(b, t - LAG)
                exponent(b, 0, 0)
                exponent(b, 0, 1)
                with act.Fori(0, PAIRS - 1) as p:
                    keep_prob(b, p, 0)
                    keep_prob(b, p, 1)
                    exponent(b, p + 1, 0)
                    exponent(b, p + 1, 1)
                keep_prob(b, PAIRS - 1, 0)
                keep_prob(b, PAIRS - 1, 1)
                if not last:
                    keep_context(b + 1)
                act.wait_ge(att_turned, b + 1)
                nc.scalar.copy(att_T[:].rearrange("p c q -> p (c q)"), bank[:, 5:7, :].rearrange("p a n -> p (a n)")).then_inc(attT_ready, 1)

            keep_context(0)
            with act.Fori(0, B - 1) as b:
                batch(b, last=False)
            batch(B - 1, last=True)

        @block.vector
        def _(dve):
            for freed in (z_ready, pen_ready, x_ready, att_ready):
                dve.sem_inc(freed, GIVEN)
            own = Chain(dve, dve_own)

            def layer_norm(src, dst, tiles, rstd_count, signal=None):
                for t in range(tiles):
                    last = nc.vector.bn_stats(stat[:, t, :], src[:, t, :])
                own.link(last)
                step(dve, passed)
                for t in range(tiles):
                    last = nc.vector.bn_aggr(mv[:, t, :], stat[:, t, :])
                own.link(last)
                nc.vector.tensor_scalar(ve[:, 0:tiles], mv[:, 0:tiles, 1], 1e-5, None, ALU.add).then_inc(var_ready, 1)
                dve.wait_ge(rstd_ready, rstd_count)
                for t in range(tiles):
                    last = nc.vector.tensor_scalar(dst[:, t, :], src[:, t, :], mv[:, t, 0:1], rstd[:, t:t + 1],
                                                   ALU.subtract, ALU.mult)
                    if signal:
                        last.then_inc(signal, 1)
                return last

            def reduce(b, t):
                dve.wait_ge(sq_ready, b * NT + (t + 1))
                own.link(nc.vector.tensor_reduce(ss[:, t % 2, :], sq[:, t % 2, :].rearrange("p (h e) -> p h e", e=DH), AX.X, ALU.add))
                nc.vector.tensor_scalar(ss[:, t % 2, :], ss[:, t % 2, :], 1e-16, None, ALU.max).then_inc(ss_ready, 1)

            def invert(b, t):
                dve.wait_ge(root_ready, b * NT + (t + 1))
                nc.vector.reciprocal(inv[:, t % 2, :], root[:, t % 2, :]).then_inc(inv_ready, 1)

            def normalise(b, t):
                dve.wait_ge(rn_ready, b * NT + (t + 1))
                if t >= 2:
                    dve.wait_ge(kn_turned, b * NT + (t - 1))
                src = bank[:, 2 * (t % LAG):2 * (t % LAG) + 2, :].rearrange("p a (h e) -> p (a h) e", e=DH)
                nc.vector.tensor_tensor(kn[:, t % 2, :].rearrange("p (h e) -> p h e", e=DH), src,
                                        rn[:, t % 2, :].unsqueeze(2).to_broadcast([P, H, DH]), ALU.mult).then_inc(kn_ready, 1)

            def mask_and_max(b, p, e, first=False):
                head = p * 2 + e
                for n, (lo, hi, banks) in enumerate(((0, 1024, 2), (1024, 2048, 4), (2048, KEYS, 5))):
                    dve.wait_ge(sim_ready, b * (H * NG) + (head * NG + banks) + GIVEN)
                    if not first:
                        dve.wait_ge(p_turned, b * (H * NG) + ((p - 1) * (2 * NG) + (e * NG + banks)))
                    step(dve, passed)
                    src = bank[:, lo // BANK:(hi + BANK - 1) // BANK, :].rearrange("p a n -> p (a n)")[:, 0:hi - lo]
                    nc.vector.tensor_tensor_reduce(out=prob[:, e, lo:hi], in0=src, in1=pen[:, lo:hi], scale=1.0,
                                                   scalar=-3e38, op0=ALU.add, op1=ALU.max,
                                                   accum_out=mx[:, e, n:n + 1]).then_inc(masked, 1)
                dve.wait_ge(masked, b * (3 * H) + (head * 3 + 3))
                nc.vector.tensor_reduce(nmax[:, e:e + 1], mx[:, e, 0:3], AX.X, ALU.max, negate=True).then_inc(max_ready, 1)

            def invert_sums(b, p):
                dve.wait_ge(exp_ready, b * H + (p * 2 + 2))
                own.link(nc.vector.reciprocal(rsum[:], psumr[:]))

            def attend(b, p):
                dve.wait_ge(o_ready, b * PAIRS + (p + 1) + GIVEN)
                nc.vector.tensor_copy(o_T[:], bank[:, 7, 0:2 * P]).then_inc(oT_ready, 1)
                dve.wait_ge(v_ready, b * PAIRS + (p + 1))
                dst = att[:].rearrange("p (c e d) -> p c e d", e=2, d=DH)[:, bass.ds(p, 1), :, :].rearrange("p c e d -> p (c e) d")
                nc.vector.tensor_tensor(dst, bank[:, 7, 2 * P:3 * P].rearrange("p (e d) -> p e d", e=2),
                                        rsum[:].unsqueeze(2).to_broadcast([P, 2, DH]), ALU.mult).then_inc(att_ready, 1)
                dve.wait_ge(att_ready, b * PAIRS + (p + 1) + GIVEN)

            last = layer_norm(x_res, lat, B, 1)
            own.link(last)
            last = layer_norm(lat, z, B, 2)
            own.link(last)
            dve.wait_ge(w_in, 16 * W_LOADS)
            own.link(nc.vector.tensor_tensor(lat[:], z[:, 0:B, :], rows[:, 2:3, :].to_broadcast([P, B, D]), ALU.mult))
            nc.vector.tensor_tensor(lat[:], lat[:], rows[:, 3:4, :].to_broadcast([P, B, D]), ALU.add).then_inc(lat_ready, 1)
            dve.wait_ge(latT_turned, 1)

            def prepare(b):
                dve.wait_ge(ctx_in, b * 16 + 16)
                layer_norm(ctx_raw, z, CT, b + 3, signal=z_ready)
                dve.wait_ge(mask_in, b * 16 + 16)
                nc.vector.tensor_scalar(pen[:, 0:CTX].rearrange("a (t p) -> a t p", p=P), maskb[:].rearrange("a (p t) -> a t p", p=P),
                                        1.0, BIG, ALU.subtract, ALU.mult).then_inc(pen_ready, 1)

            def attention(b, last):
                for t in range(NT + 1):
                    if t >= 1:
                        invert(b, t - 1)
                    if t < NT:
                        reduce(b, t)
                    if t >= 1:
                        normalise(b, t - 1)
                dve.wait_ge(pen_ready, b + 1 + GIVEN)
                step(dve, passed)
                mask_and_max(b, 0, 0, first=True)
                mask_and_max(b, 0, 1, first=True)
                invert_sums(b, 0)
                mask_and_max(b, 1, 0)
                with dve.Fori(0, PAIRS - 2) as p:
                    own.enter(p, 1)
                    mask_and_max(b, p + 1, 1)
                    attend(b, p)
                    invert_sums(b, p + 1)
                    mask_and_max(b, p + 2, 0)
                    own.leave(PAIRS - 2)
                mask_and_max(b, PAIRS - 1, 1)
                attend(b, PAIRS - 2)
                invert_sums(b, PAIRS - 1)
                if not last:
                    dve.wait_ge(xn_ready, b * KT + KT)
                    prepare(b + 1)
                attend(b, PAIRS - 1)
                xb = x_res[:, bass.ds(b, 1), :].rearrange("p a d -> p (a d)")
                own.link(nc.vector.tensor_tensor(xb, xb, rows[:, 4, :], ALU.add))
                dve.wait_ge(y_ready, b + 1)
                nc.vector.tensor_tensor(xb, xb, bank[:, 7, 3 * P:4 * P], ALU.add).then_inc(x_ready, 1)

            prepare(0)
            with dve.Fori(0, B - 1) as b:
                own.enter(b, NT + PAIRS + 1 + 2)
                attention(b, last=False)
                own.leave(B - 1)
            attention(B - 1, last=True)


def linear_attention(nc, io, g):
    NF = 4
    W = 130
    GROUPS = [range(0, 3), range(3, 6), range(6, PAIRS)]
    with ExitStack() as ctx:
        s = Stage(nc, ctx, "la")
        w_q, w_k, w_v = (s.sb(n, [P, INNER]) for n in ("w_q", "w_k", "w_v"))
        w_o = s.sb("w_o", [P, PAIRS, D])
        w_1, w_2 = s.sb("w_1", [P, NF * P]), s.sb("w_2", [P, NF, D])
        row_k, row_v = s.sb("row_k", [P, INNER]), s.sb("row_v", [P, INNER])
        rows = s.sb("rows", [P, 6, D])
        col_q, col_1 = s.sb("col_q", [P, PAIRS]), s.sb("col_1", [P, NF])
        col_nq = s.sb("col_nq", [P, PAIRS])
        norm = Norm(s, B, g["mhalf"])
        src, src_T = s.sb("src", [P, B, D]), s.sb("src_T", [P, B * P])
        k_lin, k_neg, k_exp = (s.sb(n, [P, 2, INNER]) for n in ("k_lin", "k_neg", "k_exp"))
        k_phi = s.sb("k_phi", [P, B, INNER])
        v_one = s.sb("v_one", [P, B, PAIRS, P + 1])
        q_pos, q_neg, q_exp = (s.sb(n, [P, 2, B * P]) for n in ("q_pos", "q_neg", "q_exp"))
        q_phi = s.sb("q_phi", [P, PAIRS, B * P])
        kv = s.sb("kv", [P, 2, PAIRS, W])
        den, o_tok = s.sb("den", [P, H]), s.sb("o_tok", [P, INNER])
        o_T = s.sb("o_T", [P, PAIRS, P])
        h, x1, x1_T = s.sb("h", [P, B, D]), s.sb("x1", [P, B, D]), s.sb("x1_T", [P, B * P])
        f_T = s.sb("f_T", [P, NF, B * P])
        bank = s.ps("bank", [P, 8, BANK])
        w_in, dve_own, pool_own = s.sem("w_in"), s.sem("dve_own"), s.sem("pool_own")
        ones_ready, src_ready, src_turned, srcT_ready, kv_proj = (s.sem(n) for n in
            ("ones_ready", "src_ready", "src_turned", "srcT_ready", "kv_proj"))
        klin_ready, v_ready, kneg_ready, kexp_ready, kphi_ready = (s.sem(n) for n in
            ("klin_ready", "v_ready", "kneg_ready", "kexp_ready", "kphi_ready"))
        q_proj, qpos_ready, qexp_ready, qphi_ready = (s.sem(n) for n in ("q_proj", "qpos_ready", "qexp_ready", "qphi_ready"))
        kv_made, kv_ready, num_ready, o_ready, o_turned, oT_ready, wo_ready, h_ready = (s.sem(n) for n in
            ("kv_made", "kv_ready", "num_ready", "o_ready", "o_turned", "oT_ready", "wo_ready", "h_ready"))
        x1_ready, x1_turned, x1T_ready, f_proj, f_ready, y_ready = (s.sem(n) for n in
            ("x1_ready", "x1_turned", "x1T_ready", "f_proj", "f_ready", "y_ready"))
        x_res, ident = g["x_res"], g["ident"]
        block = ctx.enter_context(nc.Block())
        N_IN = 6 + 2 + 6 + 2

        @block.sync
        def _(sp):
            for w, n in ((w_k, "Wk"), (w_v, "Wv"), (w_q, "Wq"), (w_1, "W1")):
                sp.dma_start(w[:], io["L0_attn_" + n]).then_inc(w_in, 16)
            for w, n in ((w_o, "Wo"), (w_2, "W2")):
                sp.dma_start(w[:], io["L0_attn_" + n].rearrange("(c p) n -> p c n", p=P)).then_inc(w_in, 16)
            for w, n in ((row_k, "bk"), (row_v, "bv")):
                sp.dma_start(w[:], row(io["L0_attn_" + n])).then_inc(w_in, 16)
            for j, n in enumerate(("bo", "g1", "be1", "b2", "g2", "be2")):
                sp.dma_start(rows[:, j, :], row(io["L0_attn_" + n])).then_inc(w_in, 16)
            sp.dma_start(col_q[:], io["L0_attn_bq"]).then_inc(w_in, 16)
            sp.dma_start(col_1[:], io["L0_attn_b1"]).then_inc(w_in, 16)

        @block.gpsimd
        def _(pool):
            nc.gpsimd.memset(v_one[:, :, :, P:P + 1], 1.0)
            nc.gpsimd.memset(kv[:], 0.0).then_inc(ones_ready, 1)
            for n in range(3):
                norm.pool(pool, n + 1)
                if n == 0:
                    for p in range(PAIRS):
                        pool.wait_ge(qpos_ready, p + 1)
                        pool.wait_ge(qexp_ready, p + 1)
                        nc.gpsimd.tensor_tensor(q_phi[:, p, :], q_pos[:, p % 2, :], q_exp[:, p % 2, :], ALU.add).then_inc(qphi_ready, 1)

        @block.tensor
        def _(pe):
            pe.wait_ge(src_ready, 1)
            for b in range(B):
                mm = nc.tensor.transpose(bank[:, 0, b * P:(b + 1) * P], src[:, b, :], ident[:])
            mm.then_inc(src_turned, 1)
            pe.wait_ge(srcT_ready, 1)
            pe.wait_ge(w_in, 16 * N_IN)
            for b in range(B):
                if b >= 2:
                    pe.wait_ge(klin_ready, b - 1)
                    pe.wait_ge(v_ready, b - 1)
                for c, w in enumerate((w_k[:, 0:BANK], w_k[:, BANK:], w_v[:, 0:BANK], w_v[:, BANK:])):
                    nc.tensor.matmul(bank[:, 4 * (b % 2) + c, :], src_T[:, b * P:(b + 1) * P], w, start=True, stop=True).then_inc(kv_proj, 1)
            for p in range(PAIRS):
                if p == 0:
                    pe.wait_ge(klin_ready, 3)
                    pe.wait_ge(v_ready, 3)
                if p == 4:
                    pe.wait_ge(klin_ready, 4)
                    pe.wait_ge(v_ready, 4)
                nc.tensor.matmul(bank[:, p, :], w_q[:, p * P:(p + 1) * P], src_T[:], start=True, stop=True).then_inc(q_proj, 1)
            for b in range(B):
                pe.wait_ge(kphi_ready, b + 1)
                if b == 0:
                    pe.wait_ge(qpos_ready, 3)
                    pe.wait_ge(qexp_ready, 3)
                for n, pairs in enumerate(GROUPS):
                    if b >= 1:
                        pe.wait_ge(kv_ready, b)
                    for j, p in enumerate(pairs):
                        mm = nc.tensor.matmul(bank[:, n, j * (P + 1):(j + 1) * (P + 1)], k_phi[:, b, p * P:(p + 1) * P],
                                              v_one[:, b, p, :], start=True, stop=True)
                    mm.then_inc(kv_made, 1)
                pe.wait_ge(kv_ready, b + 1)
                pe.wait_ge(qphi_ready, PAIRS)
                if b >= 1:
                    pe.wait_ge(o_ready, b)
                for n, pairs in enumerate(GROUPS):
                    for j, p in enumerate(pairs):
                        mm = nc.tensor.matmul(bank[:, 3 + n, j * W:(j + 1) * W], q_phi[:, p, b * P:(b + 1) * P],
                                              kv[:, b % 2, p, :], start=True, stop=True)
                mm.then_inc(num_ready, 1)
                pe.wait_ge(o_ready, b + 1)
                if b >= 1:
                    pe.wait_ge(oT_ready, b)
                for p in range(PAIRS):
                    mm = nc.tensor.transpose(bank[:, 6 + p // 4, (p % 4) * P:(p % 4 + 1) * P], o_tok[:, p * P:(p + 1) * P], ident[:])
                mm.then_inc(o_turned, 1)
                pe.wait_ge(oT_ready, b + 1)
                for p in range(PAIRS):
                    mm = nc.tensor.matmul(bank[:, 6, 0:D], o_T[:, p, :], w_o[:, p, :], start=(p == 0), stop=(p == PAIRS - 1))
                mm.then_inc(wo_ready, 1)
                pe.wait_ge(h_ready, b + 1)
            pe.wait_ge(x1_ready, 1)
            for b in range(B):
                mm = nc.tensor.transpose(bank[:, 0, b * P:(b + 1) * P], x1[:, b, :], ident[:])
            mm.then_inc(x1_turned, 1)
            pe.wait_ge(x1T_ready, 1)
            for c in range(NF):
                nc.tensor.matmul(bank[:, 1 + c, :], w_1[:, c * P:(c + 1) * P], x1_T[:], start=True, stop=True).then_inc(f_proj, 1)
            pe.wait_ge(f_ready, NF)
            for b in range(B):
                for c in range(NF):
                    mm = nc.tensor.matmul(bank[:, 5, b * P:(b + 1) * P], f_T[:, c, b * P:(b + 1) * P], w_2[:, c, :],
                                          start=(c == 0), stop=(c == NF - 1))
            mm.then_inc(y_ready, 1)

        @block.scalar
        def _(act):
            act.wait_ge(src_turned, 1)
            nc.scalar.copy(src_T[:], bank[:, 0, :]).then_inc(srcT_ready, 1)
            act.wait_ge(w_in, 16 * N_IN)
            nc.scalar.mul(col_nq[:], col_q[:], -1.0).then_inc(kneg_ready, 1)

            def key_exp(b):
                act.wait_ge(klin_ready, b + 1)
                if b >= 2:
                    act.wait_ge(kphi_ready, b - 1)
                nc.scalar.activation(k_neg[:, b % 2, :], k_lin[:, b % 2, :], ACT.Relu, scale=-1.0).then_inc(kneg_ready, 1)
                act.wait_ge(kneg_ready, b + 2)
                nc.scalar.activation(k_exp[:, b % 2, :], k_neg[:, b % 2, :], ACT.Exp, scale=-1.0).then_inc(kexp_ready, 1)

            for b in range(B):
                key_exp(b)
            for p in range(PAIRS):
                act.wait_ge(q_proj, p + 1)
                if p >= 2:
                    act.wait_ge(qphi_ready, p - 1)
                nc.scalar.activation(q_neg[:, p % 2, :], bank[:, p, :], ACT.Relu, bias=col_nq[:, p:p + 1], scale=-1.0).then_inc(kneg_ready, 1)
                act.wait_ge(kneg_ready, 1 + B + p + 1)
                nc.scalar.activation(q_exp[:, p % 2, :], q_neg[:, p % 2, :], ACT.Exp, scale=-1.0).then_inc(qexp_ready, 1)
            for b in range(B):
                act.wait_ge(o_turned, b + 1)
                nc.scalar.copy(o_T[:].rearrange("p c q -> p (c q)"), bank[:, 6:8, :].rearrange("p a n -> p (a n)")).then_inc(oT_ready, 1)
            act.wait_ge(x1_turned, 1)
            nc.scalar.copy(x1_T[:], bank[:, 0, :]).then_inc(x1T_ready, 1)
            for c in range(NF):
                act.wait_ge(f_proj, c + 1)
                nc.scalar.activation(f_T[:, c, :], bank[:, 1 + c, :], ACT.Gelu, bias=col_1[:, c:c + 1]).then_inc(f_ready, 1)

        @block.vector
        def _(dve):
            own = Chain(dve, dve_own)
            last = norm.vector(dve, own, x_res, src, 1)
            last.then_inc(src_ready, 1)
            dve.wait_ge(src_ready, 1)
            dve.wait_ge(w_in, 16 * N_IN)
            dve.wait_ge(ones_ready, 1)
            for b in range(B + 1):
                if b < B:
                    dve.wait_ge(kv_proj, 4 * b + 2)
                    if b >= 2:
                        dve.wait_ge(kphi_ready, b - 1)
                    kb = bank[:, 4 * (b % 2):4 * (b % 2) + 2, :].rearrange("p a n -> p (a n)")
                    nc.vector.tensor_tensor(k_lin[:, b % 2, :], kb, row_k[:], ALU.add).then_inc(klin_ready, 1)
                    dve.wait_ge(kv_proj, 4 * b + 4)
                    vb = bank[:, 4 * (b % 2) + 2:4 * (b % 2) + 4, :].rearrange("p a (c n) -> p (a c) n", n=P)
                    nc.vector.tensor_tensor(v_one[:, b, :, 0:P], vb, row_v[:].rearrange("p (c n) -> p c n", n=P), ALU.add).then_inc(v_ready, 1)
                if b >= 1:
                    dve.wait_ge(kexp_ready, b)
                    nc.vector.scalar_tensor_tensor(out=k_phi[:, b - 1, :], in0=k_lin[:, (b - 1) % 2, :], scalar=0.0,
                                                   in1=k_exp[:, (b - 1) % 2, :], op0=ALU.max, op1=ALU.add).then_inc(kphi_ready, 1)
            for p in range(PAIRS):
                dve.wait_ge(q_proj, p + 1)
                dve.wait_ge(qexp_ready, p + 1)
                if p >= 2:
                    dve.wait_ge(qphi_ready, p - 1)
                nc.vector.tensor_scalar(q_pos[:, p % 2, :], bank[:, p, :], col_q[:, p:p + 1], 0.0, ALU.add, ALU.max).then_inc(qpos_ready, 1)
            for b in range(B):
                for n, pairs in enumerate(GROUPS):
                    dve.wait_ge(kv_made, 3 * b + n + 1)
                    m = len(pairs)
                    made = bank[:, n, 0:m * (P + 1)].rearrange("p (c n) -> p c n", n=P + 1)
                    for e in range(2):
                        half = slice(e * DH, (e + 1) * DH)
                        nc.vector.tensor_copy(kv[half, b % 2, pairs[0]:pairs[0] + m, half], made[half, :, half])
                        last = nc.vector.tensor_copy(kv[half, b % 2, pairs[0]:pairs[0] + m, P + e:P + e + 1], made[half, :, P:P + 1])
                last.then_inc(kv_ready, 1)
                dve.wait_ge(num_ready, b + 1)
                for n, pairs in enumerate(GROUPS):
                    m = len(pairs)
                    num = bank[:, 3 + n, 0:m * W].rearrange("p (c n) -> p c n", n=W)
                    last = nc.vector.tensor_scalar(den[:, 2 * pairs[0]:2 * (pairs[0] + m)].rearrange("p (c e) -> p c e", e=2),
                                                   num[:, :, P:P + 2], 1e-6, None, ALU.add)
                own.link(last)
                own.link(nc.vector.reciprocal(den[:], den[:]))
                for n, pairs in enumerate(GROUPS):
                    for e in range(2):
                        m = len(pairs)
                        num = bank[:, 3 + n, 0:m * W].rearrange("p (c n) -> p c n", n=W)[:, :, e * DH:(e + 1) * DH]
                        dst = o_tok[:].rearrange("p (c e d) -> p c e d", e=2, d=DH)[:, pairs[0]:pairs[0] + m, e, :]
                        by = den[:].rearrange("p (c e) -> p c e", e=2)[:, pairs[0]:pairs[0] + m, e:e + 1].to_broadcast([P, m, DH])
                        last = nc.vector.tensor_tensor(dst, num, by, ALU.mult)
                last.then_inc(o_ready, 1)
                dve.wait_ge(wo_ready, b + 1)
                nc.vector.tensor_tensor(h[:, b, :], bank[:, 6, 0:D], src[:, b, :], ALU.add).then_inc(h_ready, 1)
            dve.wait_ge(h_ready, B)

            def spread(j):
                return rows[:, j:j + 1, :].to_broadcast([P, B, D])

            own.link(nc.vector.tensor_tensor(h[:], h[:], spread(0), ALU.add))
            own.link(norm.vector(dve, own, h, x1, 2))
            own.link(nc.vector.tensor_tensor(x1[:], x1[:], spread(1), ALU.mult))
            nc.vector.tensor_tensor(x1[:], x1[:], spread(2), ALU.add).then_inc(x1_ready, 1)
            dve.wait_ge(x1_ready, 1)
            own.link(nc.vector.tensor_tensor(h[:], x1[:], spread(3), ALU.add))
            dve.wait_ge(y_ready, 1)
            own.link(nc.vector.tensor_tensor(h[:], h[:], bank[:, 5, :].rearrange("p (b d) -> p b d", b=B), ALU.add))
            own.link(norm.vector(dve, own, h, x1, 3))
            own.link(nc.vector.tensor_tensor(x1[:], x1[:], spread(4), ALU.mult))
            own.link(nc.vector.tensor_tensor(x1[:], x1[:], spread(5), ALU.add))
            own.link(nc.vector.tensor_tensor(x_res[:], x_res[:], x1[:], ALU.add))


def local_transformer(nc, io, g):
    LAYERS = 6
    TURNS = LAYERS // 2
    FF = int(D * 4 * 2 / 3)
    FT = (FF + P - 1) // P
    SIZE = [min(P, FF - c * P) for c in range(FT)]
    HALF = D // 2
    NU = 2 * B
    N_IN = 8
    with ExitStack() as ctx:
        s = Stage(nc, ctx, "lt")
        w_qkv = s.sb("w_qkv", [P, 2, 3 * INNER])
        w_o = s.sb("w_o", [P, 2, PAIRS, D])
        w_1, w_2 = s.sb("w_1", [P, 2, 2 * FF]), s.sb("w_2", [P, 2, FT, D])
        cols = s.sb("cols", [P, 2, 8])
        gains = s.sb("gains", [P, 2, 4 * DH])
        row_2 = s.sb("row_2", [P, 2, D])
        tables, band, shift = s.sb("tables", [P, 4 * DH]), s.sb("band", [P, P]), s.sb("shift", [P, P])
        rot = s.sb("rot", [P, 4, DH])
        norm = Norm(s, B, g["mhalf"])
        xc, xs = s.sb("xc", [P, B, D]), s.sb("xs", [P, B, D])
        xs_T = s.sb("xs_T", [P, B, P])
        xn_T = s.sb("xn_T", [P, B * P])
        sq, t1, t2, qk = (s.sb(n, [P, 2, INNER]) for n in ("sq", "t1", "t2", "qk"))
        ss, root, quot, rn = (s.sb(n, [P, NU, H]) for n in ("ss", "root", "quot", "rn"))
        qk_T = s.sb("qk_T", [P, NU, PAIRS, P])
        v = s.sb("v", [P, B, INNER])
        prob = s.sb("prob", [P, 2, H, P])
        mx, scale, bias = (s.sb(n, [P, 2, H]) for n in ("mx", "scale", "bias"))
        psumr = s.sb("psumr", [P, H])
        p_T = s.sb("p_T", [P, H, P])
        rsum, o_tok, o_T = s.sb("rsum", [P, H]), s.sb("o_tok", [P, INNER]), s.sb("o_T", [P, PAIRS, P])
        gate, f_T = s.sb("gate", [P, FT, B * P]), s.sb("f_T", [P, FT, B * P])
        bank = s.ps("bank", [P, 8, BANK])
        w_in = [s.sem("w_in0"), s.sem("w_in1")]
        (const_in, passed, dve_own, pool_own, x_ready, xT_turned, xsT_ready, proj_ready, sq_ready, ss_ready, rn_ready,
         rot_ready, roped, q_ready, sum_ready, k_ready, v_ready, qk_turned, qkT_ready) = (s.sem(n) for n in (
            "const_in", "passed", "dve_own", "pool_own", "x_ready", "xT_turned", "xsT_ready", "proj_ready", "sq_ready",
            "ss_ready", "rn_ready", "rot_ready", "roped", "q_ready", "sum_ready", "k_ready", "v_ready", "qk_turned", "qkT_ready"))
        root_ready = s.sem("root_ready")
        (scores_read, sim_ready, max_ready, exp_ready, p_turned, pT_ready, pv_ready, o_ready, o_turned, oT_ready, wo_ready, x1_ready,
         shifted, xn_ready, xn_turned, xnT_ready, f_proj, gate_ready, f_ready, y_ready) = (s.sem(n) for n in (
            "scores_read", "sim_ready", "max_ready", "exp_ready", "p_turned", "pT_ready", "pv_ready", "o_ready", "o_turned", "oT_ready",
            "wo_ready", "x1_ready", "shifted", "xn_ready", "xn_turned", "xnT_ready", "f_proj", "gate_ready", "f_ready", "y_ready"))
        x_res, ident = g["x_res"], g["ident"]
        block = ctx.enter_context(nc.Block())

        def place(h):
            return (h % 2) * PAIRS + h // 2

        def at(turn, u, per, k):
            return turn * (2 * per) + (u * per + k)

        @block.sync
        def _(sp):
            sp.dma_start(tables[:], io["rotary"]).then_inc(const_in, 16)
            sp.dma_start(band[:], io["band"]).then_inc(const_in, 16)
            sp.dma_start(shift[:], io["shift"]).then_inc(const_in, 16)

            def load(layer, u):
                def of(name):
                    return io["L0_ffn_" + name][layer].rearrange("a k n -> (a k) n")
                sp.dma_start(w_qkv[:, u, :], of("Wqkv")).then_inc(w_in[u], 16)
                sp.dma_start(gains[:, u, :], io["L0_ffn_gains"][layer].partition_broadcast(P).rearrange("p a n -> p (a n)")).then_inc(w_in[u], 16)
                sp.dma_start(cols[:, u, :], of("cols")).then_inc(w_in[u], 16)
                sp.dma_start(w_o[:, u, :, :], of("Wo").rearrange("(c p) n -> p c n", p=P)).then_inc(w_in[u], 16)
                sp.dma_start(w_1[:, u, :], of("W1")).then_inc(w_in[u], 16)
                sp.dma_start(w_2[:, u, 0:FT - 1, :], of("W2")[0:(FT - 1) * P, :].rearrange("(c p) n -> p c n", p=P)).then_inc(w_in[u], 16)
                sp.dma_start(w_2[0:SIZE[-1], u, FT - 1, :], of("W2")[(FT - 1) * P:FF, :]).then_inc(w_in[u], 16)
                sp.dma_start(row_2[:, u, :], io["L0_ffn_b2"][layer].partition_broadcast(P).rearrange("p a n -> p (a n)")).then_inc(w_in[u], 16)

            for u in range(2):
                load(slice(u, u + 1), u)
            with sp.Fori(0, TURNS - 1) as t:
                for u in range(2):
                    sp.wait_ge(x_ready, at(t, u, 1, 2))
                    step(sp, passed)
                    load(bass.ds(t * 2 + (2 + u), 1), u)

        @block.gpsimd
        def _(pool):
            own = Chain(pool, pool_own)
            own.link(nc.gpsimd.memset(xs_T[:], 0.0))
            norm.pool(pool, 1)
            pool.wait_ge(const_in, 48)
            with pool.Fori(0, TURNS) as t:
                for u in range(2):
                    pool.wait_ge(w_in[u], t * (16 * N_IN) + 16 * N_IN)
                    pool.wait_ge(x_ready, at(t, u, 1, 1))
                    nc.gpsimd.tensor_tensor(rot[:].rearrange("p a e -> p (a e)"), tables[:], gains[:, u, :], ALU.mult).then_inc(rot_ready, 1)
                    for m in range(NU):
                        pool.wait_ge(roped, at(t, u, NU, m + 1))
                        if m >= 2:
                            pool.wait_ge(qk_turned, at(t, u, NU, m - 1))
                        nc.gpsimd.tensor_tensor(qk[:, m % 2, :], t1[:, m % 2, :], t2[:, m % 2, :], ALU.add).then_inc(sum_ready, 1)
                        if m % 2 == 1:
                            x = qk[:, m % 2, :].rearrange("p (h e) -> p h e", e=DH)
                            pool.wait_ge(sum_ready, at(t, u, NU, m + 1))
                            pool.wait_ge(rn_ready, at(t, u, NU, m + 1))
                            nc.gpsimd.tensor_tensor(x, x, rn[:, m, :].unsqueeze(2).to_broadcast([P, H, DH]), ALU.mult).then_inc(k_ready, 1)
                    norm.pool(pool, at(t, u, 1, 2))

        @block.tensor
        def _(pe):
            pe.wait_ge(const_in, 48)

            def layer(t, u):
                def wait(sem, per, k):
                    pe.wait_ge(sem, at(t, u, per, k))

                wait(x_ready, 1, 1)
                for b in range(B):
                    mm = nc.tensor.transpose(bank[:, 0, b * P:(b + 1) * P], xc[:, b, :], ident[:])
                mm.then_inc(xT_turned, 1)
                wait(xsT_ready, 2, 2)
                pe.wait_ge(w_in[u], t * (16 * N_IN) + 16 * N_IN)

                def turn(m):
                    if m % 2 == 0:
                        wait(sum_ready, NU, m + 1)
                    else:
                        wait(k_ready, B, m // 2 + 1)
                    if m >= 1:
                        wait(qkT_ready, NU, m)
                    for p in range(PAIRS):
                        mm = nc.tensor.transpose(bank[:, 6 + p // 4, (p % 4) * P:(p % 4 + 1) * P],
                                                 qk[:, m % 2, p * P:(p + 1) * P], ident[:])
                    mm.then_inc(qk_turned, 1)

                def project(b, kind):
                    if b >= 1 and kind < 2:
                        wait(roped, NU, 2 * (b - 1) + kind + 1)
                    elif b >= 1:
                        wait(v_ready, B, b)
                    for c in range(2):
                        mm = nc.tensor.matmul(bank[:, 2 * kind + c, :], xs_T[:, b, :],
                                              w_qkv[:, u, kind * INNER + c * BANK:kind * INNER + (c + 1) * BANK],
                                              start=True, stop=True)
                    mm.then_inc(proj_ready, 1)

                for b in range(B):
                    project(b, 0)
                    if b >= 2:
                        turn(2 * b - 3)
                    project(b, 1)
                    if b >= 1:
                        turn(2 * b - 2)
                    project(b, 2)
                turn(NU - 3)
                turn(NU - 2)

                def score(b):
                    wait(qkT_ready, NU, 2 * b + 2)
                    if b == 0:
                        wait(roped, NU, NU)
                    else:
                        wait(scores_read, B, b)
                    for h in range(H):
                        half = slice((h % 2) * DH, (h % 2 + 1) * DH)
                        i = place(h)
                        mm = nc.tensor.matmul(bank[:, i // 4, (i % 4) * P:(i % 4 + 1) * P], qk_T[half, 2 * b, h // 2, :],
                                              qk_T[half, 2 * b + 1, h // 2, :], start=True, stop=True)
                    mm.then_inc(sim_ready, 1)

                def turn_prob(b):
                    for n in range(4):
                        wait(exp_ready, 4 * B, 4 * b + n + 1)
                        if n >= 2:
                            wait(pT_ready, 4 * B, 4 * b + n - 1)
                        elif b >= 1:
                            wait(oT_ready, B, b)
                        else:
                            wait(v_ready, B, B)
                        for j in range(4):
                            mm = nc.tensor.transpose(bank[:, 4 + n % 2, j * P:(j + 1) * P], prob[:, b % 2, 4 * n + j, :], ident[:])
                        mm.then_inc(p_turned, 1)

                def gather(b):
                    if b >= 1:
                        wait(x1_ready, B, b)
                    else:
                        wait(qkT_ready, NU, NU)
                    for n in range(4):
                        wait(pT_ready, 4 * B, 4 * b + n + 1)
                        for h in (h for h in range(H) if place(h) // 4 == n):
                            mm = nc.tensor.matmul(bank[:, 6 + h // 8, (h % 8) * DH:(h % 8 + 1) * DH], p_T[:, place(h), :],
                                                  v[:, b, h * DH:(h + 1) * DH], start=True, stop=True)
                    mm.then_inc(pv_ready, 1)

                def project_out(b):
                    wait(o_ready, B, b + 1)
                    for p in range(PAIRS):
                        mm = nc.tensor.transpose(bank[:, 4 + p // 4, (p % 4) * P:(p % 4 + 1) * P], o_tok[:, p * P:(p + 1) * P], ident[:])
                    mm.then_inc(o_turned, 1)
                    wait(oT_ready, B, b + 1)
                    for p in range(PAIRS):
                        mm = nc.tensor.matmul(bank[:, 6, 0:D], o_T[:, p, :], w_o[:, u, p, :], start=(p == 0), stop=(p == PAIRS - 1))
                    mm.then_inc(wo_ready, 1)

                score(0)
                turn(NU - 1)
                score(1)
                for b in range(B):
                    turn_prob(b)
                    gather(b)
                    if b + 2 < B:
                        score(b + 2)
                    project_out(b)
                wait(x1_ready, B, B)
                nc.tensor.matmul(bank[:, 7, 0:B * HALF], shift[:], xc[:, :, HALF:D], start=True, stop=True).then_inc(shifted, 1)
                wait(xn_ready, 1, 1)
                for b in range(B):
                    mm = nc.tensor.transpose(bank[:, 6, b * P:(b + 1) * P], xs[:, b, :], ident[:])
                mm.then_inc(xn_turned, 1)
                wait(xnT_ready, 1, 1)
                for c in range(FT):
                    for side in range(2):
                        first = (1 - side) * FF + c * P
                        nc.tensor.matmul(bank[0:SIZE[c], 3 * side + c, :], w_1[:, u, first:first + SIZE[c]],
                                         xn_T[:], start=True, stop=True).then_inc(f_proj, 1)
                wait(f_ready, FT, FT)
                for b in range(B):
                    for c in range(FT):
                        mm = nc.tensor.matmul(bank[:, 7, b * P:(b + 1) * P], f_T[0:SIZE[c], c, b * P:(b + 1) * P],
                                              w_2[0:SIZE[c], u, c, :], start=(c == 0), stop=(c == FT - 1))
                mm.then_inc(y_ready, 1)

            with pe.Fori(0, TURNS) as t:
                for u in range(2):
                    layer(t, u)

        @block.scalar
        def _(act):
            def layer(t, u):
                def wait(sem, per, k):
                    act.wait_ge(sem, at(t, u, per, k))

                wait(xT_turned, 1, 1)
                src = bank[:, 0, :].rearrange("p (b n) -> p b n", b=B)
                nc.scalar.copy(xs_T[0:HALF, :, :], src[0:HALF]).then_inc(xsT_ready, 1)
                nc.scalar.copy(xs_T[HALF:P, :, 1:P], src[HALF:P, :, 0:P - 1]).then_inc(xsT_ready, 1)

                def square(m):
                    b, kind = m // 2, m % 2
                    wait(proj_ready, 3 * B, 3 * b + kind + 1)
                    if m >= 2:
                        wait(ss_ready, NU, m - 1)
                    nc.scalar.activation(sq[:, m % 2, :], bank[:, 2 * kind:2 * kind + 2, :].rearrange("p a n -> p (a n)"),
                                         ACT.Square, scale=0.5).then_inc(sq_ready, 1)

                def square_root(m):
                    wait(ss_ready, NU, m + 1)
                    nc.scalar.activation(root[:, m, :], ss[:, m, :], ACT.Sqrt).then_inc(root_ready, 1)

                def keep_turned(m):
                    wait(qk_turned, NU, m + 1)
                    nc.scalar.copy(qk_T[:, m, :, :].rearrange("p c n -> p (c n)"),
                                   bank[:, 6:8, :].rearrange("p a n -> p (a n)")).then_inc(qkT_ready, 1)

                for b in range(B):
                    square(2 * b)
                    if b >= 2:
                        keep_turned(2 * b - 3)
                    square_root(2 * b)
                    square(2 * b + 1)
                    if b >= 1:
                        keep_turned(2 * b - 2)
                    wait(proj_ready, 3 * B, 3 * b + 3)
                    nc.scalar.copy(v[:, b, :], bank[:, 4:6, :].rearrange("p a n -> p (a n)")).then_inc(v_ready, 1)
                    square_root(2 * b + 1)
                for m in range(NU - 3, NU):
                    keep_turned(m)

                def exponent(b):
                    wait(max_ready, B, b + 1)
                    for h in range(H):
                        last = nc.scalar.activation(prob[:, b % 2, h, :], prob[:, b % 2, h, :], ACT.Exp, bias=bias[:, b % 2, h:h + 1],
                                                    scale=scale[:, b % 2, h:h + 1])
                        if h % 4 == 3:
                            last.then_inc(exp_ready, 1)

                def keep_prob(b):
                    for n in range(4):
                        wait(p_turned, 4 * B, 4 * b + n + 1)
                        if b >= 1 and n == 0:
                            wait(pv_ready, B, b)
                        nc.scalar.copy(p_T[:, 4 * n:4 * n + 4, :].rearrange("p h q -> p (h q)"), bank[:, 4 + n % 2, :]).then_inc(pT_ready, 1)

                exponent(0)
                for b in range(B):
                    keep_prob(b)
                    if b + 1 < B:
                        exponent(b + 1)
                    wait(o_turned, B, b + 1)
                    nc.scalar.copy(o_T[:].rearrange("p c q -> p (c q)"), bank[:, 4:6, :].rearrange("p a n -> p (a n)")).then_inc(oT_ready, 1)
                wait(xn_turned, 1, 1)
                nc.scalar.activation(xn_T[:], bank[:, 6, :], ACT.Identity, bias=cols[:, u, 1:2], scale=cols[:, u, 0:1]).then_inc(xnT_ready, 1)
                for c in range(FT):
                    wait(f_proj, 2 * FT, 2 * c + 1)
                    n = SIZE[c]
                    nc.scalar.activation(gate[0:n, c, :], bank[0:n, c, :], ACT.Gelu, bias=cols[0:n, u, 5 + c:6 + c]).then_inc(gate_ready, 1)

            with act.Fori(0, TURNS) as t:
                for u in range(2):
                    layer(t, u)

        @block.vector
        def _(dve):
            own = Chain(dve, dve_own)
            norm.vector(dve, own, x_res, xc, 1).then_inc(x_ready, 1)

            def layer(t, u):
                def wait(sem, per, k):
                    dve.wait_ge(sem, at(t, u, per, k))

                wait(rot_ready, 1, 1)

                def rope(m):
                    b, kind = m // 2, m % 2
                    src = bank[:, 2 * kind:2 * kind + 2, :].rearrange("p a (h e) -> p (a h) e", e=DH)
                    wait(sq_ready, NU, m + 1)
                    own.link(nc.vector.tensor_reduce(ss[:, m, :], sq[:, m % 2, :].rearrange("p (h e) -> p h e", e=DH), AX.X, ALU.add))
                    nc.vector.tensor_scalar(ss[:, m, :], ss[:, m, :], 0.25e-24, None, ALU.max).then_inc(ss_ready, 1)
                    if m >= 2:
                        wait(sum_ready, NU, m - 1)
                    o1, o2 = (x[:, m % 2, :].rearrange("p (h e) -> p h e", e=DH) for x in (t1, t2))
                    by1 = rot[:, 2 * kind:2 * kind + 1, :].to_broadcast([P, H, DH])
                    nc.vector.tensor_tensor(o1, src, by1, ALU.mult)
                    r = DH // 2
                    nc.vector.tensor_tensor(o2[:, :, 0:r], src[:, :, r:DH], rot[:, 2 * kind + 1:2 * kind + 2, 0:r].to_broadcast([P, H, r]), ALU.mult)
                    nc.vector.tensor_tensor(o2[:, :, r:DH], src[:, :, 0:r], rot[:, 2 * kind + 1:2 * kind + 2, r:DH].to_broadcast([P, H, r]),
                                            ALU.mult).then_inc(roped, 1)

                def refine(m):
                    wait(root_ready, NU, m + 1)
                    own.link(nc.vector.reciprocal(quot[:, m, :], root[:, m, :]))
                    own.link(nc.vector.tensor_tensor(quot[:, m, :], quot[:, m, :], ss[:, m, :], ALU.mult))
                    own.link(nc.vector.tensor_tensor(quot[:, m, :], quot[:, m, :], root[:, m, :], ALU.add))
                    nc.vector.reciprocal(rn[:, m, :], quot[:, m, :]).then_inc(rn_ready, 1)

                for m in range(NU):
                    rope(m)
                    refine(m)

                def mask(b):
                    wait(sim_ready, B, b + 1)
                    if b >= 2:
                        wait(p_turned, 4 * B, 4 * (b - 1))
                    for n in range(4):
                        last = nc.vector.tensor_tensor(prob[:, b % 2, 4 * n:4 * n + 4, :], bank[:, n, :].rearrange("p (h j) -> p h j", h=4),
                                                       band[:].unsqueeze(1).to_broadcast([P, 4, P]), ALU.add)
                    last.then_inc(scores_read, 1)

                def maximum(b):
                    k = b % 2
                    own.link(nc.vector.tensor_scalar(scale[:, k, :].rearrange("p (e c) -> p e c", e=2),
                                                     rn[:, 2 * b, :].rearrange("p (c e) -> p e c", e=2), 8.0, None, ALU.mult))
                    own.link(nc.vector.tensor_reduce(mx[:, k, :], prob[:, k, :, :], AX.X, ALU.max))
                    nc.vector.scalar_tensor_tensor(out=bias[:, k, :], in0=mx[:, k, :], scalar=-1.0, in1=scale[:, k, :],
                                                   op0=ALU.mult, op1=ALU.mult).then_inc(max_ready, 1)

                def divide(b):
                    wait(exp_ready, 4 * B, 4 * b + 4)
                    own.link(nc.vector.tensor_reduce(psumr[:], prob[:, b % 2, :, :], AX.X, ALU.add))
                    own.link(nc.vector.reciprocal(rsum[:], psumr[:]))
                    wait(pv_ready, B, b + 1)
                    src = bank[:, 6:8, :].rearrange("p a (c e d) -> p (a c) e d", e=2, d=DH)
                    nc.vector.tensor_tensor(o_tok[:].rearrange("p (c e d) -> p c e d", e=2, d=DH), src,
                                            rsum[:].rearrange("p (e c) -> p c e", e=2).unsqueeze(3).to_broadcast([P, PAIRS, 2, DH]), ALU.mult).then_inc(o_ready, 1)

                def residual(b):
                    wait(wo_ready, B, b + 1)
                    nc.vector.tensor_tensor(xc[:, b, :], xc[:, b, :], bank[:, 6, 0:D], ALU.add).then_inc(x1_ready, 1)

                for b in range(2):
                    mask(b)
                    maximum(b)
                for b in range(B):
                    divide(b)
                    if b + 2 < B:
                        mask(b + 2)
                    residual(b)
                    if b + 2 < B:
                        maximum(b + 2)
                wait(x1_ready, B, B)
                nc.vector.tensor_copy(xs[:, :, 0:HALF], xc[:, :, 0:HALF])
                wait(shifted, 1, 1)
                own.link(nc.vector.tensor_copy(xs[:, :, HALF:D], bank[:, 7, 0:B * HALF].rearrange("p (b n) -> p b n", b=B)))
                norm.vector(dve, own, xs, xs, at(t, u, 1, 2), passed).then_inc(xn_ready, 1)
                own.link(nc.vector.tensor_tensor(xc[:], xc[:], row_2[:, u:u + 1, :].to_broadcast([P, B, D]), ALU.add))
                for c in range(FT):
                    wait(f_proj, 2 * FT, 2 * c + 2)
                    wait(gate_ready, FT, c + 1)
                    n = SIZE[c]
                    nc.vector.scalar_tensor_tensor(out=f_T[0:n, c, :], in0=bank[0:n, 3 + c, :], scalar=cols[0:n, u, 2 + c:3 + c],
                                                   in1=gate[0:n, c, :], op0=ALU.add, op1=ALU.mult).then_inc(f_ready, 1)
                wait(y_ready, 1, 1)
                nc.vector.tensor_tensor(xc[:], xc[:], bank[:, 7, :].rearrange("p (b d) -> p b d", b=B), ALU.add).then_inc(x_ready, 1)

            with dve.Fori(0, TURNS) as t:
                per = 2 * (4 * NU + 2 * B + 2 * B + 1 + 2 + 1)
                own.enter(t, per)
                for u in range(2):
                    layer(t, u)
                own.leave(TURNS)
            dve.wait_ge(x_ready, LAYERS + 1)
            nc.vector.tensor_tensor(x_res[:], x_res[:], xc[:], ALU.add)


def two_way_attention(nc, io, g):
    CK = CTX // BANK
    LEFT = CT // 2 - 1
    SCALE = D ** -0.5
    with ExitStack() as ctx:
        s = Stage(nc, ctx, "ta")
        names = ("Wq_c", "Wk_s", "Wv_s", "Wq_s", "Wk_c", "Wv_c")
        w = {n: s.sb("w_" + n, [P, D]) for n in names}
        w_g = s.sb("w_g", [P, 2, D])
        cols = s.sb("cols", [P, 4])
        rows = s.sb("rows", [P, 3, D])
        norm = Norm(s, B, g["mhalf"])
        char, char_T, qc_T, kc_T = (s.sb(n, [P, B, D]) for n in ("char", "char_T", "qc_T", "kc_T"))
        vc = s.sb("vc", [P, B, D])
        ctx_raw, ctx_T, k_T = s.sb("ctx_raw", [P, 2, CT, D]), s.sb("ctx_T", [P, 2, CTX]), s.sb("k_T", [P, 2, CTX])
        qs_T = s.sb("qs_T", [P, 2, 2, P])
        prob, p_T = s.sb("prob", [P, CTX]), s.sb("p_T", [P, CT, P])
        prob2, p2_T = s.sb("prob2", [P, 2, P]), s.sb("p2_T", [P, 2, P])
        stat = s.sb("stat", [P, 16])
        c_T, both, both_T = s.sb("c_T", [P, P]), s.sb("both", [P, 2, D]), s.sb("both_T", [P, 2, P])
        u, diff = s.sb("u", [P, D]), s.sb("diff", [P, D])
        bank = s.ps("bank", [P, 8, BANK])
        (w_in, dve_own, char_ready, char_turned, charT_ready, cproj, cproj_kept, ctx_turned, ctxT_ready, k_proj, kT_ready,
         sc_ready, max_ready, exp_ready, s2_ready, max2_ready, exp2_ready, p2_turned, p2T_ready, o2_ready, s2c_ready,
         p_turned, pT_ready, c_ready, cT_ready, c2s_raw, c2s_ready, both_turned, bothT_ready, g_ready, u_ready, e_ready,
         x_ready) = (s.sem(n) for n in (
            "w_in", "dve_own", "char_ready", "char_turned", "charT_ready", "cproj", "cproj_kept", "ctx_turned", "ctxT_ready",
            "k_proj", "kT_ready", "sc_ready", "max_ready", "exp_ready", "s2_ready", "max2_ready", "exp2_ready", "p2_turned",
            "p2T_ready", "o2_ready", "s2c_ready", "p_turned", "pT_ready", "c_ready", "cT_ready", "c2s_raw", "c2s_ready",
            "both_turned", "bothT_ready", "g_ready", "u_ready", "e_ready", "x_ready"))
        ctx_in = [s.sem("ctx_in0"), s.sem("ctx_in1")]
        x_res, ident = g["x_res"], g["ident"]
        block = ctx.enter_context(nc.Block())
        N_IN = 6 + 1 + 4 + 3
        QS = CK

        @block.sync
        def _(sp):
            for n in names:
                sp.dma_start(w[n][:], io["L1_xattn_" + n]).then_inc(w_in, 16)
            sp.dma_start(w_g[:], io["L1_xattn_Wg"].rearrange("(c p) n -> p c n", p=P)).then_inc(w_in, 16)
            for j, n in enumerate(("bq_c", "bk_s", "bq_s", "bk_c")):
                sp.dma_start(cols[:, j:j + 1], columns(io["L1_xattn_" + n], 1)).then_inc(w_in, 16)
            for j, n in enumerate(("bv_s", "bv_c", "bg")):
                sp.dma_start(rows[:, j, :], row(io["L1_xattn_" + n])).then_inc(w_in, 16)
            for b in range(B):
                if b >= 2:
                    sp.wait_ge(c_ready, b - 1)
                sp.dma_start(ctx_raw[:, b % 2, :, :], io["ctx_1024"][b].rearrange("(p t) d -> p t d", p=P)).then_inc(ctx_in[b % 2], 16)

        @block.gpsimd
        def _(pool):
            norm.pool(pool, 1)

        @block.tensor
        def _(pe):
            def prepare(b):
                k = b % 2
                pe.wait_ge(ctx_in[k], 16 * (b // 2 + 1))
                for c in range(CK):
                    if 4 * b + c >= 2:
                        pe.wait_ge(ctxT_ready, CK * b + c - 1)
                    for j in range(4):
                        mm = nc.tensor.transpose(bank[:, c % 2, j * P:(j + 1) * P], ctx_raw[:, k, 4 * c + j, :], ident[:])
                    mm.then_inc(ctx_turned, 1)
                for c in range(CK + 1):
                    n = (CK + 1) * b + c
                    if n >= 2:
                        pe.wait_ge(kT_ready, n - 1)
                    if c < CK:
                        pe.wait_ge(ctxT_ready, CK * b + c + 1)
                        nc.tensor.matmul(bank[:, 2 + c % 2, :], w["Wk_s"][:], ctx_T[:, k, c * BANK:(c + 1) * BANK],
                                         start=True, stop=True).then_inc(k_proj, 1)
                    else:
                        nc.tensor.matmul(bank[:, 2 + c % 2, 0:2 * P], w["Wq_s"][:], ctx_T[:, k, LEFT * P:(LEFT + 2) * P],
                                         start=True, stop=True).then_inc(k_proj, 1)

            def score(b):
                pe.wait_ge(kT_ready, (CK + 1) * (b + 1))
                if b == 0:
                    pe.wait_ge(cproj_kept, 3)
                else:
                    pe.wait_ge(x_ready, b)
                for c in range(CK):
                    mm = nc.tensor.matmul(bank[:, 4 + c, :], qc_T[:, b, :], k_T[:, b % 2, c * BANK:(c + 1) * BANK], start=True, stop=True)
                mm.then_inc(sc_ready, 1)

            pe.wait_ge(char_ready, 1)
            for b in range(B):
                mm = nc.tensor.transpose(bank[:, 0, b * P:(b + 1) * P], char[:, b, :], ident[:])
            mm.then_inc(char_turned, 1)
            pe.wait_ge(charT_ready, 1)
            pe.wait_ge(w_in, 16 * N_IN)
            rhs = char_T[:].rearrange("p b n -> p (b n)")
            nc.tensor.matmul(bank[:, 4, :], w["Wq_c"][:], rhs, start=True, stop=True).then_inc(cproj, 1)
            nc.tensor.matmul(bank[:, 5, :], w["Wk_c"][:], rhs, start=True, stop=True).then_inc(cproj, 1)
            for b in range(B):
                mm = nc.tensor.matmul(bank[:, 6, b * P:(b + 1) * P], char_T[:, b, :], w["Wv_c"][:], start=True, stop=True)
            mm.then_inc(cproj, 1)
            prepare(0)
            for b in range(B):
                score(b)
                if b + 1 < B:
                    prepare(b + 1)
                pe.wait_ge(exp_ready, b + 1)
                for e in range(2):
                    mm = nc.tensor.matmul(bank[:, 4, e * P:(e + 1) * P], qs_T[:, b % 2, e, :], kc_T[:, b, :], start=True, stop=True)
                mm.then_inc(s2_ready, 1)
                for c in range(CK):
                    if c >= 2:
                        pe.wait_ge(pT_ready, CK * b + c - 1)
                    else:
                        pe.wait_ge(ctxT_ready, CK * min(b + 2, B))
                    for j in range(4):
                        mm = nc.tensor.transpose(bank[:, c % 2, j * P:(j + 1) * P], prob[:, (4 * c + j) * P:(4 * c + j + 1) * P], ident[:])
                    mm.then_inc(p_turned, 1)
                pe.wait_ge(exp2_ready, b + 1)
                for e in range(2):
                    mm = nc.tensor.transpose(bank[:, 5, e * P:(e + 1) * P], prob2[:, e, :], ident[:])
                mm.then_inc(p2_turned, 1)
                pe.wait_ge(kT_ready, (CK + 1) * min(b + 2, B))
                for t in range(CT):
                    pe.wait_ge(pT_ready, CK * b + t // 4 + 1)
                    mm = nc.tensor.matmul(bank[:, 2, 0:P], ctx_raw[:, b % 2, t, :], p_T[:, t, :], start=(t == 0), stop=(t == CT - 1))
                mm.then_inc(c_ready, 1)
                pe.wait_ge(p2T_ready, b + 1)
                for e in range(2):
                    mm = nc.tensor.matmul(bank[:, 6, e * P:(e + 1) * P], p2_T[:, e, :], vc[:, b, :], start=True, stop=True)
                mm.then_inc(o2_ready, 1)
                pe.wait_ge(cT_ready, b + 1)
                nc.tensor.matmul(bank[:, 7, 0:D], c_T[:], w["Wv_s"][:], start=True, stop=True).then_inc(c2s_raw, 1)
                pe.wait_ge(c2s_ready, b + 1)
                for e in range(2):
                    mm = nc.tensor.transpose(bank[:, 3, e * P:(e + 1) * P], both[:, e, :], ident[:])
                mm.then_inc(both_turned, 1)
                pe.wait_ge(bothT_ready, b + 1)
                for e in range(2):
                    mm = nc.tensor.matmul(bank[:, 5, 0:D], both_T[:, e, :], w_g[:, e, :], start=(e == 0), stop=(e == 1))
                mm.then_inc(g_ready, 1)

        @block.scalar
        def _(act):
            def prepare(b):
                k = b % 2
                for c in range(CK):
                    act.wait_ge(ctx_turned, CK * b + c + 1)
                    nc.scalar.copy(ctx_T[:, k, c * BANK:(c + 1) * BANK], bank[:, c % 2, :]).then_inc(ctxT_ready, 1)
                for c in range(CK + 1):
                    act.wait_ge(k_proj, (CK + 1) * b + c + 1)
                    if c < CK:
                        nc.scalar.activation(k_T[:, k, c * BANK:(c + 1) * BANK], bank[:, 2 + c % 2, :], ACT.Identity,
                                             bias=cols[:, 1:2]).then_inc(kT_ready, 1)
                    else:
                        nc.scalar.activation(qs_T[:, k, :, :].rearrange("p e n -> p (e n)"), bank[:, 2 + c % 2, 0:2 * P], ACT.Identity,
                                             bias=cols[:, 2:3]).then_inc(kT_ready, 1)

            act.wait_ge(char_turned, 1)
            nc.scalar.copy(char_T[:].rearrange("p b n -> p (b n)"), bank[:, 0, :]).then_inc(charT_ready, 1)
            act.wait_ge(w_in, 16 * N_IN)
            act.wait_ge(cproj, 1)
            nc.scalar.activation(qc_T[:].rearrange("p b n -> p (b n)"), bank[:, 4, :], ACT.Identity, bias=cols[:, 0:1]).then_inc(cproj_kept, 1)
            act.wait_ge(cproj, 2)
            nc.scalar.activation(kc_T[:].rearrange("p b n -> p (b n)"), bank[:, 5, :], ACT.Identity, bias=cols[:, 3:4]).then_inc(cproj_kept, 1)
            prepare(0)
            for b in range(B):
                act.wait_ge(max_ready, b + 1)
                nc.scalar.activation(prob[:], bank[:, 4:8, :].rearrange("p a n -> p (a n)"), ACT.Exp, bias=stat[:, 1:2], scale=SCALE,
                                     accum_out=stat[:, 2:3]).then_inc(exp_ready, 1)
                if b + 1 < B:
                    prepare(b + 1)
                act.wait_ge(max2_ready, b + 1)
                for e in range(2):
                    last = nc.scalar.activation(prob2[:, e, :], bank[:, 4, e * P:(e + 1) * P], ACT.Exp, bias=stat[:, 6 + e:7 + e],
                                                scale=SCALE, accum_out=stat[:, 8 + e:9 + e])
                last.then_inc(exp2_ready, 1)
                for c in range(CK):
                    act.wait_ge(p_turned, CK * b + c + 1)
                    nc.scalar.copy(p_T[:, 4 * c:4 * c + 4, :].rearrange("p t q -> p (t q)"), bank[:, c % 2, :]).then_inc(pT_ready, 1)
                act.wait_ge(p2_turned, b + 1)
                nc.scalar.copy(p2_T[:].rearrange("p e q -> p (e q)"), bank[:, 5, 0:2 * P]).then_inc(p2T_ready, 1)
                act.wait_ge(c_ready, b + 1)
                nc.scalar.copy(c_T[:], bank[:, 2, 0:P]).then_inc(cT_ready, 1)
                act.wait_ge(both_turned, b + 1)
                nc.scalar.copy(both_T[:].rearrange("p e q -> p (e q)"), bank[:, 3, 0:2 * P]).then_inc(bothT_ready, 1)
                act.wait_ge(u_ready, b + 1)
                nc.scalar.activation(u[:], u[:], ACT.Exp, scale=-1.0).then_inc(e_ready, 1)

        @block.vector
        def _(dve):
            own = Chain(dve, dve_own)
            norm.vector(dve, own, x_res, char, 1).then_inc(char_ready, 1)
            dve.wait_ge(w_in, 16 * N_IN)
            dve.wait_ge(cproj, 3)
            nc.vector.tensor_tensor(vc[:], bank[:, 6, :].rearrange("p (b d) -> p b d", b=B), rows[:, 1:2, :].to_broadcast([P, B, D]),
                                    ALU.add).then_inc(cproj_kept, 1)
            for b in range(B):
                dve.wait_ge(sc_ready, b + 1)
                own.link(nc.vector.tensor_reduce(stat[:, 0:1], bank[:, 4:8, :].rearrange("p a n -> p (a n)"), AX.X, ALU.max))
                nc.vector.tensor_scalar(stat[:, 1:2], stat[:, 0:1], -SCALE, None, ALU.mult).then_inc(max_ready, 1)
                dve.wait_ge(s2_ready, b + 1)
                own.link(nc.vector.tensor_reduce(stat[:, 4:6], bank[:, 4, 0:2 * P].rearrange("p (e n) -> p e n", e=2), AX.X, ALU.max))
                nc.vector.tensor_scalar(stat[:, 6:8], stat[:, 4:6], -SCALE, None, ALU.mult).then_inc(max2_ready, 1)
                dve.wait_ge(exp2_ready, b + 1)
                own.link(nc.vector.tensor_scalar(stat[:, 10:12], stat[:, 8:10], 2.0, None, ALU.mult))
                nc.vector.reciprocal(stat[:, 12:14], stat[:, 10:12])
                own.link(nc.vector.reciprocal(stat[:, 3:4], stat[:, 2:3]))
                dve.wait_ge(o2_ready, b + 1)
                own.link(nc.vector.tensor_scalar(diff[:], bank[:, 6, 0:P], stat[:, 12:13], None, ALU.mult))
                own.link(nc.vector.scalar_tensor_tensor(out=both[:, 1, :], in0=bank[:, 6, P:2 * P], scalar=stat[:, 13:14], in1=diff[:],
                                                        op0=ALU.mult, op1=ALU.add))
                dve.wait_ge(c2s_raw, b + 1)
                nc.vector.scalar_tensor_tensor(out=both[:, 0, :], in0=bank[:, 7, 0:D], scalar=stat[:, 3:4], in1=rows[:, 0, :],
                                               op0=ALU.mult, op1=ALU.add).then_inc(c2s_ready, 1)
                dve.wait_ge(c2s_ready, b + 1)
                own.link(nc.vector.tensor_tensor(diff[:], both[:, 0, :], both[:, 1, :], ALU.subtract))
                dve.wait_ge(g_ready, b + 1)
                nc.vector.tensor_tensor(u[:], bank[:, 5, 0:D], rows[:, 2, :], ALU.add).then_inc(u_ready, 1)
                dve.wait_ge(e_ready, b + 1)
                own.link(nc.vector.tensor_scalar(u[:], u[:], 1.0, None, ALU.add))
                own.link(nc.vector.reciprocal(u[:], u[:]))
                own.link(nc.vector.tensor_tensor(diff[:], diff[:], u[:], ALU.mult))
                own.link(nc.vector.tensor_tensor(diff[:], diff[:], both[:, 1, :], ALU.add))
                nc.vector.tensor_tensor(x_res[:, b, :], x_res[:, b, :], diff[:], ALU.add).then_inc(x_ready, 1)
                dve.wait_ge(x_ready, b + 1)


def causal_linear_attention(nc, io, g):
    HD = D // H
    with ExitStack() as ctx:
        s = Stage(nc, ctx, "ca")
        w_q, w_k, w_v, w_c = (s.sb(n, [P, D]) for n in ("w_q", "w_k", "w_v", "w_c"))
        l_raw, l_mask = s.sb("l_raw", [P, HD]), s.sb("l_mask", [P, H, HD])
        heads, causal = s.sb("heads", [P, H]), s.sb("causal", [P, P])
        l_blk, l_T, ll, mix = (s.sb(n, [P, D]) for n in ("l_blk", "l_T", "ll", "mix"))
        norm = Norm(s, B, g["mhalf"])
        xn, xn_T, q_T, k_T, v = (s.sb(n, [P, B, D]) for n in ("xn", "xn_T", "q_T", "k_T", "v"))
        q_own = s.sb("q_own", [P, 2, H, P])
        att = s.sb("att", [P, 2, H, P])
        y, y_T = s.sb("y", [P, 2, D]), s.sb("y_T", [P, 2, P])
        bank = s.ps("bank", [P, 8, BANK])
        (w_in, dve_own, l_ready, l_turned, lT_ready, ll_made, ll_ready, mix_made, mix_ready, xn_ready, xn_turned, xnT_ready,
         proj_ready, kept, qown_ready, sc_ready, att_ready, y_made, y_ready, y_turned, yT_ready, out_ready, x_ready) = (
            s.sem(n) for n in (
                "w_in", "dve_own", "l_ready", "l_turned", "lT_ready", "ll_made", "ll_ready", "mix_made", "mix_ready", "xn_ready",
                "xn_turned", "xnT_ready", "proj_ready", "kept", "qown_ready", "sc_ready", "att_ready", "y_made", "y_ready",
                "y_turned", "yT_ready", "out_ready", "x_ready"))
        x_res, ident = g["x_res"], g["ident"]
        block = ctx.enter_context(nc.Block())
        N_IN = 8

        @block.sync
        def _(sp):
            for t, n in ((l_raw[:], io["L1_attn_Ltri"].rearrange("h d e -> (h d) e")), (l_mask[:].rearrange("p h e -> p (h e)"), io["l_mask"]),
                         (w_c[:], io["L1_attn_Wc"]), (w_q[:], io["L1_attn_Wq"]), (w_k[:], io["L1_attn_Wk"]), (w_v[:], io["L1_attn_Wv"]),
                         (heads[:], io["heads"]), (causal[:], io["causal"])):
                sp.dma_start(t, n).then_inc(w_in, 16)

        @block.gpsimd
        def _(pool):
            norm.pool(pool, 1)

        @block.tensor
        def _(pe):
            pe.wait_ge(l_ready, 1)
            nc.tensor.transpose(bank[:, 6, 0:P], l_blk[:], ident[:]).then_inc(l_turned, 1)
            pe.wait_ge(lT_ready, 1)
            nc.tensor.matmul(bank[:, 7, 0:P], l_T[:], l_T[:], start=True, stop=True).then_inc(ll_made, 1)
            pe.wait_ge(ll_ready, 1)
            nc.tensor.matmul(bank[:, 6, 0:P], ll[:], w_c[:], start=True, stop=True).then_inc(mix_made, 1)
            pe.wait_ge(xn_ready, 1)
            for b in range(B):
                mm = nc.tensor.transpose(bank[:, 0, b * P:(b + 1) * P], xn[:, b, :], ident[:])
            mm.then_inc(xn_turned, 1)
            pe.wait_ge(xnT_ready, 1)
            rhs = xn_T[:].rearrange("p b n -> p (b n)")
            nc.tensor.matmul(bank[:, 1, :], w_q[:], rhs, start=True, stop=True).then_inc(proj_ready, 1)
            nc.tensor.matmul(bank[:, 2, :], w_k[:], rhs, start=True, stop=True).then_inc(proj_ready, 1)
            for b in range(B):
                mm = nc.tensor.matmul(bank[:, 3, b * P:(b + 1) * P], xn_T[:, b, :], w_v[:], start=True, stop=True)
            mm.then_inc(proj_ready, 1)
            pe.wait_ge(kept, 3)
            pe.wait_ge(mix_ready, 1)

            def score(b):
                pe.wait_ge(qown_ready, b + 1)
                if b >= 1:
                    pe.wait_ge(att_ready, b)
                for c in range(4):
                    mm = nc.tensor.matmul(bank[:, c, :], k_T[:, b, :], q_own[:, b % 2, 4 * c:4 * c + 4, :].rearrange("p h n -> p (h n)"),
                                          start=True, stop=True)
                mm.then_inc(sc_ready, 1)

            score(0)
            for b in range(B):
                if b + 1 < B:
                    score(b + 1)
                pe.wait_ge(att_ready, b + 1)
                if b >= 1:
                    pe.wait_ge(y_ready, b)
                for h in range(H):
                    mm = nc.tensor.matmul(bank[:, 4, h * HD:(h + 1) * HD], att[:, b % 2, h, :], v[:, b, h * HD:(h + 1) * HD],
                                          start=True, stop=True)
                mm.then_inc(y_made, 1)
                pe.wait_ge(y_ready, b + 1)
                if b >= 1:
                    pe.wait_ge(yT_ready, b)
                nc.tensor.transpose(bank[:, 5, 0:P], y[:, b % 2, :], ident[:]).then_inc(y_turned, 1)
                pe.wait_ge(yT_ready, b + 1)
                if b >= 1:
                    pe.wait_ge(x_ready, b)
                nc.tensor.matmul(bank[:, 7, 0:D], y_T[:, b % 2, :], mix[:], start=True, stop=True).then_inc(out_ready, 1)

        @block.scalar
        def _(act):
            act.wait_ge(l_turned, 1)
            nc.scalar.copy(l_T[:], bank[:, 6, 0:P]).then_inc(lT_ready, 1)
            act.wait_ge(ll_made, 1)
            nc.scalar.copy(ll[:], bank[:, 7, 0:P]).then_inc(ll_ready, 1)
            act.wait_ge(mix_made, 1)
            nc.scalar.copy(mix[:], bank[:, 6, 0:P]).then_inc(mix_ready, 1)
            act.wait_ge(xn_turned, 1)
            nc.scalar.copy(xn_T[:].rearrange("p b n -> p (b n)"), bank[:, 0, :]).then_inc(xnT_ready, 1)
            for n, t in enumerate((q_T, k_T, v)):
                act.wait_ge(proj_ready, n + 1)
                nc.scalar.copy(t[:].rearrange("p b n -> p (b n)"), bank[:, 1 + n, :]).then_inc(kept, 1)
            for b in range(B):
                act.wait_ge(y_made, b + 1)
                nc.scalar.copy(y[:, b % 2, :], bank[:, 4, 0:D]).then_inc(y_ready, 1)
                act.wait_ge(y_turned, b + 1)
                nc.scalar.copy(y_T[:, b % 2, :], bank[:, 5, 0:P]).then_inc(yT_ready, 1)

        @block.vector
        def _(dve):
            own = Chain(dve, dve_own)
            dve.wait_ge(w_in, 16 * N_IN)
            nc.vector.tensor_tensor(l_blk[:].rearrange("p (h e) -> p h e", e=HD), l_mask[:], l_raw[:].unsqueeze(1).to_broadcast([P, H, HD]),
                                    ALU.mult).then_inc(l_ready, 1)
            norm.vector(dve, own, x_res, xn, 1).then_inc(xn_ready, 1)

            def own_queries(b):
                if b >= 2:
                    dve.wait_ge(sc_ready, b - 1)
                nc.vector.tensor_tensor(q_own[:, b % 2, :, :], q_T[:, b, :].unsqueeze(1).to_broadcast([P, H, P]),
                                        heads[:].unsqueeze(2).to_broadcast([P, H, P]), ALU.mult).then_inc(qown_ready, 1)

            dve.wait_ge(kept, 1)
            own_queries(0)
            own_queries(1)
            for b in range(B):
                dve.wait_ge(sc_ready, b + 1)
                if b >= 2:
                    dve.wait_ge(y_made, b - 1)
                nc.vector.tensor_tensor(att[:, b % 2, :, :], bank[:, 0:4, :].rearrange("p a (h n) -> p (a h) n", h=4),
                                        causal[:].unsqueeze(1).to_broadcast([P, H, P]), ALU.mult).then_inc(att_ready, 1)
                if b + 2 < B:
                    own_queries(b + 2)
                dve.wait_ge(out_ready, b + 1)
                nc.vector.tensor_tensor(x_res[:, b, :], x_res[:, b, :], bank[:, 7, 0:D], ALU.add).then_inc(x_ready, 1)


def mixture_of_experts(nc, io, g):
    E = 8
    ST = 2
    TOP_K = 2
    with ExitStack() as ctx:
        s = Stage(nc, ctx, "me")
        w_r = s.sb("w_r", [P, E])
        s_1, s_3, s_2 = s.sb("s_1", [P, ST * P]), s.sb("s_3", [P, ST * P]), s.sb("s_2", [P, ST, D])
        e_1, e_2 = s.sb("e_1", [P, E, P]), s.sb("e_2", [P, E, D])
        row_b, iota = s.sb("row_b", [P, E]), s.sb("iota", [P, E])
        norm = Norm(s, B, g["mhalf"])
        xn, xn_T, acc = (s.sb(n, [P, B, D]) for n in ("xn", "xn_T", "acc"))
        sig, sel, best, comb = (s.sb(n, [P, B, E]) for n in ("sig", "sel", "best", "comb"))
        idx = s.sb("idx", [P, B, E], U32)
        idx_f, hot, tmp = s.sb("idx_f", [P, B, E]), s.sb("hot", [P, B, E]), s.sb("tmp", [P, B, E])
        den, big, half = (s.sb(n, [P, B, 1]) for n in ("den", "big", "half"))
        silu, sh_T = s.sb("silu", [P, ST, B * P]), s.sb("sh_T", [P, ST, B * P])
        h_T = s.sb("h_T", [P, 2, B * P])
        bank = s.ps("bank", [P, 8, BANK])
        (w_in, dve_own, xn_ready, xn_turned, xnT_ready, r_made, sig_ready, a_made, silu_ready, sh_ready, s_made, s_ready, h_made,
         h_ready, y_made, y_used) = (s.sem(n) for n in (
            "w_in", "dve_own", "xn_ready", "xn_turned", "xnT_ready", "r_made", "sig_ready", "a_made", "silu_ready", "sh_ready",
            "s_made", "s_ready", "h_made", "h_ready", "y_made", "y_used"))
        x_res, ident = g["x_res"], g["ident"]
        block = ctx.enter_context(nc.Block())
        N_IN = 8

        @block.sync
        def _(sp):
            for t, n in ((w_r[:], io["L1_ffn_router_w"]), (s_1[:], io["L1_ffn_sw1"]), (s_3[:], io["L1_ffn_sw3"]),
                         (s_2[:], io["L1_ffn_sw2"].rearrange("(c p) n -> p c n", p=P)), (row_b[:], row(io["L1_ffn_router_bias"])),
                         (iota[:], io["iota"]), (e_1[:], io["L1_ffn_ew1"].rearrange("e d h -> d e h")),
                         (e_2[:], io["L1_ffn_ew2"].rearrange("e h d -> h e d"))):
                sp.dma_start(t, n).then_inc(w_in, 16)

        @block.gpsimd
        def _(pool):
            norm.pool(pool, 1)

        @block.tensor
        def _(pe):
            pe.wait_ge(xn_ready, 1)
            for b in range(B):
                mm = nc.tensor.transpose(bank[:, 0, b * P:(b + 1) * P], xn[:, b, :], ident[:])
            mm.then_inc(xn_turned, 1)
            pe.wait_ge(xnT_ready, 1)
            pe.wait_ge(w_in, 16 * N_IN)
            rhs = xn_T[:].rearrange("p b n -> p (b n)")
            for b in range(B):
                mm = nc.tensor.matmul(bank[:, 1, b * E:(b + 1) * E], xn_T[:, b, :], w_r[:], start=True, stop=True)
            mm.then_inc(r_made, 1)
            for c in range(ST):
                nc.tensor.matmul(bank[:, 2 + c, :], s_1[:, c * P:(c + 1) * P], rhs, start=True, stop=True)
                nc.tensor.matmul(bank[:, 4 + c, :], s_3[:, c * P:(c + 1) * P], rhs, start=True, stop=True).then_inc(a_made, 1)

            def hidden(e):
                if e == 0:
                    pe.wait_ge(sig_ready, 1)
                else:
                    pe.wait_ge(h_ready, max(e - 1, 1))
                nc.tensor.matmul(bank[:, e % 2, :], e_1[:, e, :], rhs, start=True, stop=True).then_inc(h_made, 1)

            hidden(0)
            pe.wait_ge(sh_ready, ST)
            for b in range(B):
                for c in range(ST):
                    mm = nc.tensor.matmul(bank[:, 6, b * P:(b + 1) * P], sh_T[:, c, b * P:(b + 1) * P], s_2[:, c, :],
                                          start=(c == 0), stop=(c == ST - 1))
            mm.then_inc(s_made, 1)
            for e in range(E):
                if e + 1 < E:
                    hidden(e + 1)
                pe.wait_ge(h_ready, e + 1)
                if e >= 2:
                    pe.wait_ge(y_used, e - 1)
                for b in range(B):
                    mm = nc.tensor.matmul(bank[:, 2 + e % 2, b * P:(b + 1) * P], h_T[:, e % 2, b * P:(b + 1) * P], e_2[:, e, :],
                                          start=True, stop=True)
                mm.then_inc(y_made, 1)

        @block.scalar
        def _(act):
            act.wait_ge(xn_turned, 1)
            nc.scalar.copy(xn_T[:].rearrange("p b n -> p (b n)"), bank[:, 0, :]).then_inc(xnT_ready, 1)
            act.wait_ge(r_made, 1)
            nc.scalar.activation(sig[:].rearrange("p b e -> p (b e)"), bank[:, 1, 0:B * E], ACT.Sigmoid).then_inc(sig_ready, 1)
            for c in range(ST):
                act.wait_ge(a_made, c + 1)
                nc.scalar.activation(silu[:, c, :], bank[:, 2 + c, :], ACT.Silu).then_inc(silu_ready, 1)
            for e in range(E):
                act.wait_ge(h_made, e + 1)
                if e >= 2:
                    act.wait_ge(y_made, e - 1)
                nc.scalar.activation(h_T[:, e % 2, :], bank[:, e % 2, :], ACT.Gelu).then_inc(h_ready, 1)

        @block.vector
        def _(dve):
            own = Chain(dve, dve_own)
            norm.vector(dve, own, x_res, xn, 1).then_inc(xn_ready, 1)
            dve.wait_ge(w_in, 16 * N_IN)
            dve.wait_ge(sig_ready, 1)
            own.link(nc.vector.tensor_tensor(sel[:], sig[:], row_b[:].unsqueeze(1).to_broadcast([P, B, E]), ALU.add))
            for b in range(B):
                last = nc.vector.max(out=best[:, b, :], in_=sel[:, b, :])
            own.link(last)
            for b in range(B):
                last = nc.vector.max_index(out=idx[:, b, :], in_max=best[:, b, :], in_values=sel[:, b, :])
            own.link(last)
            own.link(nc.vector.tensor_copy(idx_f[:], idx[:]))
            labels = iota[:].unsqueeze(1).to_broadcast([P, B, E])
            own.link(nc.vector.tensor_tensor(hot[:], labels, idx_f[:, :, 0:1].to_broadcast([P, B, E]), ALU.is_equal))
            own.link(nc.vector.tensor_tensor(tmp[:], labels, idx_f[:, :, 1:2].to_broadcast([P, B, E]), ALU.is_equal))
            own.link(nc.vector.tensor_tensor(hot[:], hot[:], tmp[:], ALU.add))
            own.link(nc.vector.tensor_tensor(comb[:], hot[:], sig[:], ALU.mult))
            own.link(nc.vector.tensor_reduce(den[:, :, 0], comb[:], AX.X, ALU.add))
            own.link(nc.vector.tensor_scalar(big[:], den[:], 1e-9, None, ALU.is_gt))
            own.link(nc.vector.tensor_scalar(den[:], den[:], 1e-9, None, ALU.add))
            own.link(nc.vector.reciprocal(den[:], den[:]))
            own.link(nc.vector.tensor_tensor(den[:], den[:], big[:], ALU.mult))
            own.link(nc.vector.tensor_scalar(half[:], big[:], -1.0 / TOP_K, 1.0 / TOP_K, ALU.mult, ALU.add))
            own.link(nc.vector.tensor_tensor(comb[:], comb[:], den[:].to_broadcast([P, B, E]), ALU.mult))
            own.link(nc.vector.tensor_tensor(tmp[:], hot[:], half[:].to_broadcast([P, B, E]), ALU.mult))
            own.link(nc.vector.tensor_tensor(comb[:], comb[:], tmp[:], ALU.add))
            for c in range(ST):
                dve.wait_ge(a_made, c + 1)
                dve.wait_ge(silu_ready, c + 1)
                nc.vector.tensor_tensor(sh_T[:, c, :], bank[:, 4 + c, :], silu[:, c, :], ALU.mult).then_inc(sh_ready, 1)
            dve.wait_ge(s_made, 1)
            own.link(nc.vector.tensor_tensor(acc[:], x_res[:], bank[:, 6, :].rearrange("p (b d) -> p b d", b=B), ALU.add))
            for e in range(E):
                dve.wait_ge(y_made, e + 1)
                for b in range(B):
                    last = nc.vector.scalar_tensor_tensor(out=(x_res if e == E - 1 else acc)[:, b, :], in0=bank[:, 2 + e % 2, b * P:(b + 1) * P],
                                                          scalar=comb[:, b, e:e + 1], in1=acc[:, b, :], op0=ALU.mult, op1=ALU.add)
                last.then_inc(y_used, 1)
                dve.wait_ge(y_used, e + 1)


STAGES = (latent_cross_attention, linear_attention, local_transformer, two_way_attention,
          causal_linear_attention, mixture_of_experts)


def perceiver(nc, io, out, stages=STAGES):
    with ExitStack() as ctx:
        s = Stage(nc, ctx, "g")
        g = {"x_res": s.sb("x_res", [P, B, D]), "ident": s.sb("ident", [P, P]), "ones_row": s.sb("ones_row", [1, P]),
             "mhalf": s.sb("mhalf", [P, 64])}
        first_in = s.sem("first_in")
        set_up = s.sem("set_up")
        with nc.Block() as block:
            @block.sync
            def _(sp):
                sp.dma_start(g["x_res"][:], io["x"].rearrange("b t d -> t b d")).then_inc(first_in, 16)
                sp.dma_start(g["ident"][:], io["ident"]).then_inc(first_in, 16)
                sp.wait_ge(first_in, 32)

            @block.gpsimd
            def _(pool):
                nc.gpsimd.memset(g["ones_row"][:], 1.0)
                nc.gpsimd.memset(g["mhalf"][:], -0.5).then_inc(set_up, 1)
                pool.wait_ge(set_up, 1)
        for stage in stages:
            with nc.cleanup_on_exit():
                stage(nc, io, g)
        x_out = s.sem("x_out")
        with nc.Block() as block:
            @block.sync
            def _(sp):
                sp.dma_start(out.rearrange("b t d -> t b d"), g["x_res"][:]).then_inc(x_out, 16)
                sp.wait_ge(x_out, 16)


def shape_constants():
    f = np.float32
    half = np.arange(0, DH, 2, dtype=f)
    freqs = np.arange(P, dtype=f)[:, None] * (f(1) / f(10000) ** (half / f(DH)))[None, :]
    freqs = np.concatenate([freqs, freqs], -1)
    power = (np.arange(P, dtype=f) - f(P // 2)) / f(16)
    scale = ((half + f(0.4 * DH)) / f(1.4 * DH))[None, :] ** power[:, None]
    scale = np.concatenate([scale, scale], -1)
    sign = np.where(np.arange(DH) < DH // 2, f(-1), f(1))
    rotary = np.concatenate([np.cos(freqs) * scale, np.sin(freqs) * sign * scale,
                             np.cos(freqs) / scale, np.sin(freqs) * sign / scale], 1).astype(f)
    i, j = np.arange(P)[:, None], np.arange(P)[None, :]
    return {
        "ident": np.eye(P, dtype=f),
        "rotary": rotary,
        "band": np.where((i >= j) & (i <= j + 32), f(0), f(-BIG)).astype(f),
        "heads": (i // 8 == np.arange(H)[None, :]).astype(f),
        "l_mask": ((i // 8 == j // 8) & (i >= j)).astype(f),
        "causal": (i <= j).astype(f),
        "iota": np.tile(np.arange(8, dtype=f), (P, 1)),
        "shift": (i + 1 == j).astype(f),
    }


TRANSPOSED = ("L1_xattn_Wq_c", "L1_xattn_Wk_s", "L1_xattn_Wv_s", "L1_xattn_Wq_s", "L1_xattn_Wk_c", "L1_xattn_Wv_c", "L1_xattn_Wg",
              "L1_attn_Wq", "L1_attn_Wk", "L1_attn_Wv", "L1_attn_Wc", "L1_ffn_router_w")


def device_inputs(inputs):
    arrays = {}
    for name, a in inputs.items():
        a = np.ascontiguousarray(a)
        arrays[name] = a.view(np.uint8) if a.dtype == np.bool_ else a
    for name in ("L0_attn_bq", "L0_attn_b1"):
        arrays[name] = np.ascontiguousarray(arrays[name].reshape(-1, P).T)
    for name in TRANSPOSED:
        arrays[name] = np.ascontiguousarray(arrays[name].T)
    qs, ks = arrays["L0_ffn_q_scale"], arrays["L0_ffn_k_scale"]
    arrays["L0_ffn_gains"] = np.concatenate([qs, np.roll(qs, DH // 2, 1), ks, np.roll(ks, DH // 2, 1)], 1)
    b1 = arrays["L0_ffn_b1"].reshape(-1, 2, 341)
    b1 = np.pad(b1, ((0, 0), (0, 0), (0, 3 * P - 341))).reshape(-1, 6, P)
    arrays["L0_ffn_cols"] = np.ascontiguousarray(
        np.concatenate([arrays["L0_ffn_ln_g"][:, None], arrays["L0_ffn_ln_b"][:, None], b1], 1).transpose(0, 2, 1))
    arrays.update(shape_constants())
    return arrays


def kernel(**inputs):
    import concourse.bacc as _bacc
    from concourse.bass_utils import run_bass_kernel_spmd as _run

    nc = _bacc.Bacc("TRN2", target_bir_lowering=False, num_devices=1)
    arrays = {f"in_{n}_dram": a for n, a in device_inputs(inputs).items()}
    io = {n[3:-5]: nc.dram_tensor(n, a.shape, mybir.dt.from_np(a.dtype), kind="ExternalInput").ap() for n, a in arrays.items()}
    out = nc.dram_tensor("out_0_dram", (B, P, D), F32, kind="ExternalOutput").ap()
    perceiver(nc, io, out)
    r = _run(nc, [arrays], core_ids=[0])
    return r.results[0]["out_0_dram"]
```

```python
from contextlib import ExitStack

import concourse.bass as bass
import numpy as np
from concourse import mybir
from concourse.alu_op_type import AluOpType as ALU

F32 = mybir.dt.float32
U8 = mybir.dt.uint8
U32 = mybir.dt.uint32
ACT = mybir.ActivationFunctionType
AX = mybir.AxisListType

P = 128
B = 4
D = 128
H = 16
DH = 64
INNER = H * DH
PAIRS = INNER // P
CTX = 2048
CT = CTX // P
BANK = 512
BIG = 1e30


class Chain:

    def __init__(self, eng, sem):
        self.eng, self.sem, self.done, self.loops = eng, sem, 0, []

    def enter(self, i, per):
        self.loops.append((i, per, self.done))
        self.done = 0

    def leave(self, turns):
        i, per, before = self.loops.pop()
        assert self.done == per, (self.done, per)
        self.done = before + turns * per

    def link(self, ins):
        ins.then_inc(self.sem, 1)
        self.done += 1
        value = self.done
        for i, per, before in self.loops:
            value = i * per + (value + before)
        self.eng.wait_ge(self.sem, value)


def columns(nc_ap, n):
    return nc_ap.rearrange("(c p) -> p c", c=n)


def row(ap, n=P):
    return ap.rearrange("(a d) -> a d", a=1).partition_broadcast(n).rearrange("p a d -> p (a d)")


def step(eng, sem):
    eng.sem_inc(sem, 1)


class Stage:

    def __init__(self, nc, ctx, name):
        self.nc, self.ctx, self.name = nc, ctx, name

    def sb(self, name, shape, dt=F32):
        return self.ctx.enter_context(self.nc.sbuf_tensor(f"{self.name}_{name}", shape, dt))

    def ps(self, name, shape, dt=F32):
        return self.ctx.enter_context(self.nc.psum_tensor(f"{self.name}_{name}", shape, dt))

    def sem(self, name):
        return self.nc.alloc_semaphore(f"{self.name}_{name}")


class Norm:

    def __init__(self, s, tiles, mhalf, name="ln"):
        self.nc, self.tiles, self.mhalf = s.nc, tiles, mhalf
        self.stat, self.mv = s.sb(name + "_stat", [P, tiles, 6]), s.sb(name + "_mv", [P, tiles, 2])
        self.var, self.rstd = s.sb(name + "_var", [P, tiles]), s.sb(name + "_rstd", [P, tiles])
        self.var_ready, self.rstd_ready = s.sem(name + "_var_ready"), s.sem(name + "_rstd_ready")

    def vector(self, eng, own, src, dst, count, passed=None, part=None):
        nc = self.nc
        first, end = part or (0, self.tiles)
        for t in range(first, end):
            last = nc.vector.bn_stats(self.stat[:, t, :], src[:, t, :])
        own.link(last)
        if passed is not None:
            step(eng, passed)
        for t in range(first, end):
            last = nc.vector.bn_aggr(self.mv[:, t, :], self.stat[:, t, :])
        own.link(last)
        nc.vector.tensor_scalar(self.var[:, first:end], self.mv[:, first:end, 1], 1e-5, None, ALU.add).then_inc(self.var_ready, 1)
        eng.wait_ge(self.rstd_ready, count)
        for t in range(first, end):
            last = nc.vector.tensor_scalar(dst[:, t, :], src[:, t, :], self.mv[:, t, 0:1], self.rstd[:, t:t + 1],
                                           ALU.subtract, ALU.mult)
        return last

    def pool(self, eng, count, part=None):
        first, end = part or (0, self.tiles)
        eng.wait_ge(self.var_ready, count)
        self.nc.gpsimd.tensor_tensor(self.rstd[:, first:end], self.var[:, first:end], self.mhalf[:, 0:end - first], ALU.pow).then_inc(self.rstd_ready, 1)


def latent_cross_attention(nc, io, g):
    KT = CT + 1
    KEYS = KT * P
    NT = KT + 1
    LAG = 3
    EARLY = 2
    GIVEN = 1
    GROUPS = [range(a, min(a + 4, KT)) for a in range(0, KT, 4)]
    NG = len(GROUPS)
    with ExitStack() as ctx:
        s = Stage(nc, ctx, "xa")
        w_q = s.sb("w_q", [P, INNER])
        w_kv = s.sb("w_kv", [P, 2 * INNER])
        w_out = s.sb("w_out", [P, PAIRS, D])
        cols = s.sb("cols", [P, 8])
        rows = s.sb("rows", [P, 5, D])
        stat = s.sb("stat", [P, CT, 6])
        mv = s.sb("mv", [P, CT, 2])
        ve = s.sb("ve", [P, CT])
        rstd = s.sb("rstd", [P, CT])
        lat = s.sb("lat", [P, B, D])
        lat_T = s.sb("lat_T", [P, B, P])
        ctx_raw = s.sb("ctx_raw", [P, CT, D])
        z = s.sb("z", [P, CT, D])
        xn = s.sb("xn", [P, KT, D])
        xn_T = s.sb("xn_T", [P, KEYS])
        maskb = s.sb("maskb", [P, CTX], U8)
        pen = s.sb("pen", [P, KEYS])
        ss, root, inv, rn = (s.sb(n, [P, 2, H]) for n in ("ss", "root", "inv", "rn"))
        err = s.sb("err", [P, H])
        kn_T = s.sb("kn_T", [P, PAIRS, KEYS])
        q_T = s.sb("q_T", [P, PAIRS, P])
        q_head = s.sb("q_head", [P, 2, P])
        prob = s.sb("prob", [P, 2, KEYS])
        sq = prob[:, 0, 0:2 * INNER].rearrange("p (a n) -> p a n", a=2)
        kn = prob[:, 1, 0:2 * INNER].rearrange("p (a n) -> p a n", a=2)
        mx = s.sb("mx", [P, 2, 4])
        nmax = s.sb("nmax", [P, 2])
        psumr = s.sb("psumr", [P, 2])
        rsum = s.sb("rsum", [P, 2])
        p_T = s.sb("p_T", [P, KT, 2, P])
        o_T = s.sb("o_T", [P, 2 * P])
        att = s.sb("att", [P, INNER])
        att_T = s.sb("att_T", [P, PAIRS, P])
        lat_n = att[:, 0:B * D].rearrange("p (b d) -> p b d", b=B)
        warm = s.sb("warm", [P, 1])
        bank = s.ps("bank", [P, 8, BANK])

        w_in, affine_in = s.sem("w_in"), s.sem("affine_in")
        ctx_in = s.sem("ctx_in")
        mask_in = s.sem("mask_in")
        passed = s.sem("passed")
        dve_own, act_own, pool_own = s.sem("dve_own"), s.sem("act_own"), s.sem("pool_own")
        var_ready, rstd_ready = s.sem("var_ready"), s.sem("rstd_ready")
        z_ready, zT_ready, xnT_ready, xn_ready = s.sem("z_ready"), s.sem("zT_ready"), s.sem("xnT_ready"), s.sem("xn_ready")
        pen_ready = s.sem("pen_ready")
        proj_ready, sq_ready, ss_ready, root_ready, inv_ready, rn_ready, kn_ready = (s.sem(n) for n in
            ("proj_ready", "sq_ready", "ss_ready", "root_ready", "inv_ready", "rn_ready", "kn_ready"))
        kn_turned, knT_ready = s.sem("kn_turned"), s.sem("knT_ready")
        qh_ready, sim_ready, masked, max_ready, exp_ready = (s.sem(n) for n in
            ("qh_ready", "sim_ready", "masked", "max_ready", "exp_ready"))
        p_turned, pT_ready, o_ready, oT_ready, v_ready, att_ready = (s.sem(n) for n in
            ("p_turned", "pT_ready", "o_ready", "oT_ready", "v_ready", "att_ready"))
        latn_ready, lat_ready, latT_turned, latT_ready = s.sem("latn_ready"), s.sem("lat_ready"), s.sem("latT_turned"), s.sem("latT_ready")
        att_turned, attT_ready, y_ready, x_ready = (s.sem(n) for n in ("att_turned", "attT_ready", "y_ready", "x_ready"))

        mask_dram = io["mask_BxS2_bf1"]
        x_res, ident, ones_row = g["x_res"], g["ident"], g["ones_row"]
        block = ctx.enter_context(nc.Block())

        def context(b):
            return io["ctx_1024"][b].rearrange("a (p t) d -> (a p) t d", p=P)

        def mask(b):
            return mask_dram[b].partition_broadcast(P).rearrange("p a n -> p (a n)")

        @block.sync
        def _(sp):
            sp.dma_start(ctx_raw[:], context(slice(0, 1))).then_inc(ctx_in, 16)
            sp.dma_start(w_q[:], io["L0_xattn_Wq"]).then_inc(w_in, 16)
            sp.dma_start(w_kv[:], io["L0_xattn_Wkv"]).then_inc(w_in, 16)
            sp.dma_start(maskb[:], mask(slice(0, 1))).then_inc(mask_in, 16)
            for j, n in enumerate(("qn_g", "kn_g")):
                for half in range(2):
                    sp.dma_start(cols[half * DH:(half + 1) * DH, 5 + j:6 + j],
                                 io["L0_xattn_" + n].rearrange("(p a) -> p a", a=1)).then_inc(w_in, 16)
            sp.dma_start(w_out[:], io["L0_xattn_Wout"].rearrange("(c p) n -> p c n", p=P)).then_inc(w_in, 16)
            sp.dma_start(rows[:, 4, :], row(io["L0_xattn_bout"])).then_inc(w_in, 16)
            with sp.Fori(0, B - 1) as b:
                sp.wait_ge(z_ready, b * CT + CT)
                step(sp, passed)
                sp.dma_start(ctx_raw[:], context(bass.ds(b + 1, 1))).then_inc(ctx_in, 16)
                sp.wait_ge(pen_ready, b + 1)
                step(sp, passed)
                sp.dma_start(maskb[:], mask(bass.ds(b + 1, 1))).then_inc(mask_in, 16)
        W_LOADS = 2 + 4 + 2
        AFFINE_LOADS = 8

        @block.gpsimd
        def _(pool):
            def power(out, base, expo):
                return nc.gpsimd.tensor_tensor(out, base, expo, ALU.pow)

            def queries(b, p):
                if isinstance(p, int):
                    pool.wait_ge(knT_ready, b * NT + 1)
                    step(pool, passed)
                for e in range(2):
                    if not isinstance(p, int):
                        pool.wait_ge(sim_ready, b * (H * NG) + (p * (2 * NG) + (e - 1) * NG) + GIVEN)
                    half = slice(e * DH, (e + 1) * DH)
                    nc.gpsimd.tensor_copy(q_head[half, e, :], q_T[half, bass.ds(p, 1), :].rearrange("p a d -> p (a d)")).then_inc(qh_ready, 1)

            own = Chain(pool, pool_own)
            nc.gpsimd.memset(pen[:, CTX:KEYS], 0.0)
            own.link(nc.gpsimd.memset(q_head[:], 0.0))
            for n in range(2):
                pool.wait_ge(var_ready, n + 1)
                power(rstd[:, 0:B], ve[:, 0:B], g["mhalf"][:, 0:B]).then_inc(rstd_ready, 1)
            with pool.Fori(0, B) as b:
                own.enter(b, 3 * NT + CT)
                pool.wait_ge(var_ready, b + 3)
                power(rstd[:], ve[:], g["mhalf"][:, 0:CT]).then_inc(rstd_ready, 1)
                pool.wait_ge(z_ready, b * CT + CT)
                pool.wait_ge(o_ready, b * PAIRS + GIVEN)
                for t in range(NT):
                    k = t % 2
                    pool.wait_ge(inv_ready, b * NT + (t + 1))
                    own.link(nc.gpsimd.tensor_tensor(err[:], inv[:, k, :], inv[:, k, :], ALU.mult))
                    own.link(nc.gpsimd.tensor_tensor(err[:], err[:], ss[:, k, :], ALU.mult))
                    step(pool, passed)
                    own.link(nc.gpsimd.tensor_scalar(err[:], err[:], -0.5, 1.5, ALU.mult, ALU.add))
                    nc.gpsimd.tensor_tensor(rn[:, k, :], inv[:, k, :], err[:], ALU.mult).then_inc(rn_ready, 1)
                    if t == LAG + 1:
                        pool.wait_ge(rn_ready, b * NT + (t + 1))
                        queries(b, 0)
                        pool.wait_ge(qh_ready, b * H + 2)
                    if t < CT:
                        own.link(nc.gpsimd.tensor_tensor(xn[:, t, :], z[:, t, :], rows[:, 0, :], ALU.mult))
                        nc.gpsimd.tensor_tensor(xn[:, t, :], xn[:, t, :], rows[:, 1, :], ALU.add).then_inc(xn_ready, 1)
                    elif t == CT:
                        nc.gpsimd.tensor_copy(xn[:, CT, :], lat[:, bass.ds(b, 1), :].rearrange("p a d -> p (a d)")).then_inc(xn_ready, 1)
                with pool.Fori(0, PAIRS - 1) as p:
                    queries(b, p + 1)
                own.leave(B)

        @block.tensor
        def _(pe):
            for freed in (o_ready, sim_ready):
                pe.sem_inc(freed, GIVEN)
            def project(b, t):
                if t >= LAG:
                    pe.wait_ge(kn_ready, b * NT + (t - LAG + 1))
                if t == 0:
                    pe.wait_ge(xnT_ready, b * 5 + 5)
                tile = t - 1 if t > 0 else CT
                keys = xn_T[:, tile * P:(tile + 1) * P]
                for c in range(2):
                    w = w_q[:, c * BANK:(c + 1) * BANK] if t == 0 else w_kv[:, c * BANK:(c + 1) * BANK]
                    mm = nc.tensor.matmul(bank[:, 2 * (t % LAG) + c, :], keys, w, start=True, stop=True)
                mm.then_inc(proj_ready, 1)

            def turn(b, t):
                pe.wait_ge(kn_ready, b * NT + (t + 1))
                if t >= 1:
                    pe.wait_ge(knT_ready, b * NT + t)
                else:
                    pe.wait_ge(x_ready, b + GIVEN)
                for c in range(PAIRS):
                    mm = nc.tensor.transpose(bank[:, 6 + c // 4, (c % 4) * P:(c % 4 + 1) * P],
                                             kn[:, t % 2, c * P:(c + 1) * P], ident[:])
                mm.then_inc(kn_turned, 1)

            def score(b, p, e, c, first=False):
                head = p * 2 + e
                if c == 0:
                    pe.wait_ge(qh_ready, b * H + (head + 1))
                if first:
                    pe.wait_ge(knT_ready, b * NT + min(4 * c + 5, NT))
                    pe.wait_ge(kn_ready, b * NT + (NT - LAG + 1 + c // 2))
                if not first and c in (0, 2, 4):
                    pe.wait_ge(masked, b * (3 * H) + (head * 3 + (c // 2 - 2)))
                n = len(GROUPS[c]) * P
                nc.tensor.matmul(bank[:, c, 0:n], q_head[:, e, :],
                                 kn_T[:, bass.ds(p, 1), c * BANK:c * BANK + n].rearrange("p a n -> p (a n)"),
                                 start=True, stop=True).then_inc(sim_ready, 1)

            def turn_prob(b, p, e, n):
                if n == 0:
                    pe.wait_ge(exp_ready, b * H + (p * 2 + e + 1))
                k = NG * e + n
                pe.wait_ge(pT_ready, b * (H * NG) + (p * (2 * NG) + max(k - 1, 0)) + GIVEN)
                for j, t in enumerate(GROUPS[n]):
                    mm = nc.tensor.transpose(bank[:, 5 + k % 2, j * P:(j + 1) * P], prob[:, e, t * P:(t + 1) * P], ident[:])
                mm.then_inc(p_turned, 1)

            def turn_and_score(b, p, e, scored=None, valued=None):
                for n in range(NG):
                    turn_prob(b, p, e, n)
                    if scored is not None:
                        score(b, scored, e, n)
                    if n == 1 and valued is not None:
                        value(b, valued)

            def turn_context(b, half):
                if half == 0 and not isinstance(b, int):
                    pe.wait_ge(masked, b * (3 * H))
                    step(pe, passed)
                for c in (2 * half, 2 * half + 1):
                    pe.wait_ge(z_ready, b * CT + (4 * c + 4))
                    for j in range(4):
                        mm = nc.tensor.transpose(bank[:, c, j * P:(j + 1) * P], z[:, 4 * c + j, :], ident[:])
                    mm.then_inc(zT_ready, 1)

            def gather(b, p):
                pe.wait_ge(pT_ready, b * (H * NG) + (p * (2 * NG) + (2 * NG - 1)) + GIVEN)
                pe.wait_ge(att_ready, b * PAIRS + (p + GIVEN))
                for t in range(KT):
                    if t == GROUPS[-1][0]:
                        pe.wait_ge(pT_ready, b * (H * NG) + (p * (2 * NG) + 2 * NG) + GIVEN)
                    mm = nc.tensor.matmul(bank[:, 7, 0:2 * P], xn[:, t, :], p_T[:, t, :, :].rearrange("p e q -> p (e q)"),
                                          start=(t == 0), stop=(t == KT - 1))
                mm.then_inc(o_ready, 1)

            def value(b, p):
                pe.wait_ge(oT_ready, b * PAIRS + (p + 1))
                w = w_kv[:, INNER:2 * INNER].rearrange("p (c n) -> p c n", n=P)
                for e in range(2):
                    mm = nc.tensor.matmul(bank[:, 7, 2 * P + e * DH:2 * P + (e + 1) * DH], o_T[:, e * P:(e + 1) * P],
                                          w[:, bass.ds(p, 1), e * DH:(e + 1) * DH].rearrange("p a n -> p (a n)"),
                                          start=True, stop=True)
                mm.then_inc(v_ready, 1)

            pe.wait_ge(latn_ready, 1)
            for t in range(B):
                mm = nc.tensor.transpose(bank[:, 0, t * P:(t + 1) * P], lat_n[:, t, :], ident[:])
            mm.then_inc(latT_turned, 1)
            pe.wait_ge(latT_ready, 1)

            def batch(b, last):
                for t in range(EARLY, NT + LAG):
                    if t < NT:
                        project(b, t)
                    if t >= LAG:
                        turn(b, t - LAG)
                    if t == NT + 1:
                        score(b, 0, 0, 0, first=True)
                        score(b, 0, 0, 1, first=True)
                for c in range(2, NG):
                    score(b, 0, 0, c, first=True)
                for c in range(NG):
                    score(b, 0, 1, c)
                turn_and_score(b, 0, 0, scored=1)
                pe.wait_ge(xn_ready, b * KT + KT)
                step(pe, passed)
                with pe.Fori(0, PAIRS - 2) as p:
                    turn_and_score(b, p, 1, scored=p + 1)
                    gather(b, p)
                    turn_and_score(b, p + 1, 0, scored=p + 2, valued=p)
                turn_and_score(b, PAIRS - 2, 1, scored=PAIRS - 1)
                gather(b, PAIRS - 2)
                turn_and_score(b, PAIRS - 1, 0, valued=PAIRS - 2)
                turn_and_score(b, PAIRS - 1, 1)
                if not last:
                    turn_context(b + 1, 0)
                    turn_context(b + 1, 1)
                gather(b, PAIRS - 1)
                if not last:
                    project(b + 1, 0)
                value(b, PAIRS - 1)
                pe.wait_ge(att_ready, b * PAIRS + PAIRS + GIVEN)
                for c in range(PAIRS):
                    mm = nc.tensor.transpose(bank[:, 5 + c // 4, (c % 4) * P:(c % 4 + 1) * P], att[:, c * P:(c + 1) * P], ident[:])
                mm.then_inc(att_turned, 1)
                if not last:
                    project(b + 1, 1)
                pe.wait_ge(attT_ready, b + 1)
                for c in range(PAIRS):
                    mm = nc.tensor.matmul(bank[:, 7, 3 * P:4 * P], att_T[:, c, :], w_out[:, c, :], start=(c == 0), stop=(c == PAIRS - 1))
                mm.then_inc(y_ready, 1)

            turn_context(0, 0)
            turn_context(0, 1)
            pe.wait_ge(w_in, 16 * W_LOADS)
            for t in range(EARLY):
                project(0, t)
            with pe.Fori(0, B - 1) as b:
                batch(b, last=False)
            batch(B - 1, last=True)

        @block.scalar
        def _(act):
            for j, n in enumerate(("ln_x_g", "ln_x_b", "ln_l_g", "ln_l_b")):
                act.dma_start(cols[:, j:j + 1], columns(io["L0_xattn_" + n], 1)).then_inc(affine_in, 16)
                act.dma_start(rows[:, j, :], row(io["L0_xattn_" + n])).then_inc(affine_in, 16)
            act.sem_inc(pT_ready, GIVEN)
            own = Chain(act, act_own)

            def preload(function):
                nc.scalar.activation(warm[:], ident[:, 0:1], function)

            def square(b, t):
                act.wait_ge(proj_ready, b * NT + (t + 1))
                if t >= 2:
                    act.wait_ge(ss_ready, b * NT + (t - 1))
                src = bank[:, 2 * (t % LAG):2 * (t % LAG) + 2, :].rearrange("p a n -> p (a n)")
                nc.scalar.activation(sq[:, t % 2, :], src, ACT.Square, scale=DH ** -0.5).then_inc(sq_ready, 1)

            def square_root(b, t):
                act.wait_ge(ss_ready, b * NT + (t + 1))
                nc.scalar.activation(root[:, t % 2, :], ss[:, t % 2, :], ACT.Sqrt).then_inc(root_ready, 1)

            def keep_turned(b, t):
                act.wait_ge(kn_turned, b * NT + (t + 1))
                src = bank[:, 6:8, :].rearrange("p a (c k) -> p (a c) k", k=P)
                if t == 0:
                    nc.scalar.activation(q_T[:], src, ACT.Copy, scale=cols[:, 4:5]).then_inc(knT_ready, 1)
                else:
                    nc.scalar.copy(kn_T[:, :, (t - 1) * P:t * P], src).then_inc(knT_ready, 1)

            def exponent(b, p, e):
                act.wait_ge(max_ready, b * H + (p * 2 + e + 1))
                nc.scalar.activation(prob[:, e, :], prob[:, e, :], ACT.Exp, bias=nmax[:, e:e + 1],
                                     accum_out=psumr[:, e:e + 1]).then_inc(exp_ready, 1)

            def keep_prob(b, p, e):
                for n, tiles in enumerate(GROUPS):
                    k = NG * e + n
                    act.wait_ge(p_turned, b * (H * NG) + (p * (2 * NG) + (k + 1)))
                    if k == 0:
                        act.wait_ge(o_ready, b * PAIRS + (p + GIVEN))
                    m = len(tiles)
                    nc.scalar.copy(p_T[:, tiles[0]:tiles[0] + m, e, :],
                                   bank[:, 5 + k % 2, 0:m * P].rearrange("p (t q) -> p t q", t=m)).then_inc(pT_ready, 1)

            act.wait_ge(latT_turned, 1)
            act.wait_ge(affine_in, 16 * AFFINE_LOADS)
            nc.scalar.activation(lat_T[:].rearrange("p b t -> p (b t)"), bank[:, 0, :], ACT.Identity,
                                 bias=cols[:, 3:4], scale=cols[:, 2:3]).then_inc(latT_ready, 1)
            act.wait_ge(latT_ready, 1)

            def keep_context(b, half):
                for c in (2 * half, 2 * half + 1):
                    act.wait_ge(zT_ready, b * 4 + (c + 1))
                    nc.scalar.activation(xn_T[:, c * BANK:(c + 1) * BANK], bank[:, c, :], ACT.Identity,
                                         bias=cols[:, 1:2], scale=cols[:, 0:1]).then_inc(xnT_ready, 1)
                if half == 1:
                    nc.scalar.copy(xn_T[:, CTX:KEYS], lat_T[:, bass.ds(b, 1), :].rearrange("p a t -> p (a t)")).then_inc(xnT_ready, 1)

            def batch(b, last):
                for t in range(NT + LAG):
                    if 0 < t < NT:
                        square(b, t)
                    if 1 < t <= NT:
                        square_root(b, t - 1)
                    if t == NT:
                        preload(ACT.Exp)
                    if t >= LAG:
                        keep_turned(b, t - LAG)
                exponent(b, 0, 0)
                exponent(b, 0, 1)
                with act.Fori(0, PAIRS - 1) as p:
                    keep_prob(b, p, 0)
                    keep_prob(b, p, 1)
                    exponent(b, p + 1, 0)
                    exponent(b, p + 1, 1)
                keep_prob(b, PAIRS - 1, 0)
                keep_prob(b, PAIRS - 1, 1)
                if not last:
                    preload(ACT.Sqrt)
                    keep_context(b + 1, 0)
                    keep_context(b + 1, 1)
                    square(b + 1, 0)
                act.wait_ge(att_turned, b + 1)
                nc.scalar.copy(att_T[:].rearrange("p c q -> p (c q)"), bank[:, 5:7, :].rearrange("p a n -> p (a n)")).then_inc(attT_ready, 1)
                if not last:
                    square_root(b + 1, 0)

            keep_context(0, 0)
            keep_context(0, 1)
            preload(ACT.Sqrt)
            act.wait_ge(w_in, 16 * W_LOADS)
            own.link(nc.scalar.activation(cols[:, 4:5], cols[:, 5:6], ACT.Copy, scale=cols[:, 6:7]))
            own.link(nc.scalar.mul(cols[:, 4:5], cols[:, 4:5], DH ** -0.5))
            square(0, 0)
            square_root(0, 0)
            with act.Fori(0, B - 1) as b:
                batch(b, last=False)
            batch(B - 1, last=True)

        @block.vector
        def _(dve):
            for freed in (x_ready, att_ready):
                dve.sem_inc(freed, GIVEN)
            own = Chain(dve, dve_own)

            def statistics(src, tiles):
                for t in range(tiles):
                    last = nc.vector.bn_stats(stat[:, t, :], src[:, t, :])
                own.link(last)
                step(dve, passed)
                for t in range(tiles):
                    last = nc.vector.bn_aggr(mv[:, t, :], stat[:, t, :])
                own.link(last)
                nc.vector.tensor_scalar(ve[:, 0:tiles], mv[:, 0:tiles, 1], 1e-5, None, ALU.add).then_inc(var_ready, 1)

            def standardise(src, dst, tiles, rstd_count, signal=None):
                dve.wait_ge(rstd_ready, rstd_count)
                for t in range(tiles):
                    last = nc.vector.tensor_scalar(dst[:, t, :], src[:, t, :], mv[:, t, 0:1], rstd[:, t:t + 1],
                                                   ALU.subtract, ALU.mult)
                    if signal:
                        last.then_inc(signal, 1)
                return last

            def reduce(b, t):
                dve.wait_ge(sq_ready, b * NT + (t + 1))
                own.link(nc.vector.tensor_reduce(ss[:, t % 2, :], sq[:, t % 2, :].rearrange("p (h e) -> p h e", e=DH), AX.X, ALU.add))
                nc.vector.tensor_scalar(ss[:, t % 2, :], ss[:, t % 2, :], 1e-16, None, ALU.max).then_inc(ss_ready, 1)

            def invert(b, t):
                dve.wait_ge(root_ready, b * NT + (t + 1))
                nc.vector.reciprocal(inv[:, t % 2, :], root[:, t % 2, :]).then_inc(inv_ready, 1)

            def normalise(b, t):
                dve.wait_ge(rn_ready, b * NT + (t + 1))
                if t >= 2:
                    dve.wait_ge(kn_turned, b * NT + (t - 1))
                src = bank[:, 2 * (t % LAG):2 * (t % LAG) + 2, :].rearrange("p a (h e) -> p (a h) e", e=DH)
                nc.vector.tensor_tensor(kn[:, t % 2, :].rearrange("p (h e) -> p h e", e=DH), src,
                                        rn[:, t % 2, :].unsqueeze(2).to_broadcast([P, H, DH]), ALU.mult).then_inc(kn_ready, 1)

            def mask_and_max(b, p, e, first=False):
                head = p * 2 + e
                for n, (lo, hi, banks) in enumerate(((0, 1024, 2), (1024, 2048, 4), (2048, KEYS, 5))):
                    dve.wait_ge(sim_ready, b * (H * NG) + (head * NG + banks) + GIVEN)
                    if not first:
                        dve.wait_ge(p_turned, b * (H * NG) + ((p - 1) * (2 * NG) + (e * NG + banks)))
                    step(dve, passed)
                    src = bank[:, lo // BANK:(hi + BANK - 1) // BANK, :].rearrange("p a n -> p (a n)")[:, 0:hi - lo]
                    nc.vector.tensor_tensor_reduce(out=prob[:, e, lo:hi], in0=src, in1=pen[:, lo:hi], scale=1.0,
                                                   scalar=-3e38, op0=ALU.add, op1=ALU.max,
                                                   accum_out=mx[:, e, n:n + 1]).then_inc(masked, 1)
                dve.wait_ge(masked, b * (3 * H) + (head * 3 + 3))
                nc.vector.tensor_reduce(nmax[:, e:e + 1], mx[:, e, 0:3], AX.X, ALU.max, negate=True).then_inc(max_ready, 1)

            def invert_sums(b, p):
                dve.wait_ge(exp_ready, b * H + (p * 2 + 2))
                own.link(nc.vector.reciprocal(rsum[:], psumr[:]))

            def attend(b, p):
                dve.wait_ge(o_ready, b * PAIRS + (p + 1) + GIVEN)
                nc.vector.tensor_copy(o_T[:], bank[:, 7, 0:2 * P]).then_inc(oT_ready, 1)
                dve.wait_ge(v_ready, b * PAIRS + (p + 1))
                dst = att[:].rearrange("p (c e d) -> p c e d", e=2, d=DH)[:, bass.ds(p, 1), :, :].rearrange("p c e d -> p (c e) d")
                nc.vector.tensor_tensor(dst, bank[:, 7, 2 * P:3 * P].rearrange("p (e d) -> p e d", e=2),
                                        rsum[:].unsqueeze(2).to_broadcast([P, 2, DH]), ALU.mult).then_inc(att_ready, 1)
                dve.wait_ge(att_ready, b * PAIRS + (p + 1) + GIVEN)

            statistics(x_res, B)
            own.link(standardise(x_res, lat, B, 1))
            statistics(lat, B)
            standardise(lat, lat_n, B, 2).then_inc(latn_ready, 1)
            dve.wait_ge(latn_ready, 1)

            def affine():
                dve.wait_ge(affine_in, 16 * AFFINE_LOADS)
                own.link(nc.vector.tensor_tensor(lat[:], lat_n[:], rows[:, 2:3, :].to_broadcast([P, B, D]), ALU.mult))
                nc.vector.tensor_tensor(lat[:], lat[:], rows[:, 3:4, :].to_broadcast([P, B, D]), ALU.add).then_inc(lat_ready, 1)

            def measure(b):
                dve.wait_ge(ctx_in, b * 16 + 16)
                statistics(ctx_raw, CT)

            def prepare(b):
                standardise(ctx_raw, z, CT, b + 3, signal=z_ready)

            def penalise(b):
                dve.wait_ge(mask_in, b * 16 + 16)
                nc.vector.tensor_scalar(pen[:, 0:CTX].rearrange("a (t p) -> a t p", p=P), maskb[:].rearrange("a (p t) -> a t p", p=P),
                                        1.0, BIG, ALU.subtract, ALU.mult).then_inc(pen_ready, 1)

            def begin(b):
                reduce(b, 0)
                invert(b, 0)
                reduce(b, 1)
                normalise(b, 0)

            def attention(b, last):
                for t in range(NT + 1):
                    if t > 1:
                        invert(b, t - 1)
                    if 1 < t < NT:
                        reduce(b, t)
                    if t > 1:
                        normalise(b, t - 1)
                dve.wait_ge(pen_ready, b + 1)
                step(dve, passed)
                mask_and_max(b, 0, 0, first=True)
                mask_and_max(b, 0, 1, first=True)
                invert_sums(b, 0)
                mask_and_max(b, 1, 0)
                with dve.Fori(0, PAIRS - 2) as p:
                    own.enter(p, 1)
                    mask_and_max(b, p + 1, 1)
                    attend(b, p)
                    invert_sums(b, p + 1)
                    mask_and_max(b, p + 2, 0)
                    own.leave(PAIRS - 2)
                mask_and_max(b, PAIRS - 1, 1)
                if not last:
                    measure(b + 1)
                attend(b, PAIRS - 2)
                invert_sums(b, PAIRS - 1)
                if not last:
                    dve.wait_ge(xn_ready, b * KT + KT)
                    prepare(b + 1)
                    penalise(b + 1)
                xb = x_res[:, bass.ds(b, 1), :].rearrange("p a d -> p (a d)")
                own.link(nc.vector.tensor_tensor(xb, xb, rows[:, 4, :], ALU.add))
                attend(b, PAIRS - 1)
                if not last:
                    begin(b + 1)
                dve.wait_ge(y_ready, b + 1)
                nc.vector.tensor_tensor(xb, xb, bank[:, 7, 3 * P:4 * P], ALU.add).then_inc(x_ready, 1)

            measure(0)
            prepare(0)
            affine()
            penalise(0)
            dve.wait_ge(latT_turned, 1)
            dve.wait_ge(w_in, 16 * W_LOADS)
            begin(0)
            with dve.Fori(0, B - 1) as b:
                own.enter(b, NT + PAIRS + 1 + 2)
                attention(b, last=False)
                own.leave(B - 1)
            attention(B - 1, last=True)


def linear_attention(nc, io, g):
    NF = 4
    QR = 4
    W = 130
    GROUPS = [range(0, 3), range(3, 6), range(6, PAIRS)]
    with ExitStack() as ctx:
        s = Stage(nc, ctx, "la")
        w_q, w_k, w_v = (s.sb(n, [P, INNER]) for n in ("w_q", "w_k", "w_v"))
        w_o = s.sb("w_o", [P, PAIRS, D])
        w_1, w_2 = s.sb("w_1", [P, NF * P]), s.sb("w_2", [P, NF, D])
        row_k, row_v = s.sb("row_k", [P, INNER]), s.sb("row_v", [P, INNER])
        rows = s.sb("rows", [P, 6, D])
        col_q, col_1 = s.sb("col_q", [P, PAIRS]), s.sb("col_1", [P, NF])
        col_nq = s.sb("col_nq", [P, PAIRS])
        norm = Norm(s, B, g["mhalf"])
        src, src_T = s.sb("src", [P, B, D]), s.sb("src_T", [P, B * P])
        k_lin, k_neg, k_exp = (s.sb(n, [P, 2, INNER]) for n in ("k_lin", "k_neg", "k_exp"))
        k_phi = s.sb("k_phi", [P, B, INNER])
        v_one = s.sb("v_one", [P, B, PAIRS, P + 1])
        q_pos, q_neg, q_exp = (s.sb(n, [P, QR, B * P]) for n in ("q_pos", "q_neg", "q_exp"))
        q_phi = s.sb("q_phi", [P, PAIRS, B * P])
        kv = s.sb("kv", [P, 2, PAIRS, W])
        den, o_tok = s.sb("den", [P, H]), s.sb("o_tok", [P, INNER])
        o_T = s.sb("o_T", [P, PAIRS, P])
        warm = s.sb("warm", [P, 1])
        h, x1, x1_T = s.sb("h", [P, B, D]), s.sb("x1", [P, B, D]), s.sb("x1_T", [P, B * P])
        f_T = s.sb("f_T", [P, NF, B * P])
        bank = s.ps("bank", [P, 8, BANK])
        k_in, v_in, q_in, w_in, dve_own = (s.sem(n) for n in ("k_in", "v_in", "q_in", "w_in", "dve_own"))
        ones_ready, src_ready, src_turned, srcT_ready, kv_proj = (s.sem(n) for n in
            ("ones_ready", "src_ready", "src_turned", "srcT_ready", "kv_proj"))
        klin_ready, v_ready, kneg_ready, kexp_ready, kphi_ready = (s.sem(n) for n in
            ("klin_ready", "v_ready", "kneg_ready", "kexp_ready", "kphi_ready"))
        q_proj, qpos_ready, qexp_ready, qphi_ready = (s.sem(n) for n in ("q_proj", "qpos_ready", "qexp_ready", "qphi_ready"))
        kv_made, kv_ready, num_ready, o_ready, o_turned, oT_ready, wo_ready, h_ready = (s.sem(n) for n in
            ("kv_made", "kv_ready", "num_ready", "o_ready", "o_turned", "oT_ready", "wo_ready", "h_ready"))
        x1_ready, x1_turned, x1T_ready, f_proj, f_ready, y_ready = (s.sem(n) for n in
            ("x1_ready", "x1_turned", "x1T_ready", "f_proj", "f_ready", "y_ready"))
        x_res, ident = g["x_res"], g["ident"]
        block = ctx.enter_context(nc.Block())
        N_IN = 1 + 2 + 6 + 1

        @block.sync
        def _(sp):
            def load(dst, src, sem):
                sp.dma_start(dst, src).then_inc(sem, 16)

            load(w_k[:], io["L0_attn_Wk"], k_in)
            load(row_k[:], row(io["L0_attn_bk"]), k_in)
            load(w_v[:], io["L0_attn_Wv"], v_in)
            load(row_v[:], row(io["L0_attn_bv"]), v_in)
            load(w_q[:], io["L0_attn_Wq"], q_in)
            load(col_q[:], io["L0_attn_bq"], q_in)
            load(w_1[:], io["L0_attn_W1"], w_in)
            for w, n in ((w_o, "Wo"), (w_2, "W2")):
                load(w[:], io["L0_attn_" + n].rearrange("(c p) n -> p c n", p=P), w_in)
            for j, n in enumerate(("bo", "g1", "be1", "b2", "g2", "be2")):
                load(rows[:, j, :], row(io["L0_attn_" + n]), w_in)
            load(col_1[:], io["L0_attn_b1"], w_in)

        @block.gpsimd
        def _(pool):
            nc.gpsimd.memset(v_one[:, :, :, P:P + 1], 1.0)
            nc.gpsimd.memset(kv[:], 0.0).then_inc(ones_ready, 1)
            for n in range(3):
                norm.pool(pool, n + 1)
                if n == 0:
                    for p in range(PAIRS):
                        pool.wait_ge(qpos_ready, p + 1)
                        pool.wait_ge(qexp_ready, p + 1)
                        nc.gpsimd.tensor_tensor(q_phi[:, p, :], q_pos[:, p % QR, :], q_exp[:, p % QR, :], ALU.add).then_inc(qphi_ready, 1)

        @block.tensor
        def _(pe):
            pe.wait_ge(src_ready, 1)
            for b in range(B):
                mm = nc.tensor.transpose(bank[:, 0, b * P:(b + 1) * P], src[:, b, :], ident[:])
            mm.then_inc(src_turned, 1)
            pe.wait_ge(srcT_ready, 1)
            pe.wait_ge(k_in, 32)
            for b in range(B):
                if b >= 2:
                    pe.wait_ge(klin_ready, b - 1)
                    pe.wait_ge(v_ready, b - 1)
                for c, w in enumerate((w_k[:, 0:BANK], w_k[:, BANK:], w_v[:, 0:BANK], w_v[:, BANK:])):
                    if b == 0 and c == 2:
                        pe.wait_ge(v_in, 32)
                    nc.tensor.matmul(bank[:, 4 * (b % 2) + c, :], src_T[:, b * P:(b + 1) * P], w, start=True, stop=True).then_inc(kv_proj, 1)
            for p in range(PAIRS):
                if p == 0:
                    pe.wait_ge(q_in, 32)
                    pe.wait_ge(klin_ready, 3)
                    pe.wait_ge(v_ready, 3)
                if p == 4:
                    pe.wait_ge(klin_ready, 4)
                    pe.wait_ge(v_ready, 4)
                nc.tensor.matmul(bank[:, p, :], w_q[:, p * P:(p + 1) * P], src_T[:], start=True, stop=True).then_inc(q_proj, 1)

            def sum_up(b):
                pe.wait_ge(kphi_ready, b + 1)
                if b == 0:
                    pe.wait_ge(qpos_ready, 3)
                    pe.wait_ge(qexp_ready, 3)
                else:
                    pe.wait_ge(kv_ready, b)
                for n, pairs in enumerate(GROUPS):
                    for j, p in enumerate(pairs):
                        mm = nc.tensor.matmul(bank[:, n, j * (P + 1):(j + 1) * (P + 1)], k_phi[:, b, p * P:(p + 1) * P],
                                              v_one[:, b, p, :], start=True, stop=True)
                    mm.then_inc(kv_made, 1)

            def meet(b):
                pe.wait_ge(kv_ready, b + 1)
                if b == 0:
                    pe.wait_ge(qphi_ready, PAIRS)
                else:
                    pe.wait_ge(o_ready, b)
                for n, pairs in enumerate(GROUPS):
                    for j, p in enumerate(pairs):
                        mm = nc.tensor.matmul(bank[:, 3 + n, j * W:(j + 1) * W], q_phi[:, p, b * P:(b + 1) * P],
                                              kv[:, b % 2, p, :], start=True, stop=True)
                mm.then_inc(num_ready, 1)

            def turn_out(b):
                pe.wait_ge(o_ready, b + 1)
                if b >= 1:
                    pe.wait_ge(h_ready, b)
                for p in range(PAIRS):
                    mm = nc.tensor.transpose(bank[:, 6 + p // 4, (p % 4) * P:(p % 4 + 1) * P], o_tok[:, p * P:(p + 1) * P], ident[:])
                mm.then_inc(o_turned, 1)

            def project_out(b):
                pe.wait_ge(oT_ready, b + 1)
                for p in range(PAIRS):
                    mm = nc.tensor.matmul(bank[:, 6, 0:D], o_T[:, p, :], w_o[:, p, :], start=(p == 0), stop=(p == PAIRS - 1))
                mm.then_inc(wo_ready, 1)

            for i in range(B + 2):
                if i < B:
                    sum_up(i)
                if i == 2:
                    pe.wait_ge(w_in, 16 * N_IN)
                if i >= 2:
                    turn_out(i - 2)
                if 1 <= i <= B:
                    meet(i - 1)
                if i >= 2:
                    project_out(i - 2)
            pe.wait_ge(h_ready, B)
            pe.wait_ge(x1_ready, 1)
            for b in range(B):
                mm = nc.tensor.transpose(bank[:, 0, b * P:(b + 1) * P], x1[:, b, :], ident[:])
            mm.then_inc(x1_turned, 1)
            pe.wait_ge(x1T_ready, 1)
            for c in range(NF):
                nc.tensor.matmul(bank[:, 1 + c, :], w_1[:, c * P:(c + 1) * P], x1_T[:], start=True, stop=True).then_inc(f_proj, 1)
            pe.wait_ge(f_ready, NF)
            for b in range(B):
                for c in range(NF):
                    mm = nc.tensor.matmul(bank[:, 5, b * P:(b + 1) * P], f_T[:, c, b * P:(b + 1) * P], w_2[:, c, :],
                                          start=(c == 0), stop=(c == NF - 1))
            mm.then_inc(y_ready, 1)

        @block.scalar
        def _(act):
            act.wait_ge(src_turned, 1)
            nc.scalar.copy(src_T[:], bank[:, 0, :]).then_inc(srcT_ready, 1)
            def key_exp(b):
                act.wait_ge(klin_ready, b + 1)
                if b >= 2:
                    act.wait_ge(kphi_ready, b - 1)
                nc.scalar.activation(k_neg[:, b % 2, :], k_lin[:, b % 2, :], ACT.Relu, scale=-1.0).then_inc(kneg_ready, 1)
                act.wait_ge(kneg_ready, b + 1)
                nc.scalar.activation(k_exp[:, b % 2, :], k_neg[:, b % 2, :], ACT.Exp, scale=-1.0).then_inc(kexp_ready, 1)

            for b in range(B):
                key_exp(b)
            act.wait_ge(q_in, 32)
            nc.scalar.mul(col_nq[:], col_q[:], -1.0).then_inc(kneg_ready, 1)
            act.wait_ge(kneg_ready, B + 1)
            for p in range(PAIRS):
                act.wait_ge(q_proj, p + 1)
                if p >= QR:
                    act.wait_ge(qphi_ready, p - QR + 1)
                nc.scalar.activation(q_neg[:, p % QR, :], bank[:, p, :], ACT.Relu, bias=col_nq[:, p:p + 1], scale=-1.0).then_inc(kneg_ready, 1)
                act.wait_ge(kneg_ready, 1 + B + p + 1)
                nc.scalar.activation(q_exp[:, p % QR, :], q_neg[:, p % QR, :], ACT.Exp, scale=-1.0).then_inc(qexp_ready, 1)
            for b in range(B):
                act.wait_ge(o_turned, b + 1)
                if b >= 1:
                    act.wait_ge(wo_ready, b)
                nc.scalar.copy(o_T[:].rearrange("p c q -> p (c q)"), bank[:, 6:8, :].rearrange("p a n -> p (a n)")).then_inc(oT_ready, 1)
            nc.scalar.activation(warm[:], ident[:, 0:1], ACT.Gelu)
            act.wait_ge(x1_turned, 1)
            nc.scalar.copy(x1_T[:], bank[:, 0, :]).then_inc(x1T_ready, 1)
            for c in range(NF):
                act.wait_ge(f_proj, c + 1)
                nc.scalar.activation(f_T[:, c, :], bank[:, 1 + c, :], ACT.Gelu, bias=col_1[:, c:c + 1]).then_inc(f_ready, 1)

        @block.vector
        def _(dve):
            own = Chain(dve, dve_own)
            last = norm.vector(dve, own, x_res, src, 1)
            last.then_inc(src_ready, 1)
            dve.wait_ge(src_ready, 1)
            dve.wait_ge(k_in, 32)
            dve.wait_ge(v_in, 32)
            dve.wait_ge(q_in, 32)
            dve.wait_ge(ones_ready, 1)
            for b in range(B + 1):
                if b < B:
                    dve.wait_ge(kv_proj, 4 * b + 2)
                    if b >= 2:
                        dve.wait_ge(kphi_ready, b - 1)
                    kb = bank[:, 4 * (b % 2):4 * (b % 2) + 2, :].rearrange("p a n -> p (a n)")
                    nc.vector.tensor_tensor(k_lin[:, b % 2, :], kb, row_k[:], ALU.add).then_inc(klin_ready, 1)
                    dve.wait_ge(kv_proj, 4 * b + 4)
                    vb = bank[:, 4 * (b % 2) + 2:4 * (b % 2) + 4, :].rearrange("p a (c n) -> p (a c) n", n=P)
                    nc.vector.tensor_tensor(v_one[:, b, :, 0:P], vb, row_v[:].rearrange("p (c n) -> p c n", n=P), ALU.add).then_inc(v_ready, 1)
                if b >= 1:
                    dve.wait_ge(kexp_ready, b)
                    nc.vector.scalar_tensor_tensor(out=k_phi[:, b - 1, :], in0=k_lin[:, (b - 1) % 2, :], scalar=0.0,
                                                   in1=k_exp[:, (b - 1) % 2, :], op0=ALU.max, op1=ALU.add).then_inc(kphi_ready, 1)
            for p in range(PAIRS):
                dve.wait_ge(q_proj, p + 1)
                dve.wait_ge(qexp_ready, p + 1)
                if p >= QR:
                    dve.wait_ge(qphi_ready, p - QR + 1)
                nc.vector.tensor_scalar(q_pos[:, p % QR, :], bank[:, p, :], col_q[:, p:p + 1], 0.0, ALU.add, ALU.max).then_inc(qpos_ready, 1)

            def keep_sums(b):
                for n, pairs in enumerate(GROUPS):
                    dve.wait_ge(kv_made, 3 * b + n + 1)
                    m = len(pairs)
                    made = bank[:, n, 0:m * (P + 1)].rearrange("p (c n) -> p c n", n=P + 1)
                    for e in range(2):
                        half = slice(e * DH, (e + 1) * DH)
                        nc.vector.tensor_copy(kv[half, b % 2, pairs[0]:pairs[0] + m, half], made[half, :, half])
                        last = nc.vector.tensor_copy(kv[half, b % 2, pairs[0]:pairs[0] + m, P + e:P + e + 1], made[half, :, P:P + 1])
                last.then_inc(kv_ready, 1)

            def divide(b):
                dve.wait_ge(num_ready, b + 1)
                for n, pairs in enumerate(GROUPS):
                    m = len(pairs)
                    num = bank[:, 3 + n, 0:m * W].rearrange("p (c n) -> p c n", n=W)
                    last = nc.vector.tensor_scalar(den[:, 2 * pairs[0]:2 * (pairs[0] + m)].rearrange("p (c e) -> p c e", e=2),
                                                   num[:, :, P:P + 2], 1e-6, None, ALU.add)
                own.link(last)
                own.link(nc.vector.reciprocal(den[:], den[:]))
                if b >= 1:
                    dve.wait_ge(o_turned, b)
                for n, pairs in enumerate(GROUPS):
                    for e in range(2):
                        m = len(pairs)
                        num = bank[:, 3 + n, 0:m * W].rearrange("p (c n) -> p c n", n=W)[:, :, e * DH:(e + 1) * DH]
                        dst = o_tok[:].rearrange("p (c e d) -> p c e d", e=2, d=DH)[:, pairs[0]:pairs[0] + m, e, :]
                        by = den[:].rearrange("p (c e) -> p c e", e=2)[:, pairs[0]:pairs[0] + m, e:e + 1].to_broadcast([P, m, DH])
                        last = nc.vector.tensor_tensor(dst, num, by, ALU.mult)
                last.then_inc(o_ready, 1)

            for i in range(B + 2):
                if i < B:
                    keep_sums(i)
                if 1 <= i <= B:
                    divide(i - 1)
                if i == 2:
                    dve.wait_ge(w_in, 16 * N_IN)
                if i >= 2:
                    dve.wait_ge(wo_ready, i - 1)
                    nc.vector.tensor_tensor(h[:, i - 2, :], bank[:, 6, 0:D], src[:, i - 2, :], ALU.add).then_inc(h_ready, 1)
            dve.wait_ge(h_ready, B)

            def spread(j):
                return rows[:, j:j + 1, :].to_broadcast([P, B, D])

            own.link(nc.vector.tensor_tensor(h[:], h[:], spread(0), ALU.add))
            own.link(norm.vector(dve, own, h, x1, 2))
            own.link(nc.vector.tensor_tensor(x1[:], x1[:], spread(1), ALU.mult))
            nc.vector.tensor_tensor(x1[:], x1[:], spread(2), ALU.add).then_inc(x1_ready, 1)
            dve.wait_ge(x1_ready, 1)
            own.link(nc.vector.tensor_tensor(h[:], x1[:], spread(3), ALU.add))
            dve.wait_ge(y_ready, 1)
            own.link(nc.vector.tensor_tensor(h[:], h[:], bank[:, 5, :].rearrange("p (b d) -> p b d", b=B), ALU.add))
            own.link(norm.vector(dve, own, h, x1, 3))
            own.link(nc.vector.tensor_tensor(x1[:], x1[:], spread(4), ALU.mult))
            own.link(nc.vector.tensor_tensor(x1[:], x1[:], spread(5), ALU.add))
            own.link(nc.vector.tensor_tensor(x_res[:], x_res[:], x1[:], ALU.add))


def local_transformer(nc, io, g):
    LAYERS = 6
    TURNS = LAYERS // 2
    FF = int(D * 4 * 2 / 3)
    FT = (FF + P - 1) // P
    SIZE = [min(P, FF - c * P) for c in range(FT)]
    HALF = D // 2
    NU = 2 * B
    Y_BANK, XT_BANK = (0, 3, 6, 7), (1, 2, 4, 5)
    N_IN = 8
    HN = BANK // P
    NJ = H // HN
    UNITS = B * NJ
    TURN, GATHER, OUT = 4, 5, 6
    EARLY = ((0, B - 1), (B - 1, B))
    WO_BANK = (7,) * (B - 1) + (0,)
    RING, PRING = 2 * NJ, 4
    with ExitStack() as ctx:
        s = Stage(nc, ctx, "lt")
        w_qkv = s.sb("w_qkv", [P, 2, 3 * INNER])
        w_o = s.sb("w_o", [P, 2, PAIRS, D])
        w_1, w_2 = s.sb("w_1", [P, 2, 2 * FF]), s.sb("w_2", [P, 2, FT, D])
        cols = s.sb("cols", [P, 2, 8])
        gains = s.sb("gains", [P, 2, 4 * DH])
        row_2 = s.sb("row_2", [P, 2, D])
        tables, band, shift = s.sb("tables", [P, 4 * DH]), s.sb("band", [P, P]), s.sb("shift", [P, P])
        rot = s.sb("rot", [P, 4, DH])
        norm = Norm(s, B, g["mhalf"])
        warm = s.sb("warm", [P, 1])
        xc, xs = s.sb("xc", [P, B, D]), s.sb("xs", [P, B, D])
        xs_T = s.sb("xs_T", [P, B, P])
        xn_T = s.sb("xn_T", [P, B * P])
        sq, t1, t2, qk = (s.sb(n, [P, 2, INNER]) for n in ("sq", "t1", "t2", "qk"))
        ss, root, inv, rn = (s.sb(n, [P, B, 2, H]) for n in ("ss", "root", "inv", "rn"))
        err_k, err_q = s.sb("err_k", [P, H]), s.sb("err_q", [P, B, H])
        q_T = s.sb("q_T", [P, B, PAIRS, P])
        k_T = s.sb("k_T", [P, B, PAIRS, 2, P])
        v = s.sb("v", [P, B, INNER])
        prob = s.sb("prob", [P, RING, HN, P])
        mx, scale, bias, psumr, rsum = (s.sb(n, [P, B, H]) for n in ("mx", "scale", "bias", "psumr", "rsum"))
        p_T = s.sb("p_T", [P, PRING, HN, P])
        o_T = s.sb("o_T", [P, PAIRS, P])
        gate, f_T = s.sb("gate", [P, FT, B * P]), s.sb("f_T", [P, FT, B * P])
        bank = s.ps("bank", [P, 8, BANK])
        w_in = [s.sem("w_in0"), s.sem("w_in1")]
        (const_in, passed, dve_own, pool_own, x_ready, xT_turned, xsT_ready, proj_ready, sq_ready, ss_ready, inv_ready,
         rot_ready, roped, q_ready, sum_ready, k_ready, v_ready, qk_turned, qkT_ready) = (s.sem(n) for n in (
            "const_in", "passed", "dve_own", "pool_own", "x_ready", "xT_turned", "xsT_ready", "proj_ready", "sq_ready",
            "ss_ready", "inv_ready", "rot_ready", "roped", "q_ready", "sum_ready", "k_ready", "v_ready", "qk_turned", "qkT_ready"))
        root_ready, zeros_ready, summed, rsum_ready, weighed, found_max = (s.sem(n) for n in
            ("root_ready", "zeros_ready", "summed", "rsum_ready", "weighed", "found_max"))
        (scores_read, sim_ready, max_ready, exp_ready, p_turned, pT_ready, pv_ready, oT_ready, wo_ready, x1_ready,
         shifted, xn_ready, xn_turned, xnT_ready, f_proj, gate_ready, f_ready, y_ready) = (s.sem(n) for n in (
            "scores_read", "sim_ready", "max_ready", "exp_ready", "p_turned", "pT_ready", "pv_ready", "oT_ready",
            "wo_ready", "x1_ready", "shifted", "xn_ready", "xn_turned", "xnT_ready", "f_proj", "gate_ready", "f_ready", "y_ready"))
        x_res, ident = g["x_res"], g["ident"]
        block = ctx.enter_context(nc.Block())

        def at(turn, u, per, k):
            return turn * (2 * per) + (u * per + k)

        def heads(j):
            return j // NJ, slice(j % NJ * HN, (j % NJ + 1) * HN)

        @block.sync
        def _(sp):
            sp.dma_start(tables[:], io["rotary"]).then_inc(const_in, 16)
            sp.dma_start(band[:], io["band"]).then_inc(const_in, 16)
            sp.dma_start(shift[:], io["shift"]).then_inc(const_in, 16)

            def load(layer, u):
                def of(name):
                    return io["L0_ffn_" + name][layer].rearrange("a k n -> (a k) n")
                sp.dma_start(w_qkv[:, u, :], of("Wqkv")).then_inc(w_in[u], 16)
                sp.dma_start(gains[:, u, :], io["L0_ffn_gains"][layer].partition_broadcast(P).rearrange("p a n -> p (a n)")).then_inc(w_in[u], 16)
                sp.dma_start(cols[:, u, :], of("cols")).then_inc(w_in[u], 16)
                sp.dma_start(w_o[:, u, :, :], of("Wo").rearrange("(c p) n -> p c n", p=P)).then_inc(w_in[u], 16)
                sp.dma_start(w_1[:, u, :], of("W1")).then_inc(w_in[u], 16)
                sp.dma_start(w_2[:, u, 0:FT - 1, :], of("W2")[0:(FT - 1) * P, :].rearrange("(c p) n -> p c n", p=P)).then_inc(w_in[u], 16)
                sp.dma_start(w_2[0:SIZE[-1], u, FT - 1, :], of("W2")[(FT - 1) * P:FF, :]).then_inc(w_in[u], 16)
                sp.dma_start(row_2[:, u, :], io["L0_ffn_b2"][layer].partition_broadcast(P).rearrange("p a n -> p (a n)")).then_inc(w_in[u], 16)

            for u in range(2):
                load(slice(u, u + 1), u)
            with sp.Fori(0, TURNS - 1) as t:
                for u in range(2):
                    sp.wait_ge(x_ready, at(t, u, B, 2 * B))
                    step(sp, passed)
                    load(bass.ds(t * 2 + (2 + u), 1), u)

        @block.gpsimd
        def _(pool):
            own = Chain(pool, pool_own)
            nc.gpsimd.memset(k_T[:], 0.0).then_inc(zeros_ready, 1)
            own.link(nc.gpsimd.memset(xs_T[:], 0.0))
            norm.pool(pool, 1)
            pool.wait_ge(const_in, 48)
            with pool.Fori(0, TURNS) as t:
                own.enter(t, 2 * 4 * B)
                for u in range(2):
                    pool.wait_ge(w_in[u], t * (16 * N_IN) + 16 * N_IN)
                    pool.wait_ge(x_ready, at(t, u, B, B))
                    nc.gpsimd.tensor_tensor(rot[:].rearrange("p a e -> p (a e)"), tables[:], gains[:, u, :], ALU.mult).then_inc(rot_ready, 1)
                    for m in range(NU):
                        b, kind = m // 2, m % 2
                        if kind == 1:
                            pool.wait_ge(inv_ready, at(t, u, B, b + 1))
                            own.link(nc.gpsimd.tensor_tensor(err_k[:], inv[:, b, 1, :], inv[:, b, 1, :], ALU.mult))
                            own.link(nc.gpsimd.tensor_tensor(err_k[:], err_k[:], ss[:, b, 1, :], ALU.mult))
                            step(pool, passed)
                            own.link(nc.gpsimd.tensor_scalar(err_k[:], err_k[:], -0.5, 1.5, ALU.mult, ALU.add))
                            own.link(nc.gpsimd.tensor_tensor(rn[:, b, 1, :], inv[:, b, 1, :], err_k[:], ALU.mult))
                        pool.wait_ge(roped, at(t, u, NU, m + 1))
                        if m >= 2:
                            pool.wait_ge(qk_turned, at(t, u, NU, m - 1))
                        nc.gpsimd.tensor_tensor(qk[:, kind, :], t1[:, kind, :], t2[:, kind, :], ALU.add).then_inc(sum_ready, 1)
                        if kind == 1:
                            x = qk[:, 1, :].rearrange("p (h e) -> p h e", e=DH)
                            pool.wait_ge(sum_ready, at(t, u, NU, m + 1))
                            nc.gpsimd.tensor_tensor(x, x, rn[:, b, 1, :].unsqueeze(2).to_broadcast([P, H, DH]), ALU.mult).then_inc(k_ready, 1)
                    for j in range(UNITS):
                        pool.wait_ge(rsum_ready, at(t, u, UNITS, j + 1))
                        b, hs = heads(j)
                        x = prob[:, j % RING, :, :]
                        nc.gpsimd.tensor_tensor(x, x, rsum[:, b, hs].unsqueeze(2).to_broadcast([P, HN, P]), ALU.mult).then_inc(weighed, 1)
                    for k, part in enumerate(EARLY):
                        norm.pool(pool, at(t, u, 2, 2 + k), part)
                own.leave(TURNS)

        @block.tensor
        def _(pe):
            pe.wait_ge(const_in, 48)
            pe.wait_ge(zeros_ready, 1)

            def layer(t, u):
                def wait(sem, per, k):
                    pe.wait_ge(sem, at(t, u, per, k))

                for b in range(B):
                    wait(x_ready, B, b + 1)
                    nc.tensor.transpose(bank[:, XT_BANK[b], 0:P], xc[:, b, :], ident[:]).then_inc(xT_turned, 1)
                pe.wait_ge(w_in[u], t * (16 * N_IN) + 16 * N_IN)

                def turn(m):
                    if m % 2 == 0:
                        wait(sum_ready, NU, m + 1)
                    else:
                        wait(k_ready, B, m // 2 + 1)
                    if m >= 1:
                        wait(qkT_ready, NU, m)
                    for p in range(PAIRS):
                        mm = nc.tensor.transpose(bank[:, 6 + p // 4, (p % 4) * P:(p % 4 + 1) * P],
                                                 qk[:, m % 2, p * P:(p + 1) * P], ident[:])
                    mm.then_inc(qk_turned, 1)

                def project(b, kind):
                    if b >= 1 and kind < 2:
                        wait(roped, NU, 2 * (b - 1) + kind + 1)
                    elif b >= 1:
                        wait(v_ready, B, b)
                    else:
                        wait(xsT_ready, 2 * B, 2 * (1, 2, B)[kind])
                    for c in range(2):
                        mm = nc.tensor.matmul(bank[:, 2 * kind + c, :], xs_T[:, b, :],
                                              w_qkv[:, u, kind * INNER + c * BANK:kind * INNER + (c + 1) * BANK],
                                              start=True, stop=True)
                    mm.then_inc(proj_ready, 1)

                for b in range(B):
                    project(b, 0)
                    if b >= 2:
                        turn(2 * b - 3)
                    project(b, 1)
                    if b >= 1:
                        turn(2 * b - 2)
                    project(b, 2)
                turn(NU - 3)

                def score(j):
                    b, n = j // NJ, j % NJ
                    if n == 0:
                        wait(qkT_ready, NU, 2 * b + 2)
                    if b >= 1:
                        wait(scores_read, UNITS, j - NJ + 1)
                    else:
                        wait(roped, NU, NU - 1 + n // 2)
                    for p in (2 * n, 2 * n + 1):
                        mm = nc.tensor.matmul(bank[:, n, (p % 2) * 2 * P:(p % 2 + 1) * 2 * P], q_T[:, b, p, :],
                                              k_T[:, b, p, :, :].rearrange("p e n -> p (e n)"), start=True, stop=True)
                    mm.then_inc(sim_ready, 1)

                def turn_prob(j):
                    wait(weighed, UNITS, j + 1)
                    if j >= 2:
                        wait(pT_ready, UNITS, j - 1)
                    else:
                        wait(v_ready, B, B)
                    for i in range(HN):
                        mm = nc.tensor.transpose(bank[:, 4 + j % 2, i * P:(i + 1) * P], prob[:, j % RING, i, :], ident[:])
                    mm.then_inc(p_turned, 1)

                def gather(j):
                    b, n = j // NJ, j % NJ
                    wait(pT_ready, UNITS, j + 1)
                    if b == 0 and n == 0:
                        wait(qkT_ready, NU, NU)
                    elif n == 0:
                        wait(oT_ready, 2 * B, 2 * b - 1)
                    elif b >= 1 and n == NJ // 2:
                        wait(x1_ready, B, b)
                    for i in range(HN):
                        h = n * HN + i
                        mm = nc.tensor.matmul(bank[(h % 2) * DH:(h % 2 + 1) * DH, 6 + h // 8, (h // 2 % 4) * P:(h // 2 % 4 + 1) * P],
                                              v[:, b, h * DH:(h + 1) * DH], p_T[:, j % PRING, i, :], start=True, stop=True)
                    mm.then_inc(pv_ready, 1)

                def project_out(b):
                    if b < B - 1:
                        wait(oT_ready, 2 * B, 2 * b + 2)
                    else:
                        wait(oT_ready, 2 * B, 2 * b + 1)
                    for p in range(PAIRS):
                        if b == B - 1 and p == PAIRS // 2:
                            wait(oT_ready, 2 * B, 2 * b + 2)
                        mm = nc.tensor.matmul(bank[:, WO_BANK[b], 0:D], o_T[:, p, :], w_o[:, u, p, :], start=(p == 0), stop=(p == PAIRS - 1))
                    mm.then_inc(wo_ready, 1)

                score(0)
                score(1)
                turn(NU - 2)
                score(2)
                score(3)
                turn(NU - 1)
                def shift_right(k):
                    first, end = EARLY[k]
                    wait(x1_ready, B, end)
                    nc.tensor.matmul(bank[:, 1 + k, 0:(end - first) * HALF], shift[:], xc[:, first:end, HALF:D],
                                     start=True, stop=True).then_inc(shifted, 1)

                def turn_norm(k):
                    wait(xn_ready, 2, k + 1)
                    for b in range(*EARLY[k]):
                        mm = nc.tensor.transpose(bank[:, 3 - k, b * P:(b + 1) * P], xs[:, b, :], ident[:])
                    mm.then_inc(xn_turned, 1)

                for j in range(TURN, UNITS + OUT - 1):
                    if j < UNITS:
                        score(j)
                    if TURN <= j < UNITS + TURN:
                        turn_prob(j - TURN)
                    if GATHER <= j < UNITS + GATHER:
                        gather(j - GATHER)
                    if j - OUT >= 0 and (j - OUT) % NJ == NJ - 1:
                        project_out((j - OUT) // NJ)
                    if j == UNITS + TURN - 1:
                        wait(scores_read, UNITS, UNITS)
                        shift_right(0)
                project_out(B - 1)
                turn_norm(0)
                shift_right(1)
                turn_norm(1)
                wait(xnT_ready, 2, 2)
                for c in range(FT):
                    for side in range(2):
                        first = (1 - side) * FF + c * P
                        nc.tensor.matmul(bank[0:SIZE[c], 3 * side + c, :], w_1[:, u, first:first + SIZE[c]],
                                         xn_T[:], start=True, stop=True).then_inc(f_proj, 1)
                for c in range(FT):
                    wait(f_ready, FT, c + 1)
                    for b in range(B):
                        mm = nc.tensor.matmul(bank[:, Y_BANK[b], 0:D], f_T[0:SIZE[c], c, b * P:(b + 1) * P],
                                              w_2[0:SIZE[c], u, c, :], start=(c == 0), stop=(c == FT - 1))
                        if c == FT - 1:
                            mm.then_inc(y_ready, 1)

            with pe.Fori(0, TURNS) as t:
                for u in range(2):
                    layer(t, u)

        @block.scalar
        def _(act):
            def preload(function):
                nc.scalar.activation(warm[:], ident[:, 0:1], function)

            def layer(t, u):
                def wait(sem, per, k):
                    act.wait_ge(sem, at(t, u, per, k))

                for b in range(B):
                    wait(xT_turned, B, b + 1)
                    src = bank[:, XT_BANK[b], 0:P]
                    nc.scalar.copy(xs_T[0:HALF, b, :], src[0:HALF]).then_inc(xsT_ready, 1)
                    nc.scalar.copy(xs_T[HALF:P, b, 1:P], src[HALF:P, 0:P - 1]).then_inc(xsT_ready, 1)

                def square(m):
                    b, kind = m // 2, m % 2
                    wait(proj_ready, 3 * B, 3 * b + kind + 1)
                    if m >= 2:
                        wait(ss_ready, NU, m - 1)
                    nc.scalar.activation(sq[:, m % 2, :], bank[:, 2 * kind:2 * kind + 2, :].rearrange("p a n -> p (a n)"),
                                         ACT.Square).then_inc(sq_ready, 1)

                def square_root(m):
                    wait(ss_ready, NU, m + 1)
                    nc.scalar.activation(root[:, m // 2, m % 2, :], ss[:, m // 2, m % 2, :], ACT.Sqrt).then_inc(root_ready, 1)

                def keep_turned(m):
                    wait(qk_turned, NU, m + 1)
                    if m % 2 == 0:
                        nc.scalar.copy(q_T[:, m // 2, :, :].rearrange("p c n -> p (c n)"),
                                       bank[:, 6:8, :].rearrange("p a n -> p (a n)")).then_inc(qkT_ready, 1)
                    else:
                        for e in range(2):
                            half = slice(e * DH, (e + 1) * DH)
                            last = nc.scalar.copy(k_T[half, m // 2, :, e, :], bank[half, 6:8, :].rearrange("p a (c n) -> p (a c) n", n=P))
                        last.then_inc(qkT_ready, 1)

                for b in range(B):
                    square(2 * b)
                    if b >= 2:
                        keep_turned(2 * b - 3)
                    square_root(2 * b)
                    square(2 * b + 1)
                    if b >= 1:
                        keep_turned(2 * b - 2)
                    wait(proj_ready, 3 * B, 3 * b + 3)
                    nc.scalar.copy(v[:, b, :], bank[:, 4:6, :].rearrange("p a n -> p (a n)")).then_inc(v_ready, 1)
                    square_root(2 * b + 1)
                preload(ACT.Exp)
                keep_turned(NU - 3)
                keep_turned(NU - 2)

                def exponent(j):
                    wait(max_ready, UNITS, j + 1)
                    b, hs = heads(j)
                    for i, h in enumerate(range(hs.start, hs.stop)):
                        last = nc.scalar.activation(prob[:, j % RING, i, :], prob[:, j % RING, i, :], ACT.Exp, bias=bias[:, b, h:h + 1],
                                                    scale=scale[:, b, h:h + 1])
                    last.then_inc(exp_ready, 1)

                def keep_prob(j):
                    wait(p_turned, UNITS, j + 1)
                    if j >= PRING:
                        wait(pv_ready, UNITS, j - PRING + 1)
                    nc.scalar.copy(p_T[:, j % PRING, :, :].rearrange("p h q -> p (h q)"), bank[:, 4 + j % 2, :]).then_inc(pT_ready, 1)

                def keep_out(b, half):
                    wait(pv_ready, UNITS, b * NJ + (half + 1) * NJ // 2)
                    if b >= 1:
                        wait(wo_ready, B, b)
                    nc.scalar.copy(o_T[:, half * 4:(half + 1) * 4, :].rearrange("p c q -> p (c q)"), bank[:, 6 + half, :]).then_inc(oT_ready, 1)

                for j in range(1, UNITS + OUT):
                    if TURN <= j < UNITS + TURN:
                        keep_prob(j - TURN)
                    if j - OUT >= 0 and (j - OUT) % 2 == 1:
                        keep_out((j - OUT) // NJ, (j - OUT) % NJ // 2)
                    if j <= UNITS:
                        exponent(j - 1)
                    if j == 2:
                        keep_turned(NU - 1)
                    if j == UNITS + 2:
                        preload(ACT.Gelu)
                for k, (first, end) in enumerate(EARLY):
                    wait(xn_turned, 2, k + 1)
                    nc.scalar.activation(xn_T[:, first * P:end * P], bank[:, 3 - k, first * P:end * P], ACT.Identity, bias=cols[:, u, 1:2],
                                         scale=cols[:, u, 0:1]).then_inc(xnT_ready, 1)
                for c in range(FT):
                    wait(f_proj, 2 * FT, 2 * c + 1)
                    n = SIZE[c]
                    nc.scalar.activation(gate[0:n, c, :], bank[0:n, c, :], ACT.Gelu, bias=cols[0:n, u, 5 + c:6 + c]).then_inc(gate_ready, 1)
                preload(ACT.Sqrt)

            with act.Fori(0, TURNS) as t:
                for u in range(2):
                    layer(t, u)

        @block.vector
        def _(dve):
            own = Chain(dve, dve_own)
            norm.vector(dve, own, x_res, xc, 1).then_inc(x_ready, B)

            def layer(t, u):
                def wait(sem, per, k):
                    dve.wait_ge(sem, at(t, u, per, k))

                wait(rot_ready, 1, 1)

                def rope(m):
                    b, kind = m // 2, m % 2
                    src = bank[:, 2 * kind:2 * kind + 2, :].rearrange("p a (h e) -> p (a h) e", e=DH)
                    wait(sq_ready, NU, m + 1)
                    own.link(nc.vector.tensor_reduce(ss[:, m // 2, m % 2, :], sq[:, m % 2, :].rearrange("p (h e) -> p h e", e=DH), AX.X, ALU.add))
                    nc.vector.tensor_scalar(ss[:, m // 2, m % 2, :], ss[:, m // 2, m % 2, :], 1e-24, None, ALU.max).then_inc(ss_ready, 1)
                    if m >= 2:
                        wait(sum_ready, NU, m - 1)
                    o1, o2 = (x[:, m % 2, :].rearrange("p (h e) -> p h e", e=DH) for x in (t1, t2))
                    by1 = rot[:, 2 * kind:2 * kind + 1, :].to_broadcast([P, H, DH])
                    nc.vector.tensor_tensor(o1, src, by1, ALU.mult)
                    if kind == 1:
                        wait(root_ready, NU, m + 1)
                        nc.vector.reciprocal(inv[:, b, 1, :], root[:, b, 1, :]).then_inc(inv_ready, 1)
                    r = DH // 2
                    nc.vector.tensor_tensor(o2[:, :, 0:r], src[:, :, r:DH], rot[:, 2 * kind + 1:2 * kind + 2, 0:r].to_broadcast([P, H, r]), ALU.mult)
                    nc.vector.tensor_tensor(o2[:, :, r:DH], src[:, :, 0:r], rot[:, 2 * kind + 1:2 * kind + 2, r:DH].to_broadcast([P, H, r]),
                                            ALU.mult).then_inc(roped, 1)

                for m in range(NU):
                    rope(m)

                wait(root_ready, NU, NU)
                y, q_ss = inv[:, :, 0, :], ss[:, :, 0, :]
                own.link(nc.vector.reciprocal(y, root[:, :, 0, :]))
                own.link(nc.vector.tensor_tensor(err_q[:], y, y, ALU.mult))
                own.link(nc.vector.tensor_tensor(err_q[:], err_q[:], q_ss, ALU.mult))
                own.link(nc.vector.tensor_scalar(err_q[:], err_q[:], -4.0, 12.0, ALU.mult, ALU.add))
                own.link(nc.vector.tensor_tensor(scale[:], y, err_q[:], ALU.mult))

                def mask(j):
                    wait(sim_ready, UNITS, j + 1)
                    if j >= RING:
                        wait(p_turned, UNITS, j - RING + 1)
                    nc.vector.tensor_tensor(prob[:, j % RING, :, :], bank[:, j % NJ, :].rearrange("p (h j) -> p h j", h=HN),
                                            band[:].unsqueeze(1).to_broadcast([P, HN, P]), ALU.add).then_inc(scores_read, 1)

                def maximum(j):
                    b, hs = heads(j)
                    wait(scores_read, UNITS, j + 1)
                    nc.vector.tensor_reduce(mx[:, b, hs], prob[:, j % RING, :, :], AX.X, ALU.max).then_inc(found_max, 1)
                    wait(found_max, UNITS, j + 1)
                    nc.vector.scalar_tensor_tensor(out=bias[:, b, hs], in0=mx[:, b, hs], scalar=-1.0, in1=scale[:, b, hs],
                                                   op0=ALU.mult, op1=ALU.mult).then_inc(max_ready, 1)

                def sum_up(j):
                    b, hs = heads(j)
                    wait(exp_ready, UNITS, j + 1)
                    nc.vector.tensor_reduce(psumr[:, b, hs], prob[:, j % RING, :, :], AX.X, ALU.add).then_inc(summed, 1)

                def invert(j):
                    b, hs = heads(j)
                    wait(summed, UNITS, j + 1)
                    nc.vector.reciprocal(rsum[:, b, hs], psumr[:, b, hs]).then_inc(rsum_ready, 1)

                def residual(b):
                    wait(wo_ready, B, b + 1)
                    nc.vector.tensor_tensor(xc[:, b, :], xc[:, b, :], bank[:, WO_BANK[b], 0:D], ALU.add).then_inc(x1_ready, 1)

                for j in range(UNITS + 3):
                    if 2 <= j < UNITS + 2:
                        sum_up(j - 2)
                    if j < UNITS:
                        mask(j)
                    if 2 <= j < UNITS + 2:
                        invert(j - 2)
                    if j < UNITS:
                        maximum(j)
                    if j - OUT - 1 >= 0 and (j - OUT - 1) % NJ == NJ - 1:
                        residual((j - OUT - 1) // NJ)

                def shift_norm(k):
                    first, end = EARLY[k]
                    wait(x1_ready, B, end)
                    nc.vector.tensor_copy(xs[:, first:end, 0:HALF], xc[:, first:end, 0:HALF])
                    wait(shifted, 2, k + 1)
                    own.link(nc.vector.tensor_copy(xs[:, first:end, HALF:D],
                                                   bank[:, 1 + k, 0:(end - first) * HALF].rearrange("p (b n) -> p b n", n=HALF)))
                    norm.vector(dve, own, xs, xs, at(t, u, 2, 2 + k), passed, EARLY[k]).then_inc(xn_ready, 1)

                shift_norm(0)
                residual(B - 1)
                shift_norm(1)
                own.link(nc.vector.tensor_tensor(xc[:], xc[:], row_2[:, u:u + 1, :].to_broadcast([P, B, D]), ALU.add))
                for c in range(FT):
                    wait(f_proj, 2 * FT, 2 * c + 2)
                    wait(gate_ready, FT, c + 1)
                    n = SIZE[c]
                    nc.vector.scalar_tensor_tensor(out=f_T[0:n, c, :], in0=bank[0:n, 3 + c, :], scalar=cols[0:n, u, 2 + c:3 + c],
                                                   in1=gate[0:n, c, :], op0=ALU.add, op1=ALU.mult).then_inc(f_ready, 1)
                for b in range(B):
                    wait(y_ready, B, b + 1)
                    nc.vector.tensor_tensor(xc[:, b, :], xc[:, b, :], bank[:, Y_BANK[b], 0:D], ALU.add).then_inc(x_ready, 1)

            with dve.Fori(0, TURNS) as t:
                per = 2 * (NU + 5 + 3 * len(EARLY) + 1)
                own.enter(t, per)
                for u in range(2):
                    layer(t, u)
                own.leave(TURNS)
            dve.wait_ge(x_ready, (LAYERS + 1) * B)
            nc.vector.tensor_tensor(x_res[:], x_res[:], xc[:], ALU.add)


def two_way_attention(nc, io, g):
    CK = CTX // BANK
    LEFT = CT // 2 - 1
    SCALE = D ** -0.5
    with ExitStack() as ctx:
        s = Stage(nc, ctx, "ta")
        names = ("Wq_c", "Wk_s", "Wv_s", "Wq_s", "Wk_c", "Wv_c")
        w = {n: s.sb("w_" + n, [P, D]) for n in names}
        w_g = s.sb("w_g", [P, 2, D])
        cols = s.sb("cols", [P, 4])
        rows = s.sb("rows", [P, 3, D])
        norm = Norm(s, B, g["mhalf"])
        char, char_T, qc_T, kc_T = (s.sb(n, [P, B, D]) for n in ("char", "char_T", "qc_T", "kc_T"))
        vc = s.sb("vc", [P, B, D])
        ctx_raw, ctx_T, k_T = s.sb("ctx_raw", [P, B, CT, D]), s.sb("ctx_T", [P, CTX]), s.sb("k_T", [P, 2, CTX])
        qs_T = s.sb("qs_T", [P, B, 2, P])
        prob, p_T = s.sb("prob", [P, 2, CTX]), s.sb("p_T", [P, CT, P])
        top, bias, psumr, rsum = (s.sb(n, [P, B]) for n in ("top", "bias", "psumr", "rsum"))
        prob2, p2_T = s.sb("prob2", [P, B, 2, P]), s.sb("p2_T", [P, B, 2, P])
        top2, sum2, inv2 = (s.sb(n, [P, B, 2]) for n in ("top2", "sum2", "inv2"))
        half_out = s.sb("half_out", [P, B, 2, D])
        c_T, both, both_T = s.sb("c_T", [P, B, P]), s.sb("both", [P, B, 2, D]), s.sb("both_T", [P, B, 2, P])
        u, diff = s.sb("u", [P, B, D]), s.sb("diff", [P, B, D])
        bank = s.ps("bank", [P, 8, BANK])
        (w_in, dve_own, char_ready, char_turned, charT_ready, cproj, cproj_kept, ctx_turned, ctxT_ready, k_proj, kT_ready,
         sc_ready, found_top, max_ready, exp_ready, p_turned, pT_ready, c_ready, cT_ready) = (s.sem(n) for n in (
            "w_in", "dve_own", "char_ready", "char_turned", "charT_ready", "cproj", "cproj_kept", "ctx_turned", "ctxT_ready",
            "k_proj", "kT_ready", "sc_ready", "found_top", "max_ready", "exp_ready", "p_turned", "pT_ready", "c_ready", "cT_ready"))
        (s2_ready, sub2_ready, exp2_ready, p2_turned, p2T_ready, o2_ready, c2s_raw, both_ready, both_turned, bothT_ready, g_ready,
         u_ready, e_ready) = (s.sem(n) for n in (
            "s2_ready", "sub2_ready", "exp2_ready", "p2_turned", "p2T_ready", "o2_ready", "c2s_raw", "both_ready", "both_turned",
            "bothT_ready", "g_ready", "u_ready", "e_ready"))
        ctx_in = [s.sem(f"ctx_in{b}") for b in range(B)]
        x_res, ident = g["x_res"], g["ident"]
        block = ctx.enter_context(nc.Block())
        N_IN = 6 + 1 + 4 + 3

        @block.sync
        def _(sp):
            for n in names:
                sp.dma_start(w[n][:], io["L1_xattn_" + n]).then_inc(w_in, 16)
            for j, n in enumerate(("bq_c", "bk_s", "bq_s", "bk_c")):
                sp.dma_start(cols[:, j:j + 1], columns(io["L1_xattn_" + n], 1)).then_inc(w_in, 16)
            for j, n in enumerate(("bv_s", "bv_c", "bg")):
                sp.dma_start(rows[:, j, :], row(io["L1_xattn_" + n])).then_inc(w_in, 16)
            sp.dma_start(w_g[:], io["L1_xattn_Wg"].rearrange("(c p) n -> p c n", p=P)).then_inc(w_in, 16)
            for b in range(1, B):
                sp.dma_start(ctx_raw[:, b, :, :], io["ctx_1024"][b].rearrange("(p t) d -> p t d", p=P)).then_inc(ctx_in[b], 16)

        @block.gpsimd
        def _(pool):
            norm.pool(pool, 1)

        @block.tensor
        def _(pe):
            def prepare(b):
                pe.wait_ge(ctx_in[b], 16)
                for c in range(CK):
                    n = CK * b + c
                    if n >= 2:
                        pe.wait_ge(ctxT_ready, n - 1)
                    if c < 2 and b >= 2:
                        pe.wait_ge(pT_ready, CK * (b - 1))
                    for j in range(4):
                        mm = nc.tensor.transpose(bank[:, c % 2, j * P:(j + 1) * P], ctx_raw[:, b, 4 * c + j, :], ident[:])
                    mm.then_inc(ctx_turned, 1)
                for c in range(CK + 1):
                    n = (CK + 1) * b + c
                    if n >= 2:
                        pe.wait_ge(kT_ready, n - 1)
                    if c == 0 and b >= 2:
                        pe.wait_ge(cT_ready, b - 1)
                    if c < CK:
                        pe.wait_ge(ctxT_ready, CK * b + c + 1)
                        nc.tensor.matmul(bank[:, 2 + n % 2, :], w["Wk_s"][:], ctx_T[:, c * BANK:(c + 1) * BANK],
                                         start=True, stop=True).then_inc(k_proj, 1)
                    else:
                        nc.tensor.matmul(bank[:, 2 + n % 2, 0:2 * P], w["Wq_s"][:], ctx_T[:, LEFT * P:(LEFT + 2) * P],
                                         start=True, stop=True).then_inc(k_proj, 1)

            def score(b):
                if b == 0:
                    pe.wait_ge(cproj_kept, 3)
                else:
                    pe.wait_ge(exp_ready, b)
                for c in range(CK):
                    pe.wait_ge(kT_ready, (CK + 1) * b + c + 1)
                    mm = nc.tensor.matmul(bank[:, 4 + c, :], qc_T[:, b, :], k_T[:, b % 2, c * BANK:(c + 1) * BANK], start=True, stop=True)
                mm.then_inc(sc_ready, 1)

            def gather(b):
                pe.wait_ge(exp_ready, b + 1)
                for c in range(CK):
                    if CK * b + c >= 2 and not (c < 2 and b + 1 < B):
                        pe.wait_ge(pT_ready, CK * b + c - 1)
                    if c < 2 and b + 1 < B:
                        pe.wait_ge(ctxT_ready, CK * (b + 2))
                        if b >= 1:
                            pe.wait_ge(pT_ready, CK * b + c - 1)
                    for j in range(4):
                        mm = nc.tensor.transpose(bank[:, c % 2, j * P:(j + 1) * P], prob[:, b % 2, (4 * c + j) * P:(4 * c + j + 1) * P], ident[:])
                    mm.then_inc(p_turned, 1)
                pe.wait_ge(kT_ready, (CK + 1) * min(b + 2, B))
                for t in range(CT):
                    if t % 4 == 0:
                        pe.wait_ge(pT_ready, CK * b + t // 4 + 1)
                    mm = nc.tensor.matmul(bank[:, 2, 0:P], ctx_raw[:, b, t, :], p_T[:, t, :], start=(t == 0), stop=(t == CT - 1))
                mm.then_inc(c_ready, 1)

            pe.wait_ge(char_ready, 1)
            for b in range(B):
                mm = nc.tensor.transpose(bank[:, 4, b * P:(b + 1) * P], char[:, b, :], ident[:])
            mm.then_inc(char_turned, 1)
            pe.wait_ge(charT_ready, 1)
            pe.wait_ge(w_in, 16 * N_IN)
            rhs = char_T[:].rearrange("p b n -> p (b n)")
            nc.tensor.matmul(bank[:, 5, :], w["Wq_c"][:], rhs, start=True, stop=True).then_inc(cproj, 1)
            nc.tensor.matmul(bank[:, 6, :], w["Wk_c"][:], rhs, start=True, stop=True).then_inc(cproj, 1)
            for b in range(B):
                mm = nc.tensor.matmul(bank[:, 7, b * P:(b + 1) * P], char_T[:, b, :], w["Wv_c"][:], start=True, stop=True)
            mm.then_inc(cproj, 1)
            prepare(0)
            score(0)
            for b in range(B - 1):
                prepare(b + 1)
                score(b + 1)
                gather(b)
            pe.wait_ge(exp_ready, B)
            for b in range(B):
                for e in range(2):
                    mm = nc.tensor.matmul(bank[:, 4 + b // 2, (b % 2 * 2 + e) * P:(b % 2 * 2 + e + 1) * P], qs_T[:, b, e, :], kc_T[:, b, :],
                                          start=True, stop=True)
            mm.then_inc(s2_ready, 1)
            pe.wait_ge(cT_ready, B - 1)
            gather(B - 1)
            pe.wait_ge(exp2_ready, 1)
            for b in range(B):
                for e in range(2):
                    mm = nc.tensor.transpose(bank[:, 6 + b // 2, (b % 2 * 2 + e) * P:(b % 2 * 2 + e + 1) * P], prob2[:, b, e, :], ident[:])
            mm.then_inc(p2_turned, 1)
            pe.wait_ge(cT_ready, B)
            for b in range(B):
                mm = nc.tensor.matmul(bank[:, 3, b * P:(b + 1) * P], c_T[:, b, :], w["Wv_s"][:], start=True, stop=True)
            mm.then_inc(c2s_raw, 1)
            pe.wait_ge(p2T_ready, 1)
            for b in range(B):
                for e in range(2):
                    mm = nc.tensor.matmul(bank[:, b // 2, (b % 2 * 2 + e) * P:(b % 2 * 2 + e + 1) * P], p2_T[:, b, e, :], vc[:, b, :],
                                          start=True, stop=True)
            mm.then_inc(o2_ready, 1)
            for e in range(2):
                pe.wait_ge(both_ready, e + 1)
                for b in range(B):
                    mm = nc.tensor.transpose(bank[:, 4 + e, b * P:(b + 1) * P], both[:, b, e, :], ident[:])
                mm.then_inc(both_turned, 1)
            pe.wait_ge(bothT_ready, 2)
            for b in range(B):
                for e in range(2):
                    mm = nc.tensor.matmul(bank[:, 6, b * P:(b + 1) * P], both_T[:, b, e, :], w_g[:, e, :], start=(e == 0), stop=(e == 1))
            mm.then_inc(g_ready, 1)

        @block.scalar
        def _(act):
            def keep_keys(b):
                for c in range(CK + 1):
                    n = (CK + 1) * b + c
                    act.wait_ge(k_proj, n + 1)
                    if c < CK:
                        nc.scalar.activation(k_T[:, b % 2, c * BANK:(c + 1) * BANK], bank[:, 2 + n % 2, :], ACT.Identity,
                                             bias=cols[:, 1:2]).then_inc(kT_ready, 1)
                    else:
                        nc.scalar.activation(qs_T[:, b, :, :].rearrange("p e n -> p (e n)"), bank[:, 2 + n % 2, 0:2 * P], ACT.Identity,
                                             bias=cols[:, 2:3]).then_inc(kT_ready, 1)

            def exponent(b):
                act.wait_ge(max_ready, b + 1)
                if b >= 2:
                    act.wait_ge(p_turned, CK * (b - 1))
                nc.scalar.activation(prob[:, b % 2, :], bank[:, 4:8, :].rearrange("p a n -> p (a n)"), ACT.Exp, bias=bias[:, b:b + 1],
                                     scale=SCALE, accum_out=psumr[:, b:b + 1]).then_inc(exp_ready, 1)

            def keep_prob(b):
                for c in range(CK):
                    act.wait_ge(p_turned, CK * b + c + 1)
                    if c == 0 and b >= 1:
                        act.wait_ge(c_ready, b)
                    nc.scalar.copy(p_T[:, 4 * c:4 * c + 4, :].rearrange("p t q -> p (t q)"), bank[:, c % 2, :]).then_inc(pT_ready, 1)

            def keep_context(b):
                act.wait_ge(c_ready, b + 1)
                nc.scalar.copy(c_T[:, b, :], bank[:, 2, 0:P]).then_inc(cT_ready, 1)

            act.dma_start(ctx_raw[:, 0, :, :], io["ctx_1024"][0].rearrange("(p t) d -> p t d", p=P)).then_inc(ctx_in[0], 16)
            act.wait_ge(char_turned, 1)
            nc.scalar.copy(char_T[:].rearrange("p b n -> p (b n)"), bank[:, 4, :]).then_inc(charT_ready, 1)
            act.wait_ge(w_in, 16 * N_IN)
            act.wait_ge(cproj, 1)
            nc.scalar.activation(qc_T[:].rearrange("p b n -> p (b n)"), bank[:, 5, :], ACT.Identity, bias=cols[:, 0:1]).then_inc(cproj_kept, 1)
            act.wait_ge(cproj, 2)
            nc.scalar.activation(kc_T[:].rearrange("p b n -> p (b n)"), bank[:, 6, :], ACT.Identity, bias=cols[:, 3:4]).then_inc(cproj_kept, 1)
            keep_keys(0)
            exponent(0)
            for b in range(B - 1):
                keep_keys(b + 1)
                keep_prob(b)
                exponent(b + 1)
                keep_context(b)
            keep_prob(B - 1)
            act.wait_ge(sub2_ready, 1)
            nc.scalar.activation(prob2[:], prob2[:], ACT.Exp, scale=SCALE).then_inc(exp2_ready, 1)
            keep_context(B - 1)
            act.wait_ge(p2_turned, 1)
            nc.scalar.copy(p2_T[:].rearrange("p b e q -> p (b e q)"), bank[:, 6:8, :].rearrange("p a n -> p (a n)")).then_inc(p2T_ready, 1)
            for e in range(2):
                act.wait_ge(both_turned, e + 1)
                nc.scalar.copy(both_T[:, :, e, :], bank[:, 4 + e, :].rearrange("p (b n) -> p b n", b=B)).then_inc(bothT_ready, 1)
            act.wait_ge(u_ready, 1)
            nc.scalar.activation(u[:], u[:], ACT.Exp, scale=-1.0).then_inc(e_ready, 1)

        @block.vector
        def _(dve):
            def keep_turned(b):
                for c in range(CK):
                    dve.wait_ge(ctx_turned, CK * b + c + 1)
                    if b >= 1 and c == 0:
                        dve.wait_ge(k_proj, (CK + 1) * b)
                    nc.vector.tensor_copy(ctx_T[:, c * BANK:(c + 1) * BANK], bank[:, c % 2, :]).then_inc(ctxT_ready, 1)

            def maximum(b):
                dve.wait_ge(sc_ready, b + 1)
                nc.vector.tensor_reduce(top[:, b:b + 1], bank[:, 4:8, :].rearrange("p a n -> p (a n)"), AX.X, ALU.max).then_inc(found_top, 1)
                dve.wait_ge(found_top, b + 1)
                nc.vector.tensor_scalar(bias[:, b:b + 1], top[:, b:b + 1], -SCALE, None, ALU.mult).then_inc(max_ready, 1)

            own = Chain(dve, dve_own)
            norm.vector(dve, own, x_res, char, 1).then_inc(char_ready, 1)
            dve.wait_ge(w_in, 16 * N_IN)
            dve.wait_ge(cproj, 3)
            nc.vector.tensor_tensor(vc[:], bank[:, 7, :].rearrange("p (b d) -> p b d", b=B), rows[:, 1:2, :].to_broadcast([P, B, D]),
                                    ALU.add).then_inc(cproj_kept, 1)
            keep_turned(0)
            maximum(0)
            for b in range(1, B):
                keep_turned(b)
                maximum(b)

            dve.wait_ge(s2_ready, 1)
            small = bank[:, 4:6, :].rearrange("p a (c n) -> p (a c) n", n=P)
            per_row = [P, 2 * B, P]
            own.link(nc.vector.tensor_reduce(top2[:].rearrange("p b e -> p (b e)"), small, AX.X, ALU.max))
            nc.vector.tensor_tensor(prob2[:].rearrange("p b e n -> p (b e) n"), small,
                                    top2[:].rearrange("p b e -> p (b e)").unsqueeze(2).to_broadcast(per_row), ALU.subtract).then_inc(sub2_ready, 1)
            dve.wait_ge(exp2_ready, 1)
            own.link(nc.vector.tensor_reduce(sum2[:], prob2[:], AX.X, ALU.add))
            own.link(nc.vector.tensor_scalar(sum2[:], sum2[:], 2.0, None, ALU.mult))
            nc.vector.reciprocal(inv2[:], sum2[:])
            dve.wait_ge(exp_ready, B)
            own.link(nc.vector.reciprocal(rsum[:], psumr[:]))
            dve.wait_ge(c2s_raw, 1)
            own.link(nc.vector.tensor_tensor(both[:, :, 0, :], bank[:, 3, :].rearrange("p (b d) -> p b d", b=B),
                                             rsum[:].unsqueeze(2).to_broadcast([P, B, D]), ALU.mult))
            nc.vector.tensor_tensor(both[:, :, 0, :], both[:, :, 0, :], rows[:, 0:1, :].to_broadcast([P, B, D]), ALU.add).then_inc(both_ready, 1)
            dve.wait_ge(o2_ready, 1)
            own.link(nc.vector.tensor_tensor(half_out[:].rearrange("p b e n -> p (b e) n"), bank[:, 0:2, :].rearrange("p a (c n) -> p (a c) n", n=P),
                                             inv2[:].rearrange("p b e -> p (b e)").unsqueeze(2).to_broadcast(per_row), ALU.mult))
            nc.vector.tensor_tensor(both[:, :, 1, :], half_out[:, :, 0, :], half_out[:, :, 1, :], ALU.add).then_inc(both_ready, 1)
            dve.wait_ge(both_ready, 2)
            own.link(nc.vector.tensor_tensor(diff[:], both[:, :, 0, :], both[:, :, 1, :], ALU.subtract))
            own.link(nc.vector.tensor_tensor(x_res[:], x_res[:], both[:, :, 1, :], ALU.add))
            dve.wait_ge(g_ready, 1)
            nc.vector.tensor_tensor(u[:], bank[:, 6, :].rearrange("p (b d) -> p b d", b=B), rows[:, 2:3, :].to_broadcast([P, B, D]),
                                    ALU.add).then_inc(u_ready, 1)
            dve.wait_ge(e_ready, 1)
            own.link(nc.vector.tensor_scalar(u[:], u[:], 1.0, None, ALU.add))
            own.link(nc.vector.reciprocal(u[:], u[:]))
            own.link(nc.vector.tensor_tensor(diff[:], diff[:], u[:], ALU.mult))
            nc.vector.tensor_tensor(x_res[:], x_res[:], diff[:], ALU.add)


def causal_linear_attention(nc, io, g):
    HD = D // H
    GH = 32 // HD
    with ExitStack() as ctx:
        s = Stage(nc, ctx, "ca")
        w_q, w_k, w_v, w_c = (s.sb(n, [P, D]) for n in ("w_q", "w_k", "w_v", "w_c"))
        l_raw, l_mask = s.sb("l_raw", [P, HD]), s.sb("l_mask", [P, H, HD])
        heads, causal = s.sb("heads", [P, H]), s.sb("causal", [P, P])
        l_blk, l_T, ll, mix = (s.sb(n, [P, D]) for n in ("l_blk", "l_T", "ll", "mix"))
        norm = Norm(s, B, g["mhalf"])
        xn, xn_T, q_T, k_T = (s.sb(n, [P, B, D]) for n in ("xn", "xn_T", "q_T", "k_T"))
        v_own = s.sb("v_own", [P, B, H, GH * HD])
        q_own = s.sb("q_own", [P, B, H, P])
        att = s.sb("att", [P, 2, H, P])
        y_T = s.sb("y_T", [P, 2, P])
        bank = s.ps("bank", [P, 8, BANK])
        (w_in, dve_own, l_ready, l_turned, lT_ready, ll_made, ll_ready, mix_made, mix_ready, xn_ready, xn_turned, xnT_ready,
         proj_ready, kept, zeros_ready, qown_d, qown_p, sc_ready, att_ready, y_made, yT_ready, out_ready, x_ready, mix_in) = (
            s.sem(n) for n in (
                "w_in", "dve_own", "l_ready", "l_turned", "lT_ready", "ll_made", "ll_ready", "mix_made", "mix_ready", "xn_ready",
                "xn_turned", "xnT_ready", "proj_ready", "kept", "zeros_ready", "qown_d", "qown_p", "sc_ready", "att_ready", "y_made",
                "yT_ready", "out_ready", "x_ready", "mix_in"))
        x_res, ident = g["x_res"], g["ident"]
        block = ctx.enter_context(nc.Block())
        @block.sync
        def _(sp):
            for t, n in ((w_q[:], io["L1_attn_Wq"]), (w_k[:], io["L1_attn_Wk"]), (w_v[:], io["L1_attn_Wv"]),
                         (heads[:], io["heads"]), (causal[:], io["causal"])):
                sp.dma_start(t, n).then_inc(w_in, 16)
            for t, n in ((l_raw[:], io["L1_attn_Ltri"].rearrange("h d e -> (h d) e")), (l_mask[:].rearrange("p h e -> p (h e)"), io["l_mask"]),
                         (w_c[:], io["L1_attn_Wc"])):
                sp.dma_start(t, n).then_inc(mix_in, 16)
        N_IN, N_MIX = 5, 3
        BY_POOL = 2

        def own_queries(engine, b):
            return engine.tensor_tensor(q_own[:, b, :, :], q_T[:, b, :].unsqueeze(1).to_broadcast([P, H, P]),
                                        heads[:].unsqueeze(2).to_broadcast([P, H, P]), ALU.mult)

        @block.gpsimd
        def _(pool):
            nc.gpsimd.memset(v_own[:], 0.0).then_inc(zeros_ready, 1)
            norm.pool(pool, 1)
            pool.wait_ge(w_in, 16 * N_IN)
            pool.wait_ge(kept, 1)
            for b in range(B - BY_POOL, B):
                own_queries(nc.gpsimd, b).then_inc(qown_p, 1)

        @block.tensor
        def _(pe):
            def score(b):
                if b < B - BY_POOL:
                    pe.wait_ge(qown_d, b + 1)
                else:
                    pe.wait_ge(qown_p, b - (B - BY_POOL) + 1)
                for c in range(4):
                    if b >= 1:
                        pe.wait_ge(att_ready, 4 * (b - 1) + c + 1)
                    nc.tensor.matmul(bank[:, c, :], k_T[:, b, :], q_own[:, b, 4 * c:4 * c + 4, :].rearrange("p h n -> p (h n)"),
                                     start=True, stop=True).then_inc(sc_ready, 1)

            def gather(b):
                if b >= 1:
                    pe.wait_ge(yT_ready, b)
                for c in range(4):
                    pe.wait_ge(att_ready, 4 * b + c + 1)
                    for j in range(GH):
                        h = GH * c + j
                        mm = nc.tensor.matmul(bank[GH * HD * c:GH * HD * (c + 1), 4, 0:P], v_own[:, b, h, :], att[:, b % 2, h, :],
                                              start=(j == 0), stop=(j == GH - 1))
                mm.then_inc(y_made, 1)

            def project_out(b):
                pe.wait_ge(yT_ready, b + 1)
                if b == 0:
                    pe.wait_ge(mix_ready, 1)
                else:
                    pe.wait_ge(x_ready, b)
                nc.tensor.matmul(bank[:, 7, 0:D], y_T[:, b % 2, :], mix[:], start=True, stop=True).then_inc(out_ready, 1)

            pe.wait_ge(xn_ready, 1)
            for b in range(B):
                mm = nc.tensor.transpose(bank[:, 0, b * P:(b + 1) * P], xn[:, b, :], ident[:])
            mm.then_inc(xn_turned, 1)
            pe.wait_ge(w_in, 16 * N_IN)
            pe.wait_ge(xnT_ready, 1)
            rhs = xn_T[:].rearrange("p b n -> p (b n)")
            nc.tensor.matmul(bank[:, 1, :], w_q[:], rhs, start=True, stop=True).then_inc(proj_ready, 1)
            nc.tensor.matmul(bank[:, 2, :], w_k[:], rhs, start=True, stop=True).then_inc(proj_ready, 1)
            for b in range(B):
                mm = nc.tensor.matmul(bank[:, 3, b * P:(b + 1) * P], xn_T[:, b, :], w_v[:], start=True, stop=True)
            mm.then_inc(proj_ready, 1)
            pe.wait_ge(l_ready, 1)
            nc.tensor.transpose(bank[:, 6, 0:P], l_blk[:], ident[:]).then_inc(l_turned, 1)
            pe.wait_ge(lT_ready, 1)
            nc.tensor.matmul(bank[:, 7, 0:P], l_T[:], l_T[:], start=True, stop=True).then_inc(ll_made, 1)
            pe.wait_ge(kept, 3)
            score(0)
            pe.wait_ge(ll_ready, 1)
            nc.tensor.matmul(bank[:, 6, 0:P], ll[:], w_c[:], start=True, stop=True).then_inc(mix_made, 1)
            for b in range(B):
                if b + 1 < B:
                    score(b + 1)
                gather(b)
                if b >= 1:
                    project_out(b - 1)
            project_out(B - 1)

        @block.scalar
        def _(act):
            act.wait_ge(xn_turned, 1)
            nc.scalar.copy(xn_T[:].rearrange("p b n -> p (b n)"), bank[:, 0, :]).then_inc(xnT_ready, 1)
            for n, t in enumerate((q_T, k_T)):
                act.wait_ge(proj_ready, n + 1)
                nc.scalar.copy(t[:].rearrange("p b n -> p (b n)"), bank[:, 1 + n, :]).then_inc(kept, 1)
            act.wait_ge(proj_ready, 3)
            act.wait_ge(zeros_ready, 1)
            v = bank[:, 3, :].rearrange("p (b c j d) -> p b c j d", b=B, j=GH, d=HD)
            for j in range(GH):
                last = nc.scalar.copy(v_own[:].rearrange("p b (c j) n -> p b c j n", j=GH)[:, :, :, j, j * HD:(j + 1) * HD], v[:, :, :, j, :])
            last.then_inc(kept, 1)
            act.wait_ge(l_turned, 1)
            nc.scalar.copy(l_T[:], bank[:, 6, 0:P]).then_inc(lT_ready, 1)
            act.wait_ge(ll_made, 1)
            nc.scalar.copy(ll[:], bank[:, 7, 0:P]).then_inc(ll_ready, 1)
            act.wait_ge(mix_made, 1)
            nc.scalar.copy(mix[:], bank[:, 6, 0:P]).then_inc(mix_ready, 1)
            for b in range(B):
                act.wait_ge(y_made, b + 1)
                if b >= 2:
                    act.wait_ge(out_ready, b - 1)
                nc.scalar.copy(y_T[:, b % 2, :], bank[:, 4, 0:P]).then_inc(yT_ready, 1)

        @block.vector
        def _(dve):
            own = Chain(dve, dve_own)
            norm.vector(dve, own, x_res, xn, 1).then_inc(xn_ready, 1)
            dve.wait_ge(mix_in, 16 * N_MIX)
            nc.vector.tensor_tensor(l_blk[:].rearrange("p (h e) -> p h e", e=HD), l_mask[:], l_raw[:].unsqueeze(1).to_broadcast([P, H, HD]),
                                    ALU.mult).then_inc(l_ready, 1)
            dve.wait_ge(w_in, 16 * N_IN)
            dve.wait_ge(kept, 1)
            for b in range(B - BY_POOL):
                own_queries(nc.vector, b).then_inc(qown_d, 1)
            for b in range(B + 1):
                if b < B:
                    if b >= 2:
                        dve.wait_ge(y_made, b - 1)
                    for c in range(4):
                        dve.wait_ge(sc_ready, 4 * b + c + 1)
                        nc.vector.tensor_tensor(att[:, b % 2, 4 * c:4 * c + 4, :], bank[:, c, :].rearrange("p (h n) -> p h n", h=4),
                                                causal[:].unsqueeze(1).to_broadcast([P, 4, P]), ALU.mult).then_inc(att_ready, 1)
                if b >= 2:
                    dve.wait_ge(out_ready, b - 1)
                    nc.vector.tensor_tensor(x_res[:, b - 2, :], x_res[:, b - 2, :], bank[:, 7, 0:D], ALU.add).then_inc(x_ready, 1)
            dve.wait_ge(out_ready, B)
            nc.vector.tensor_tensor(x_res[:, B - 1, :], x_res[:, B - 1, :], bank[:, 7, 0:D], ALU.add)


def mixture_of_experts(nc, io, g):
    E = 8
    ST = 2
    TOP_K = 2
    with ExitStack() as ctx:
        s = Stage(nc, ctx, "me")
        w_r = s.sb("w_r", [P, E])
        s_1, s_3, s_2 = s.sb("s_1", [P, ST * P]), s.sb("s_3", [P, ST * P]), s.sb("s_2", [P, ST, D])
        e_1, e_2 = s.sb("e_1", [P, E, P]), s.sb("e_2", [P, E, D])
        row_b, iota = s.sb("row_b", [P, E]), s.sb("iota", [P, E])
        norm = Norm(s, B, g["mhalf"])
        xn, xn_T, acc = (s.sb(n, [P, B, D]) for n in ("xn", "xn_T", "acc"))
        sig, sel, best, comb = (s.sb(n, [P, B, E]) for n in ("sig", "sel", "best", "comb"))
        idx = s.sb("idx", [P, B, E], U32)
        idx_f, hot, tmp = s.sb("idx_f", [P, B, E]), s.sb("hot", [P, B, E]), s.sb("tmp", [P, B, E])
        den, big, half = (s.sb(n, [P, B, 1]) for n in ("den", "big", "half"))
        silu, sh_T = s.sb("silu", [P, ST, B * P]), s.sb("sh_T", [P, ST, B * P])
        warm = s.sb("warm", [P, 1])
        h_T = s.sb("h_T", [P, 2, B * P])
        bank = s.ps("bank", [P, 8, BANK])
        (w_in, e_in, dve_own, xn_ready, xn_turned, xnT_ready, r_made, sig_ready, a_made, silu_ready, sh_ready, s_made, s_ready, h_made,
         h_ready, y_made, y_used) = (s.sem(n) for n in (
            "w_in", "e_in", "dve_own", "xn_ready", "xn_turned", "xnT_ready", "r_made", "sig_ready", "a_made", "silu_ready", "sh_ready",
            "s_made", "s_ready", "h_made", "h_ready", "y_made", "y_used"))
        x_res, ident = g["x_res"], g["ident"]
        block = ctx.enter_context(nc.Block())
        N_SHARED, N_EXPERTS = 6, 2

        @block.sync
        def _(sp):
            for t, n in ((w_r[:], io["L1_ffn_router_w"]), (s_1[:], io["L1_ffn_sw1"]), (s_3[:], io["L1_ffn_sw3"]),
                         (s_2[:], io["L1_ffn_sw2"].rearrange("(c p) n -> p c n", p=P)), (row_b[:], row(io["L1_ffn_router_bias"])),
                         (iota[:], io["iota"])):
                sp.dma_start(t, n).then_inc(w_in, 16)
            sp.dma_start(e_1[:], io["L1_ffn_ew1"].rearrange("e d h -> d e h")).then_inc(e_in, 16)
            sp.dma_start(e_2[:], io["L1_ffn_ew2"].rearrange("e h d -> h e d")).then_inc(e_in, 16)

        @block.gpsimd
        def _(pool):
            norm.pool(pool, 1)

        @block.tensor
        def _(pe):
            pe.wait_ge(xn_ready, 1)
            for b in range(B):
                mm = nc.tensor.transpose(bank[:, 0, b * P:(b + 1) * P], xn[:, b, :], ident[:])
            mm.then_inc(xn_turned, 1)
            pe.wait_ge(xnT_ready, 1)
            pe.wait_ge(w_in, 16 * N_SHARED)
            rhs = xn_T[:].rearrange("p b n -> p (b n)")
            for b in range(B):
                mm = nc.tensor.matmul(bank[:, 1, b * E:(b + 1) * E], xn_T[:, b, :], w_r[:], start=True, stop=True)
            mm.then_inc(r_made, 1)
            for c in range(ST):
                nc.tensor.matmul(bank[:, 2 + c, :], s_1[:, c * P:(c + 1) * P], rhs, start=True, stop=True)
                nc.tensor.matmul(bank[:, 4 + c, :], s_3[:, c * P:(c + 1) * P], rhs, start=True, stop=True).then_inc(a_made, 1)

            def hidden(e):
                if e == 0:
                    pe.wait_ge(e_in, 16 * N_EXPERTS)
                elif e == 1:
                    pe.wait_ge(sig_ready, 1)
                else:
                    pe.wait_ge(h_ready, e - 1)
                nc.tensor.matmul(bank[:, e % 2, :], e_1[:, e, :], rhs, start=True, stop=True).then_inc(h_made, 1)

            hidden(0)
            pe.wait_ge(sh_ready, ST)
            for b in range(B):
                for c in range(ST):
                    mm = nc.tensor.matmul(bank[:, 6, b * P:(b + 1) * P], sh_T[:, c, b * P:(b + 1) * P], s_2[:, c, :],
                                          start=(c == 0), stop=(c == ST - 1))
            mm.then_inc(s_made, 1)
            for e in range(E):
                if e + 1 < E:
                    hidden(e + 1)
                pe.wait_ge(h_ready, e + 1)
                if e >= 2:
                    pe.wait_ge(y_used, e - 1)
                for b in range(B):
                    mm = nc.tensor.matmul(bank[:, 2 + e % 2, b * P:(b + 1) * P], h_T[:, e % 2, b * P:(b + 1) * P], e_2[:, e, :],
                                          start=True, stop=True)
                mm.then_inc(y_made, 1)

        @block.scalar
        def _(act):
            nc.scalar.activation(warm[:], ident[:, 0:1], ACT.Sigmoid)
            act.wait_ge(xn_turned, 1)
            nc.scalar.copy(xn_T[:].rearrange("p b n -> p (b n)"), bank[:, 0, :]).then_inc(xnT_ready, 1)
            act.wait_ge(r_made, 1)
            nc.scalar.activation(sig[:].rearrange("p b e -> p (b e)"), bank[:, 1, 0:B * E], ACT.Sigmoid).then_inc(sig_ready, 1)
            for c in range(ST):
                act.wait_ge(a_made, c + 1)
                nc.scalar.activation(silu[:, c, :], bank[:, 2 + c, :], ACT.Silu).then_inc(silu_ready, 1)
            for e in range(E):
                act.wait_ge(h_made, e + 1)
                if e >= 2:
                    act.wait_ge(y_made, e - 1)
                nc.scalar.activation(h_T[:, e % 2, :], bank[:, e % 2, :], ACT.Gelu).then_inc(h_ready, 1)

        @block.vector
        def _(dve):
            own = Chain(dve, dve_own)
            norm.vector(dve, own, x_res, xn, 1).then_inc(xn_ready, 1)
            dve.wait_ge(w_in, 16 * N_SHARED)
            dve.wait_ge(sig_ready, 1)
            own.link(nc.vector.tensor_tensor(sel[:], sig[:], row_b[:].unsqueeze(1).to_broadcast([P, B, E]), ALU.add))
            for b in range(B):
                last = nc.vector.max(out=best[:, b, :], in_=sel[:, b, :])
            own.link(last)
            for b in range(B):
                last = nc.vector.max_index(out=idx[:, b, :], in_max=best[:, b, :], in_values=sel[:, b, :])
            own.link(last)
            own.link(nc.vector.tensor_copy(idx_f[:], idx[:]))
            labels = iota[:].unsqueeze(1).to_broadcast([P, B, E])
            own.link(nc.vector.tensor_tensor(hot[:], labels, idx_f[:, :, 0:1].to_broadcast([P, B, E]), ALU.is_equal))
            own.link(nc.vector.tensor_tensor(tmp[:], labels, idx_f[:, :, 1:2].to_broadcast([P, B, E]), ALU.is_equal))
            own.link(nc.vector.tensor_tensor(hot[:], hot[:], tmp[:], ALU.add))
            own.link(nc.vector.tensor_tensor(comb[:], hot[:], sig[:], ALU.mult))
            own.link(nc.vector.tensor_reduce(den[:, :, 0], comb[:], AX.X, ALU.add))
            own.link(nc.vector.tensor_scalar(big[:], den[:], 1e-9, None, ALU.is_gt))
            own.link(nc.vector.tensor_scalar(den[:], den[:], 1e-9, None, ALU.add))
            own.link(nc.vector.reciprocal(den[:], den[:]))
            own.link(nc.vector.tensor_tensor(den[:], den[:], big[:], ALU.mult))
            own.link(nc.vector.tensor_scalar(half[:], big[:], -1.0 / TOP_K, 1.0 / TOP_K, ALU.mult, ALU.add))
            own.link(nc.vector.tensor_tensor(comb[:], comb[:], den[:].to_broadcast([P, B, E]), ALU.mult))
            own.link(nc.vector.tensor_tensor(tmp[:], hot[:], half[:].to_broadcast([P, B, E]), ALU.mult))
            own.link(nc.vector.tensor_tensor(comb[:], comb[:], tmp[:], ALU.add))
            for c in range(ST):
                dve.wait_ge(a_made, c + 1)
                dve.wait_ge(silu_ready, c + 1)
                nc.vector.tensor_tensor(sh_T[:, c, :], bank[:, 4 + c, :], silu[:, c, :], ALU.mult).then_inc(sh_ready, 1)
            dve.wait_ge(s_made, 1)
            own.link(nc.vector.tensor_tensor(acc[:], x_res[:], bank[:, 6, :].rearrange("p (b d) -> p b d", b=B), ALU.add))
            for e in range(E):
                dve.wait_ge(y_made, e + 1)
                for b in range(B):
                    last = nc.vector.scalar_tensor_tensor(out=(x_res if e == E - 1 else acc)[:, b, :], in0=bank[:, 2 + e % 2, b * P:(b + 1) * P],
                                                          scalar=comb[:, b, e:e + 1], in1=acc[:, b, :], op0=ALU.mult, op1=ALU.add)
                last.then_inc(y_used, 1)
                dve.wait_ge(y_used, e + 1)


STAGES = (latent_cross_attention, linear_attention, local_transformer, two_way_attention,
          causal_linear_attention, mixture_of_experts)


def perceiver(nc, io, out, stages=STAGES):
    with ExitStack() as ctx:
        s = Stage(nc, ctx, "g")
        g = {"x_res": s.sb("x_res", [P, B, D]), "ident": s.sb("ident", [P, P]), "ones_row": s.sb("ones_row", [1, P]),
             "mhalf": s.sb("mhalf", [P, 64])}
        first_in = s.sem("first_in")
        set_up = s.sem("set_up")
        with nc.Block() as block:
            @block.sync
            def _(sp):
                sp.dma_start(g["x_res"][:], io["x"].rearrange("b t d -> t b d")).then_inc(first_in, 16)
                sp.dma_start(g["ident"][:], io["ident"]).then_inc(first_in, 16)
                sp.wait_ge(first_in, 32)

            @block.gpsimd
            def _(pool):
                nc.gpsimd.memset(g["ones_row"][:], 1.0)
                nc.gpsimd.memset(g["mhalf"][:], -0.5).then_inc(set_up, 1)
                pool.wait_ge(set_up, 1)
        for stage in stages:
            with nc.cleanup_on_exit():
                stage(nc, io, g)
        x_out = s.sem("x_out")
        with nc.Block() as block:
            @block.sync
            def _(sp):
                sp.dma_start(out.rearrange("b t d -> t b d"), g["x_res"][:]).then_inc(x_out, 16)
                sp.wait_ge(x_out, 16)


def shape_constants():
    f = np.float32
    half = np.arange(0, DH, 2, dtype=f)
    freqs = np.arange(P, dtype=f)[:, None] * (f(1) / f(10000) ** (half / f(DH)))[None, :]
    freqs = np.concatenate([freqs, freqs], -1)
    power = (np.arange(P, dtype=f) - f(P // 2)) / f(16)
    scale = ((half + f(0.4 * DH)) / f(1.4 * DH))[None, :] ** power[:, None]
    scale = np.concatenate([scale, scale], -1)
    sign = np.where(np.arange(DH) < DH // 2, f(-1), f(1))
    rotary = np.concatenate([np.cos(freqs) * scale, np.sin(freqs) * sign * scale,
                             np.cos(freqs) / scale, np.sin(freqs) * sign / scale], 1).astype(f)
    i, j = np.arange(P)[:, None], np.arange(P)[None, :]
    return {
        "ident": np.eye(P, dtype=f),
        "rotary": rotary,
        "band": np.where((i >= j) & (i <= j + 32), f(0), f(-BIG)).astype(f),
        "heads": (i // 8 == np.arange(H)[None, :]).astype(f),
        "l_mask": ((i // 8 == j // 8) & (i >= j)).astype(f),
        "causal": (i <= j).astype(f),
        "iota": np.tile(np.arange(8, dtype=f), (P, 1)),
        "shift": (i + 1 == j).astype(f),
    }


TRANSPOSED = ("L1_xattn_Wq_c", "L1_xattn_Wk_s", "L1_xattn_Wv_s", "L1_xattn_Wq_s", "L1_xattn_Wk_c", "L1_xattn_Wv_c", "L1_xattn_Wg",
              "L1_attn_Wq", "L1_attn_Wk", "L1_attn_Wv", "L1_attn_Wc", "L1_ffn_router_w")


def device_inputs(inputs):
    arrays = {}
    for name, a in inputs.items():
        a = np.ascontiguousarray(a)
        arrays[name] = a.view(np.uint8) if a.dtype == np.bool_ else a
    for name in ("L0_attn_bq", "L0_attn_b1"):
        arrays[name] = np.ascontiguousarray(arrays[name].reshape(-1, P).T)
    for name in TRANSPOSED:
        arrays[name] = np.ascontiguousarray(arrays[name].T)
    qs, ks = arrays["L0_ffn_q_scale"], arrays["L0_ffn_k_scale"]
    arrays["L0_ffn_gains"] = np.concatenate([qs, np.roll(qs, DH // 2, 1), ks, np.roll(ks, DH // 2, 1)], 1)
    b1 = arrays["L0_ffn_b1"].reshape(-1, 2, 341)
    b1 = np.pad(b1, ((0, 0), (0, 0), (0, 3 * P - 341))).reshape(-1, 6, P)
    arrays["L0_ffn_cols"] = np.ascontiguousarray(
        np.concatenate([arrays["L0_ffn_ln_g"][:, None], arrays["L0_ffn_ln_b"][:, None], b1], 1).transpose(0, 2, 1))
    arrays.update(shape_constants())
    return arrays


def kernel(**inputs):
    import concourse.bacc as _bacc
    from concourse.bass_utils import run_bass_kernel_spmd as _run

    nc = _bacc.Bacc("TRN2", target_bir_lowering=False, num_devices=1)
    arrays = {f"in_{n}_dram": a for n, a in device_inputs(inputs).items()}
    io = {n[3:-5]: nc.dram_tensor(n, a.shape, mybir.dt.from_np(a.dtype), kind="ExternalInput").ap() for n, a in arrays.items()}
    out = nc.dram_tensor("out_0_dram", (B, P, D), F32, kind="ExternalOutput").ap()
    perceiver(nc, io, out)
    r = _run(nc, [arrays], core_ids=[0])
    return r.results[0]["out_0_dram"]
```
